# Optimizing a Trainium2 kernel written in Bass

```python
import numpy as np
import jax
import jax.numpy as jnp

def _softmax(x, axis=-1):
    return jax.nn.softmax(x, axis=axis)

def _gelu(x):
    return jax.nn.gelu(x, approximate=True)

def _silu(x):
    return jax.nn.silu(x)

def _sigmoid(x):
    return jax.nn.sigmoid(x)

def _layernorm(x, axis=-1, eps=1e-05):
    m = jnp.mean(x, axis=axis, keepdims=True)
    v = jnp.var(x, axis=axis, keepdims=True)
    return (x - m) / jnp.sqrt(v + eps)

def _scatter_add(tgt, idx, src, axis=0):
    return tgt.at[idx].add(src)

def _segment_sum(src, seg, n):
    return jax.ops.segment_sum(src, seg, n)
kernel_name = 'mk_vit_tower_cls_d2_tok_img1024_r4_5558ce'

def setup_inputs(seed: int=0):
    np.random.seed(seed)
    _w = jnp.asarray

    def _rec_inputs():
        import jax
        import jax.numpy as jnp
        _rk = jax.random.key(seed)
        x = -0.00150118 + 0.499729 * jax.random.normal(jax.random.fold_in(_rk, 1), (16, 256, 64, 2), jnp.float32)
        cls_tok = 0.02 * jax.random.normal(jax.random.fold_in(_rk, 5), (1, 1, 256), jnp.float32)
        return (x, cls_tok)
    x, cls_tok = _rec_inputs()

    def _L0_tok_setup():
        import jax, jax.numpy as jnp
        import numpy as np
        import math
        H = 256
        N = 64
        CH = 1
        SEQ_L = 256
        key = jax.random.key(seed)
        k1, k2, k3, k4 = jax.random.split(key, 4)
        log_dt = jax.random.uniform(k1, (H,), dtype=jnp.float32, minval=math.log(0.001), maxval=math.log(0.1))
        inv_A_real = jnp.log(0.5 * jnp.ones((H, N), jnp.float32)) + 0.1 * jax.random.normal(k2, (H, N), dtype=jnp.float32)
        A_imag = jnp.broadcast_to(math.pi * jnp.arange(N, dtype=jnp.float32), (H, N)).copy()
        B_ri = jax.random.normal(k3, (H, N, 2), dtype=jnp.float32) * 0.5
        C_ri = jax.random.normal(k4, (CH, H, N, 2), dtype=jnp.float32) * 0.5
        return {'log_dt': log_dt, 'inv_A_real': inv_A_real, 'A_imag': A_imag, 'B_ri': B_ri, 'C_ri': C_ri, 'L': SEQ_L}
    _L0_tok_all = _L0_tok_setup()
    _L0_tok_in = {k: v for k, v in _L0_tok_all.items() if k in ('log_dt', 'inv_A_real', 'A_imag', 'B_ri')}
    del _L0_tok_all

    def _L0_attn_setup():
        import math
        import jax, jax.numpy as jnp
        import numpy as np
        D_MODEL = 256
        N_HEADS = 16
        HEAD_DIM = D_MODEL // N_HEADS
        B, L = (2, 512)
        EPS = 1e-05

        def _gammas():
            return jnp.array([1.0 - 2.0 ** (-5 - math.floor(8 * i / N_HEADS)) for i in range(N_HEADS)], dtype=jnp.float32)

        def _decay_mask(seq_len):
            idx = jnp.arange(seq_len)
            diff = idx[:, None] - idx[None, :]
            g = _gammas()[:, None, None]
            pow_ = g ** jnp.maximum(diff, 0).astype(jnp.float32)
            return jnp.where(diff >= 0, pow_, 0.0)
        key = jax.random.key(seed)
        ks = jax.random.split(key, 7)
        s = 1.0 / math.sqrt(D_MODEL)
        x = jax.random.normal(ks[0], (B, L, D_MODEL), dtype=jnp.float32)
        Wq = jax.random.normal(ks[1], (N_HEADS, D_MODEL, HEAD_DIM), dtype=jnp.float32) * s
        Wk = jax.random.normal(ks[2], (N_HEADS, D_MODEL, HEAD_DIM), dtype=jnp.float32) * s
        Wv = jax.random.normal(ks[3], (N_HEADS, D_MODEL, HEAD_DIM), dtype=jnp.float32) * s
        gn_weight = jnp.ones((D_MODEL,), dtype=jnp.float32)
        gn_bias = jnp.zeros((D_MODEL,), dtype=jnp.float32)
        Wout = jax.random.normal(ks[4], (D_MODEL, D_MODEL), dtype=jnp.float32) * s
        return {'x': x, 'Wq': Wq, 'Wk': Wk, 'Wv': Wv, 'gn_weight': gn_weight, 'gn_bias': gn_bias, 'Wout': Wout}
    _L0_attn_all = _L0_attn_setup()
    _L0_attn_in = {k: v for k, v in _L0_attn_all.items() if k in ('Wq', 'Wk', 'Wv', 'gn_weight', 'gn_bias', 'Wout')}
    del _L0_attn_all

    def _L0_ffn_setup():
        import jax, jax.numpy as jnp
        import numpy as np
        N_HEAD = 16
        NUM_EXPERTS = 8
        TOP_K = 2
        LN_EPS = 1e-05

        def _layernorm(x, g, b):
            mu = jnp.mean(x, axis=-1, keepdims=True)
            var = jnp.mean(jnp.square(x - mu), axis=-1, keepdims=True)
            return (x - mu) * jax.lax.rsqrt(var + LN_EPS) * g + b

        def _attention(h, Wq, bq, Wk, bk, Wv, bv, Wp, bp):
            B, T, D = h.shape
            hd = D // N_HEAD

            def split(z):
                return z.reshape(B, T, N_HEAD, hd).transpose(0, 2, 1, 3)
            q = split(h @ Wq + bq)
            k = split(h @ Wk + bk)
            v = split(h @ Wv + bv)
            att = jnp.einsum('bhqd,bhkd->bhqk', q, k) / jnp.sqrt(jnp.float32(hd))
            causal = jnp.tril(jnp.ones((T, T), bool))
            att = jnp.where(causal, att, -jnp.inf)
            att = jax.nn.softmax(att, axis=-1)
            y = jnp.einsum('bhqk,bhkd->bhqd', att, v)
            y = y.transpose(0, 2, 1, 3).reshape(B, T, D)
            return y @ Wp + bp

        def _token_moe(h, gate_W, gate_b, exp_W1, exp_b1, exp_W2, exp_b2):
            B, T, D = h.shape
            flat = h.reshape(-1, D)
            N = flat.shape[0]
            logits = flat @ gate_W + gate_b
            top_v, top_i = jax.lax.top_k(logits, TOP_K)
            w = jax.nn.softmax(top_v, axis=-1)
            w_full = jnp.zeros((N, NUM_EXPERTS), flat.dtype)
            w_full = w_full.at[jnp.arange(N)[:, None], top_i].add(w)
            out = jnp.zeros_like(flat)
            for e in range(NUM_EXPERTS):
                mid = jax.nn.gelu(flat @ exp_W1[e] + exp_b1[e], approximate=False)
                y_e = mid @ exp_W2[e] + exp_b2[e]
                out = out + w_full[:, e:e + 1] * y_e
            return out.reshape(B, T, D)
        key = jax.random.key(seed)
        B, T, D = (8, 256, 256)
        H = 4 * D
        E = NUM_EXPERTS
        ks = jax.random.split(key, 24)
        s = 0.02
        inp = {'x': jax.random.normal(ks[0], (B, T, D), jnp.float32), 'ln1_g': jnp.ones((D,), jnp.float32), 'ln1_b': jnp.zeros((D,), jnp.float32), 'ln2_g': jnp.ones((D,), jnp.float32), 'ln2_b': jnp.zeros((D,), jnp.float32), 'Wq': jax.random.normal(ks[1], (D, D), jnp.float32) * s, 'bq': jnp.zeros((D,), jnp.float32), 'Wk': jax.random.normal(ks[2], (D, D), jnp.float32) * s, 'bk': jnp.zeros((D,), jnp.float32), 'Wv': jax.random.normal(ks[3], (D, D), jnp.float32) * s, 'bv': jnp.zeros((D,), jnp.float32), 'Wp': jax.random.normal(ks[4], (D, D), jnp.float32) * s, 'bp': jnp.zeros((D,), jnp.float32), 'gate_W': jax.random.normal(ks[5], (D, E), jnp.float32) * s, 'gate_b': jnp.zeros((E,), jnp.float32), 'exp_W1': jax.random.normal(ks[6], (E, D, H), jnp.float32) * s, 'exp_b1': jnp.zeros((E, H), jnp.float32), 'exp_W2': jax.random.normal(ks[7], (E, H, D), jnp.float32) * s, 'exp_b2': jnp.zeros((E, D), jnp.float32)}
        return inp
    _L0_ffn_all = _L0_ffn_setup()
    _L0_ffn_in = {k: v for k, v in _L0_ffn_all.items() if k in ('ln1_g', 'ln1_b', 'ln2_g', 'ln2_b', 'Wq', 'bq', 'Wk', 'bk', 'Wv', 'bv', 'Wp', 'bp', 'gate_W', 'gate_b', 'exp_W1', 'exp_b1', 'exp_W2', 'exp_b2')}
    del _L0_ffn_all

    def _L1_attn_setup():
        import jax, jax.numpy as jnp
        import numpy as np
        NUM_HEADS = 16

        def _stablemax3_s(x):
            pos = 1.0 + x * (1.0 + 0.5 * x * (1.0 + x / 3.0))
            neg = 1.0 / (1.0 - x * (1.0 - 0.5 * x * (1.0 - x / 3.0)))
            return jnp.where(x >= 0, pos, neg)

        def stablemax3(logits, axis=-1):
            logits = logits - jnp.max(logits, axis=axis, keepdims=True)
            s = _stablemax3_s(logits)
            return s / jnp.sum(s, axis=axis, keepdims=True)
        key = jax.random.key(seed)
        k1, k2, k3 = jax.random.split(key, 3)
        B, S, D = (2, 512, 256)
        x = jax.random.normal(k1, (B, S, D), dtype=jnp.float32)
        w_qkv = jax.random.normal(k2, (3 * D, D), dtype=jnp.float32) * 0.02
        w_out = jax.random.normal(k3, (D, D), dtype=jnp.float32) * 0.02
        b_out = jnp.zeros((D,), dtype=jnp.float32)
        return {'x': x, 'w_qkv': w_qkv, 'w_out': w_out, 'b_out': b_out}
    _L1_attn_all = _L1_attn_setup()
    _L1_attn_in = {k: v for k, v in _L1_attn_all.items() if k in ('w_qkv', 'w_out', 'b_out')}
    del _L1_attn_all

    def _L1_ffn_setup():
        import jax, jax.numpy as jnp
        import numpy as np
        B, T, D = (2, 256, 256)
        H, DK, K = (8, 128, 8)
        NKEYS = 64
        NEXP = NKEYS * NKEYS

        def _rmsnorm(x, w, eps=1e-06):
            inv = jax.lax.rsqrt(jnp.mean(x * x, axis=-1, keepdims=True) + eps)
            return x * inv * w
        key = jax.random.key(seed)
        ks = jax.random.split(key, 5)
        return {'x': jax.random.normal(ks[0], (B, T, D), jnp.float32), 'w_q': jax.random.normal(ks[1], (H * 2 * DK, D), jnp.float32) * 0.02, 'keys': jax.random.normal(ks[2], (H, NKEYS, 2, DK), jnp.float32) * 0.02, 'expert_down': jax.random.normal(ks[3], (NEXP, D), jnp.float32) * 0.02, 'expert_up': jax.random.normal(ks[4], (NEXP, D), jnp.float32) * 0.02, 'norm_w': jnp.ones((D,), jnp.float32)}
    _L1_ffn_all = _L1_ffn_setup()
    _L1_ffn_in = {k: v for k, v in _L1_ffn_all.items() if k in ('w_q', 'keys', 'expert_down', 'expert_up', 'norm_w')}
    del _L1_ffn_all
    return {'x': x, 'cls_tok': cls_tok, 'L0_tok_log_dt': _L0_tok_in['log_dt'], 'L0_tok_inv_A_real': _L0_tok_in['inv_A_real'], 'L0_tok_A_imag': _L0_tok_in['A_imag'], 'L0_tok_B_ri': _L0_tok_in['B_ri'], 'L0_attn_Wq': _L0_attn_in['Wq'], 'L0_attn_Wk': _L0_attn_in['Wk'], 'L0_attn_Wv': _L0_attn_in['Wv'], 'L0_attn_gn_weight': _L0_attn_in['gn_weight'], 'L0_attn_gn_bias': _L0_attn_in['gn_bias'], 'L0_attn_Wout': _L0_attn_in['Wout'], 'L0_ffn_ln1_g': _L0_ffn_in['ln1_g'], 'L0_ffn_ln1_b': _L0_ffn_in['ln1_b'], 'L0_ffn_ln2_g': _L0_ffn_in['ln2_g'], 'L0_ffn_ln2_b': _L0_ffn_in['ln2_b'], 'L0_ffn_Wq': _L0_ffn_in['Wq'], 'L0_ffn_bq': _L0_ffn_in['bq'], 'L0_ffn_Wk': _L0_ffn_in['Wk'], 'L0_ffn_bk': _L0_ffn_in['bk'], 'L0_ffn_Wv': _L0_ffn_in['Wv'], 'L0_ffn_bv': _L0_ffn_in['bv'], 'L0_ffn_Wp': _L0_ffn_in['Wp'], 'L0_ffn_bp': _L0_ffn_in['bp'], 'L0_ffn_gate_W': _L0_ffn_in['gate_W'], 'L0_ffn_gate_b': _L0_ffn_in['gate_b'], 'L0_ffn_exp_W1': _L0_ffn_in['exp_W1'], 'L0_ffn_exp_b1': _L0_ffn_in['exp_b1'], 'L0_ffn_exp_W2': _L0_ffn_in['exp_W2'], 'L0_ffn_exp_b2': _L0_ffn_in['exp_b2'], 'L1_attn_w_qkv': _L1_attn_in['w_qkv'], 'L1_attn_w_out': _L1_attn_in['w_out'], 'L1_attn_b_out': _L1_attn_in['b_out'], 'L1_ffn_w_q': _L1_ffn_in['w_q'], 'L1_ffn_keys': _L1_ffn_in['keys'], 'L1_ffn_expert_down': _L1_ffn_in['expert_down'], 'L1_ffn_expert_up': _L1_ffn_in['expert_up'], 'L1_ffn_norm_w': _L1_ffn_in['norm_w']}

def reference(x, cls_tok, L0_tok_log_dt, L0_tok_inv_A_real, L0_tok_A_imag, L0_tok_B_ri, L0_attn_Wq, L0_attn_Wk, L0_attn_Wv, L0_attn_gn_weight, L0_attn_gn_bias, L0_attn_Wout, L0_ffn_ln1_g, L0_ffn_ln1_b, L0_ffn_ln2_g, L0_ffn_ln2_b, L0_ffn_Wq, L0_ffn_bq, L0_ffn_Wk, L0_ffn_bk, L0_ffn_Wv, L0_ffn_bv, L0_ffn_Wp, L0_ffn_bp, L0_ffn_gate_W, L0_ffn_gate_b, L0_ffn_exp_W1, L0_ffn_exp_b1, L0_ffn_exp_W2, L0_ffn_exp_b2, L1_attn_w_qkv, L1_attn_w_out, L1_attn_b_out, L1_ffn_w_q, L1_ffn_keys, L1_ffn_expert_down, L1_ffn_expert_up, L1_ffn_norm_w):
    import jax
    import jax.numpy as jnp

    def _L0_tok_ref(log_dt, inv_A_real, A_imag, B_ri, C_ri, L):
        import jax, jax.numpy as jnp
        import numpy as np
        import math
        H = 256
        N = 64
        CH = 1
        SEQ_L = 256
        dt = jnp.exp(log_dt)
        A = -jnp.exp(inv_A_real) + 1j * A_imag
        B = B_ri[..., 0] + 1j * B_ri[..., 1]
        C = C_ri[..., 0] + 1j * C_ri[..., 1]
        dtA = A * dt[:, None]
        dA = (1.0 + dtA / 2) / (1.0 - dtA / 2)
        C_term = C * B[None]
        log_dA = jnp.log(dA)
        V = jnp.exp(log_dA[:, :, None] * jnp.arange(L))
        K = 2.0 * jnp.einsum('chn,hnl->chl', C_term, V).real
        return K.astype(jnp.float32)

    def _L0_attn_ref(x, Wq, Wk, Wv, gn_weight, gn_bias, Wout):
        import math
        import jax, jax.numpy as jnp
        import numpy as np
        D_MODEL = 256
        N_HEADS = 16
        HEAD_DIM = D_MODEL // N_HEADS
        B, L = (2, 512)
        EPS = 1e-05

        def _gammas():
            return jnp.array([1.0 - 2.0 ** (-5 - math.floor(8 * i / N_HEADS)) for i in range(N_HEADS)], dtype=jnp.float32)

        def _decay_mask(seq_len):
            idx = jnp.arange(seq_len)
            diff = idx[:, None] - idx[None, :]
            g = _gammas()[:, None, None]
            pow_ = g ** jnp.maximum(diff, 0).astype(jnp.float32)
            return jnp.where(diff >= 0, pow_, 0.0)
        Bq, Lq, _ = x.shape
        Q = jnp.einsum('bld,hde->bhle', x, Wq)
        K = jnp.einsum('bld,hde->bhle', x, Wk)
        V = jnp.einsum('bld,hde->bhle', x, Wv)
        Dm = _decay_mask(Lq)
        scores = jnp.einsum('bhle,bhme->bhlm', Q, K) * Dm[None] / math.sqrt(HEAD_DIM)
        out = jnp.einsum('bhlm,bhme->bhle', scores, V)
        combined = out.transpose(0, 2, 1, 3).reshape(Bq, Lq, D_MODEL)
        c = combined.transpose(0, 2, 1).reshape(Bq, N_HEADS, HEAD_DIM, Lq)
        mean = jnp.mean(c, axis=(2, 3), keepdims=True)
        var = jnp.var(c, axis=(2, 3), keepdims=True)
        c = (c - mean) / jnp.sqrt(var + EPS)
        c = c.reshape(Bq, D_MODEL, Lq)
        c = c * gn_weight[None, :, None] + gn_bias[None, :, None]
        combined = c.transpose(0, 2, 1)
        return combined @ Wout

    def _L0_ffn_ref(x, ln1_g, ln1_b, ln2_g, ln2_b, Wq, bq, Wk, bk, Wv, bv, Wp, bp, gate_W, gate_b, exp_W1, exp_b1, exp_W2, exp_b2):
        import jax, jax.numpy as jnp
        import numpy as np
        N_HEAD = 16
        NUM_EXPERTS = 8
        TOP_K = 2
        LN_EPS = 1e-05

        def _layernorm(x, g, b):
            mu = jnp.mean(x, axis=-1, keepdims=True)
            var = jnp.mean(jnp.square(x - mu), axis=-1, keepdims=True)
            return (x - mu) * jax.lax.rsqrt(var + LN_EPS) * g + b

        def _attention(h, Wq, bq, Wk, bk, Wv, bv, Wp, bp):
            B, T, D = h.shape
            hd = D // N_HEAD

            def split(z):
                return z.reshape(B, T, N_HEAD, hd).transpose(0, 2, 1, 3)
            q = split(h @ Wq + bq)
            k = split(h @ Wk + bk)
            v = split(h @ Wv + bv)
            att = jnp.einsum('bhqd,bhkd->bhqk', q, k) / jnp.sqrt(jnp.float32(hd))
            causal = jnp.tril(jnp.ones((T, T), bool))
            att = jnp.where(causal, att, -jnp.inf)
            att = jax.nn.softmax(att, axis=-1)
            y = jnp.einsum('bhqk,bhkd->bhqd', att, v)
            y = y.transpose(0, 2, 1, 3).reshape(B, T, D)
            return y @ Wp + bp

        def _token_moe(h, gate_W, gate_b, exp_W1, exp_b1, exp_W2, exp_b2):
            B, T, D = h.shape
            flat = h.reshape(-1, D)
            N = flat.shape[0]
            logits = flat @ gate_W + gate_b
            top_v, top_i = jax.lax.top_k(logits, TOP_K)
            w = jax.nn.softmax(top_v, axis=-1)
            w_full = jnp.zeros((N, NUM_EXPERTS), flat.dtype)
            w_full = w_full.at[jnp.arange(N)[:, None], top_i].add(w)
            out = jnp.zeros_like(flat)
            for e in range(NUM_EXPERTS):
                mid = jax.nn.gelu(flat @ exp_W1[e] + exp_b1[e], approximate=False)
                y_e = mid @ exp_W2[e] + exp_b2[e]
                out = out + w_full[:, e:e + 1] * y_e
            return out.reshape(B, T, D)
        x = x + _attention(_layernorm(x, ln1_g, ln1_b), Wq, bq, Wk, bk, Wv, bv, Wp, bp)
        x = x + _token_moe(_layernorm(x, ln2_g, ln2_b), gate_W, gate_b, exp_W1, exp_b1, exp_W2, exp_b2)
        return x

    def _L1_attn_ref(x, w_qkv, w_out, b_out):
        import jax, jax.numpy as jnp
        import numpy as np
        NUM_HEADS = 16

        def _stablemax3_s(x):
            pos = 1.0 + x * (1.0 + 0.5 * x * (1.0 + x / 3.0))
            neg = 1.0 / (1.0 - x * (1.0 - 0.5 * x * (1.0 - x / 3.0)))
            return jnp.where(x >= 0, pos, neg)

        def stablemax3(logits, axis=-1):
            logits = logits - jnp.max(logits, axis=axis, keepdims=True)
            s = _stablemax3_s(logits)
            return s / jnp.sum(s, axis=axis, keepdims=True)
        B, S, D = x.shape
        H = NUM_HEADS
        hd = D // H
        scale = hd ** (-0.5)
        qkv = x @ w_qkv.T
        qkv = qkv.reshape(B, S, 3, H, hd)
        qkv = jnp.transpose(qkv, (2, 0, 3, 1, 4))
        q, k, v = (qkv[0], qkv[1], qkv[2])
        attn = jnp.einsum('bhsd,bhtd->bhst', q, k) * scale
        attn = stablemax3(attn, axis=-1)
        out = jnp.einsum('bhst,bhtd->bhsd', attn, v)
        out = jnp.transpose(out, (0, 2, 1, 3)).reshape(B, S, D)
        return out @ w_out.T + b_out

    def _L1_ffn_ref(x, w_q, keys, expert_down, expert_up, norm_w):
        import jax, jax.numpy as jnp
        import numpy as np
        B, T, D = (2, 256, 256)
        H, DK, K = (8, 128, 8)
        NKEYS = 64
        NEXP = NKEYS * NKEYS

        def _rmsnorm(x, w, eps=1e-06):
            inv = jax.lax.rsqrt(jnp.mean(x * x, axis=-1, keepdims=True) + eps)
            return x * inv * w
        b, t, d = x.shape
        xn = _rmsnorm(x, norm_w)
        q = (xn @ w_q.T).reshape(b, t, H, 2, DK)
        sim1 = jnp.einsum('bthd,hkd->bthk', q[..., 0, :], keys[:, :, 0, :])
        sim2 = jnp.einsum('bthd,hkd->bthk', q[..., 1, :], keys[:, :, 1, :])
        s1, i1 = jax.lax.top_k(sim1, K)
        s2, i2 = jax.lax.top_k(sim2, K)
        all_idx = (i1[..., :, None] * NKEYS + i2[..., None, :]).reshape(b, t, H, K * K)
        all_sc = (s1[..., :, None] + s2[..., None, :]).reshape(b, t, H, K * K)
        fs, pk = jax.lax.top_k(all_sc, K)
        fi = jnp.take_along_axis(all_idx, pk, axis=-1)
        wd = expert_down[fi]
        wu = expert_up[fi]
        hidden = jax.nn.gelu(jnp.einsum('btd,bthkd->bthk', xn, wd), approximate=False)
        hidden = hidden * jax.nn.relu(fs)
        return jnp.einsum('bthk,bthkd->btd', hidden, wu)
    h = _L0_tok_ref(L0_tok_log_dt, L0_tok_inv_A_real, L0_tok_A_imag, L0_tok_B_ri, x, 256)
    h = jnp.concatenate([jnp.broadcast_to(cls_tok, (h.shape[0], 1, h.shape[2])), h], axis=1)
    h = h + _L0_attn_ref(_layernorm(h, axis=-1), L0_attn_Wq, L0_attn_Wk, L0_attn_Wv, L0_attn_gn_weight, L0_attn_gn_bias, L0_attn_Wout)
    h = h + _L0_ffn_ref(_layernorm(h, axis=-1), L0_ffn_ln1_g, L0_ffn_ln1_b, L0_ffn_ln2_g, L0_ffn_ln2_b, L0_ffn_Wq, L0_ffn_bq, L0_ffn_Wk, L0_ffn_bk, L0_ffn_Wv, L0_ffn_bv, L0_ffn_Wp, L0_ffn_bp, L0_ffn_gate_W, L0_ffn_gate_b, L0_ffn_exp_W1, L0_ffn_exp_b1, L0_ffn_exp_W2, L0_ffn_exp_b2)
    h = h + _L1_attn_ref(_layernorm(h, axis=-1), L1_attn_w_qkv, L1_attn_w_out, L1_attn_b_out)
    h = h + _L1_ffn_ref(_layernorm(h, axis=-1), L1_ffn_w_q, L1_ffn_keys, L1_ffn_expert_down, L1_ffn_expert_up, L1_ffn_norm_w)
    return h

_drawn_inputs = setup_inputs


def setup_inputs(seed=0):
    import zlib

    import numpy as np

    out = dict(_drawn_inputs(seed))
    spreads = {'L0_attn_gn_weight': (1.0, 0.2),
     'L0_attn_gn_bias': (0.0, 0.32),
     'L0_ffn_ln1_g': (1.0, 0.6),
     'L0_ffn_ln1_b': (0.0, 0.8),
     'L0_ffn_ln2_g': (1.0, 0.6),
     'L0_ffn_ln2_b': (0.0, 0.8),
     'L0_ffn_bq': (0.0, 0.8),
     'L0_ffn_bk': (0.0, 0.8),
     'L0_ffn_bv': (0.0, 0.8),
     'L0_ffn_bp': (0.0, 0.406),
     'L0_ffn_gate_b': (0.0, 0.631),
     'L0_ffn_exp_b1': (0.0, 0.8),
     'L0_ffn_exp_b2': (0.0, 0.588),
     'L1_attn_b_out': (0.0, 0.433),
     'L1_ffn_norm_w': (1.0, 0.6)}
    factors = {'cls_tok': 3.425,
     'L0_ffn_Wq': 8.0,
     'L0_ffn_Wk': 8.0,
     'L0_ffn_Wv': 8.0,
     'L0_ffn_Wp': 7.2,
     'L0_ffn_gate_W': 3.055,
     'L0_ffn_exp_W1': 3.778,
     'L0_ffn_exp_W2': 3.54,
     'L1_attn_w_qkv': 8.0,
     'L1_attn_w_out': 8.0,
     'L1_ffn_w_q': 8.0,
     'L1_ffn_keys': 8.0,
     'L1_ffn_expert_down': 8.0,
     'L1_ffn_expert_up': 8.0}
    for name, (base, spread) in spreads.items():
        noise = np.random.default_rng([zlib.crc32(name.encode()), seed]).standard_normal(out[name].shape)
        drawn = base * np.exp(spread * noise) if base else spread * noise
        out[name] = jnp.asarray(drawn.astype(out[name].dtype))
    for name, factor in factors.items():
        out[name] = (out[name] * factor).astype(out[name].dtype)
    return out
```

```python
import math
from contextlib import ExitStack

import numpy as np

import concourse.bass as bass
from concourse import mybir

F32 = mybir.dt.float32
U32 = mybir.dt.uint32
ALU = mybir.AluOpType
ACT = mybir.ActivationFunctionType
AX = mybir.AxisListType

P = 128
B = 16
D = 256
DC = D // P
T = D + 1
NTOK = B * T
HEADS, HD = 16, 16
SLOT = 32
SLOTS = P // SLOT
HG = HEADS // SLOTS
GROUP = 512
NGROUPS = NTOK // GROUP
TAIL = NTOK - NGROUPS * GROUP
LN_EPS = 1e-5
RMS_EPS = 1e-6


class Chain:

    def __init__(self, engine, sem, per=0, turn=0, base=0):
        self.engine, self.sem, self.per, self.turn, self.base, self.count = engine, sem, per, turn, base, 0

    def link(self, instruction):
        instruction.then_inc(self.sem, 1)
        self.count += 1
        self.engine.wait_ge(self.sem, self.turn * self.per + self.base + self.count)

    def link_apart(self, instruction):
        self.link(instruction)
        self.engine.sem_inc(self.sem, 1)
        self.count += 1

    def done(self):
        assert self.count == self.per, (self.count, self.per)


class Room:

    def __init__(self, nc, ctx, name):
        self.nc, self.ctx, self.name, self.sems = nc, ctx, name, []
        ctx.callback(self.close)

    def close(self):
        self.nc.clear_and_free_semaphores(self.sems)
        self.nc.all_engine_barrier()

    def sb(self, name, shape, dt=F32):
        return self.ctx.enter_context(self.nc.sbuf_tensor(f"{self.name}_{name}", shape, dt))

    def ps(self, name, shape, dt=F32):
        return self.ctx.enter_context(self.nc.psum_tensor(f"{self.name}_{name}", shape, dt))

    def sem(self, name):
        self.sems.append(self.nc.alloc_semaphore(f"{self.name}_{name}"))
        return self.sems[-1]


L1 = 64
LA = D // L1
PAIRS = D // 2
PC = 16
LN2 = math.log(2.0)
LN2_HI = math.floor(LN2 * 2 ** 15) / 2 ** 15
LN2_LO = LN2 - LN2_HI
ROUND = 1.5 * 2 ** 23
EXP_TERMS = 8
TOK_LINKS = 75


def token_mixer(nc, log_dt, inv_A_real, A_imag, B_ri, C_ri, cls_tok, h_out):
    ctx = ExitStack()
    with ctx:
        r = Room(nc, ctx, "tok")
        par = r.sb("par", [P, 5, PC])
        c_ri = r.sb("c_ri", [P, 2, PC, B])
        ex = r.sb("ex", [P, 2, PC])
        two_k = r.sb("two_k", [P, PC], mybir.dt.int32)
        tmp = r.sb("tmp", [P, 6, PC])
        E = r.sb("E", [P, 2, 8, PC])
        V = r.sb("V", [P, 2, PC, L1])
        W = r.sb("W", [P, 2, PC, LA, B])
        prod = r.sb("prod", [P, 4, PC * 32])
        res = r.sb("res", [P, PC, L1])
        cls = r.sb("cls", [B, D])
        acc = r.ps("acc", [P, PC, L1])
        loaded, inputs_free = r.sem("loaded"), r.sem("inputs_free")
        exps, chained, powers_ready, products_done = r.sem("exps"), r.sem("chained"), r.sem("powers"), r.sem("products")
        res_ready, stored, cls_in, cls_out = r.sem("res_ready"), r.sem("stored"), r.sem("cls_in"), r.sem("cls_out")
        waits_passed = r.sem("waits_passed")
        turns = PAIRS // PC
        block = ctx.enter_context(nc.Block())

        @block.sync
        def _(sp):
            sp.dma_start(cls[:, :], cls_tok[0:1, :].broadcast_to([B, D])).then_inc(cls_in, 16)
            sp.wait_ge(cls_in, 16)
            sp.dma_start(h_out[:, 0, :], cls[:, :]).then_inc(cls_out, 16)
            sp.sem_inc(stored, 16)
            with sp.Fori(0, turns) as t:
                sp.wait_ge(inputs_free, t + 1)
                at = bass.ds(t * PC, PC)
                for h2 in range(2):
                    half = slice(64 * h2, 64 * h2 + 64)
                    sp.dma_start(par[half, 0, :], log_dt[h2:h2 + 1, at].broadcast_to([64, PC])).then_inc(loaded, 16)
                sp.dma_start(par[:, 1, :], inv_A_real[:, at]).then_inc(loaded, 16)
                sp.dma_start(par[:, 2, :], A_imag[:, at]).then_inc(loaded, 16)
                sp.dma_start(par[:, 3:5, :], B_ri[:, :, at]).then_inc(loaded, 16)
                sp.dma_start(c_ri[:, :, :, :], C_ri[:, :, at, :]).then_inc(loaded, 16)
                sp.wait_ge(res_ready, t + 2)
                for h2 in range(2):
                    for a in range(LA):
                        p0 = 64 * h2 + B * a
                        dst = h_out[:, bass.ds(1 + h2 + t * (2 * PC), PC, 2), L1 * a:L1 * a + L1]
                        sp.dma_start(dst, res[p0:p0 + B, :, :]).then_inc(stored, 16)
            sp.wait_ge(stored, 16 * 8 * turns + 16)
            sp.wait_ge(cls_out, 16)

        @block.scalar
        def _(act):
            act.sem_inc(res_ready, 1)
            with act.Fori(0, turns) as t:
                act.wait_ge(loaded, (t + 1) * 96)
                nc.scalar.activation(ex[:, 1, :], par[:, 1, :], ACT.Exp).then_inc(exps, 1)
                act.wait_ge(stored, t * 128 + 16)
                act.wait_ge(products_done, t + 2)
                nc.scalar.activation(res[:, :, :], acc[:, :, :], ACT.Copy, scale=2.0).then_inc(res_ready, 1)

        @block.vector
        def _(dve):
            nc.vector.memset(prod[:, :, 0:1], 0.0).then_inc(inputs_free, 1)
            v = nc.vector

            def products(chain, x, er, ei, n):
                shape = x[0].shape
                q = [prod[:, k, 0:n].rearrange("p (a b) -> p a b", a=shape[1]) if len(shape) == 3 else
                     prod[:, k, 0:n].rearrange("p (a b c) -> p a b c", a=shape[1], b=shape[2]) for k in range(4)]
                v.tensor_tensor(q[0], x[0], er, ALU.mult)
                v.tensor_tensor(q[1], x[1], ei, ALU.mult)
                v.tensor_tensor(q[2], x[0], ei, ALU.mult)
                chain.link(v.tensor_tensor(q[3], x[1], er, ALU.mult))
                return q

            with dve.Fori(0, turns) as t:
                chain = Chain(dve, chained, TOK_LINKS, t)
                link = chain.link
                a, b, den, x2, y2, na = (tmp[:, k, :] for k in range(6))
                dve.wait_ge(loaded, (t + 1) * 96)
                x, k_, rem, p, dt = par[:, 0, :], tmp[:, 0, :], tmp[:, 1, :], tmp[:, 2, :], ex[:, 0, :]
                link(v.tensor_scalar(k_, x, 1.0 / LN2, None, ALU.mult))
                link(v.tensor_scalar(k_, k_, ROUND, None, ALU.add))
                link(v.tensor_scalar(k_, k_, ROUND, None, ALU.subtract))
                link(v.tensor_scalar(k_, k_, -126.0, 127.0, ALU.max, ALU.min))
                link(v.scalar_tensor_tensor(rem, k_, -LN2_HI, x, ALU.mult, ALU.add))
                link(v.scalar_tensor_tensor(rem, k_, -LN2_LO, rem, ALU.mult, ALU.add))
                link(v.tensor_scalar(p, rem, 1.0 / math.factorial(EXP_TERMS), None, ALU.mult))
                for n in range(EXP_TERMS - 1, 0, -1):
                    link(v.scalar_tensor_tensor(p, p, 1.0 / math.factorial(n), rem, ALU.add, ALU.mult))
                link(v.tensor_scalar(two_k[:, :], k_, 127.0, float(1 << 23), ALU.add, ALU.mult))
                link(v.scalar_tensor_tensor(dt, p, 1.0, two_k[:, :].bitcast(F32), ALU.add, ALU.mult))
                dve.wait_ge(exps, t + 1)
                link(v.scalar_tensor_tensor(a, ex[:, 1, :], -0.5, dt, ALU.mult, ALU.mult))
                link(v.scalar_tensor_tensor(b, par[:, 2, :], 0.5, dt, ALU.mult, ALU.mult))
                link(v.tensor_scalar(na, a, -1.0, 1.0, ALU.mult, ALU.add))
                link(v.tensor_tensor(den, na, na, ALU.mult))
                link(v.tensor_tensor(y2, b, b, ALU.mult))
                link(v.tensor_tensor(den, den, y2, ALU.add))
                link(v.reciprocal(den, den))
                link(v.scalar_tensor_tensor(x2, a, -1.0, a, ALU.mult, ALU.mult))
                link(v.scalar_tensor_tensor(x2, x2, 1.0, y2, ALU.add, ALU.subtract))
                dve.wait_ge(products_done, t + 1)
                link(v.tensor_tensor(E[:, 0, 0, :], x2, den, ALU.mult))
                link(v.scalar_tensor_tensor(E[:, 1, 0, :], b, -2.0, den, ALU.mult, ALU.mult))
                for k in range(7):
                    link(v.tensor_tensor(x2, E[:, 0, k, :], E[:, 0, k, :], ALU.mult))
                    link(v.tensor_tensor(y2, E[:, 1, k, :], E[:, 1, k, :], ALU.mult))
                    link(v.scalar_tensor_tensor(E[:, 1, k + 1, :], E[:, 0, k, :], 2.0, E[:, 1, k, :], ALU.mult, ALU.mult))
                    link(v.tensor_tensor(E[:, 0, k + 1, :], x2, y2, ALU.subtract))
                link(v.memset(V[:, 0, :, 0:1], 1.0))
                link(v.memset(V[:, 1, :, 0:1], 0.0))
                for k in range(6):
                    n = 1 << k
                    e = [E[:, c, k, :].rearrange("p (a b) -> p a b", b=1).broadcast_to([P, PC, n]) for c in range(2)]
                    q = products(chain, [V[:, c, :, 0:n] for c in range(2)], e[0], e[1], PC * n)
                    v.tensor_tensor(V[:, 0, :, n:2 * n], q[0], q[1], ALU.subtract)
                    link(v.tensor_tensor(V[:, 1, :, n:2 * n], q[2], q[3], ALU.add))
                bb = [par[:, 3 + c, :].rearrange("p (a b) -> p a b", b=1).broadcast_to([P, PC, B]) for c in range(2)]
                q = products(chain, [c_ri[:, c, :, :] for c in range(2)], bb[0], bb[1], PC * B)
                v.tensor_tensor(W[:, 0, :, 0, :], q[0], q[1], ALU.subtract)
                last = v.tensor_tensor(W[:, 1, :, 0, :], q[2], q[3], ALU.add)
                link(last)
                v.memset(prod[:, :, 0:1], 0.0).then_inc(inputs_free, 1)
                dve.wait_ge(inputs_free, t + 2)
                for k, s in ((6, 1), (7, 2)):
                    e = [E[:, c, k, :].rearrange("p (a b) -> p a b", b=1).broadcast_to([P, PC, s * B]) for c in range(2)]
                    w = [W[:, c, :, :, :].rearrange("p a s c -> p a (s c)") for c in range(2)]
                    q = products(chain, [w[c][:, :, 0:s * B] for c in range(2)], e[0], e[1], PC * s * B)
                    v.tensor_tensor(w[0][:, :, s * B:2 * s * B], q[0], q[1], ALU.add)
                    link(v.tensor_tensor(w[1][:, :, s * B:2 * s * B], q[3], q[2], ALU.subtract))
                v.memset(prod[:, :, 0:1], 0.0).then_inc(powers_ready, 1)
                dve.wait_ge(powers_ready, t + 1)
                chain.done()

        @block.tensor
        def _(pe):
            pe.sem_inc(products_done, 1)
            with pe.Fori(0, turns) as t:
                pe.wait_ge(powers_ready, t + 1)
                pe.wait_ge(res_ready, t + 1)
                pe.sem_inc(waits_passed, 1)
                for i in range(PC):
                    for h2 in range(2):
                        half = slice(64 * h2, 64 * h2 + 64)
                        for c in range(2):
                            last = nc.tensor.matmul(acc[half, i, :], W[half, c, i, :, :].rearrange("p a c -> p (a c)"),
                                                    V[half, c, i, :], start=c == 0, stop=c == 1)
                last.then_inc(products_done, 1)


def groups(engine, step):
    with engine.Fori(0, NGROUPS) as g:
        step(g * GROUP, g, GROUP // P, P)
    step(NGROUPS * GROUP, NGROUPS, 1, TAIL)


def tokens(ap, t0, tiles, rows):
    return ap[bass.ds(t0, tiles * rows), :].rearrange("(j p) d -> p j d", p=rows)


def statistics(v, chain, x, stats, mv, ve, tiles, rows, eps):
    for j in range(tiles):
        last = v.bn_stats(stats[:rows, j, :], x[:rows, j, :])
    chain.link_apart(last)
    for j in range(tiles):
        last = v.bn_aggr(mv[:rows, j, :], stats[:rows, j, :])
    chain.link(last)
    return v.tensor_scalar(ve[:rows, 0:tiles], mv[:rows, 0:tiles, 1], eps, None, ALU.add)


def normalise(v, x, out, mv, rstd, tiles, rows):
    for j in range(tiles):
        last = v.tensor_scalar(out[:rows, j, :], x[:rows, j, :], mv[:rows, j, 0:1], rstd[:rows, j:j + 1],
                               ALU.subtract, ALU.mult)
    return last


def transposed(nc, out, x, ident, tiles, rows):
    for c in range(DC):
        for j in range(tiles):
            last = nc.tensor.transpose(out[:, c, j * P:j * P + rows], x[:rows, j, c * P:c * P + P],
                                       ident[:rows, :rows])
    return last


def enter_retention(nc, h, ident_in, xT_out):
    ctx = ExitStack()
    with ctx:
        r = Room(nc, ctx, "ent")
        ident = r.sb("ident", [P, P])
        hs = r.sb("hs", [P, 2, 4, D])
        xn = r.sb("xn", [P, 4, D])
        xt = r.sb("xt", [P, DC, GROUP])
        stats, mv = r.sb("stats", [P, 4, 6]), r.sb("mv", [P, 4, 2])
        ve, rstd, minus_half = r.sb("ve", [P, 4]), r.sb("rstd", [P, 4]), r.sb("mh", [P, 4])
        tp = r.ps("tp", [P, DC, GROUP])
        const_in, loaded, h_free = r.sem("const_in"), r.sem("loaded"), r.sem("h_free")
        const_made, chained, var_ready, rstd_ready = r.sem("const_made"), r.sem("chained"), r.sem("var"), r.sem("rstds")
        xn_ready, tp_ready, xt_ready, stored = r.sem("xn_ready"), r.sem("tp_ready"), r.sem("xt_ready"), r.sem("stored")
        block = ctx.enter_context(nc.Block())

        @block.sync
        def _(sp):
            sp.dma_start(ident[:, :], ident_in).then_inc(const_in, 16)

            def step(t0, g, tiles, rows):
                sp.wait_ge(h_free, g + 1)
                sp.dma_start(hs[:rows, 0, 0:tiles, :], tokens(h, t0, tiles, rows)).then_inc(loaded, 16)
            groups(sp, step)

        @block.vector
        def _(dve):
            v = nc.vector
            dve.sem_inc(h_free, 1)

            def step(t0, g, tiles, rows):
                chain = Chain(dve, chained, 3, g)
                dve.wait_ge(loaded, g * 16 + 16)
                statistics(v, chain, hs[:, 0], stats, mv, ve, tiles, rows, LN_EPS).then_inc(var_ready, 1)
                dve.wait_ge(rstd_ready, g + 1)
                dve.wait_ge(tp_ready, g + 1)
                normalise(v, hs[:, 0], xn, mv, rstd, tiles, rows).then_inc(xn_ready, 1)
                dve.wait_ge(xn_ready, g + 1)
                dve.sem_inc(h_free, 1)
                chain.done()
            groups(dve, step)

        @block.gpsimd
        def _(pool):
            nc.gpsimd.memset(minus_half[:, :], -0.5).then_inc(const_made, 1)
            pool.wait_ge(const_made, 1)

            def step(t0, g, tiles, rows):
                pool.wait_ge(var_ready, g + 1)
                nc.gpsimd.tensor_tensor(rstd[:rows, 0:tiles], ve[:rows, 0:tiles], minus_half[:rows, 0:tiles],
                                        ALU.pow).then_inc(rstd_ready, 1)
            groups(pool, step)

        @block.tensor
        def _(pe):
            pe.sem_inc(tp_ready, 1)
            pe.wait_ge(const_in, 16)

            def step(t0, g, tiles, rows):
                pe.wait_ge(xt_ready, g + 1)
                pe.wait_ge(xn_ready, g + 1)
                transposed(nc, tp, xn, ident, tiles, rows).then_inc(tp_ready, 1)
            groups(pe, step)

        @block.scalar
        def _(act):
            act.sem_inc(xt_ready, 1)
            act.sem_inc(stored, 16)

            def step(t0, g, tiles, rows):
                act.wait_ge(stored, g * 16 + 16)
                act.wait_ge(tp_ready, g + 2)
                n = tiles * rows
                nc.scalar.activation(xt[:, :, 0:n], tp[:, :, 0:n], ACT.Copy).then_inc(xt_ready, 1)
                act.wait_ge(xt_ready, g + 2)
                act.dma_start(xT_out[:, bass.ds(t0, n)].rearrange("(c p) t -> p c t", p=P),
                              xt[:, :, 0:n]).then_inc(stored, 16)
            groups(act, step)
            act.wait_ge(stored, 16 * (NGROUPS + 2))


ODD = T - 1
SPAN = T + (T - P)
PAIRS_OF_HEADS = HEADS // 2
PROJ = 2 * HG + DC + 1
SCALE = HD ** -0.5


def slot(head):
    return head // SLOTS, slice(SLOT * (head % SLOTS), SLOT * (head % SLOTS) + HD)


def retention(nc, xT_in, wq, wk, wv, gnw_in, gnb_in, decay_in, own_in, sel_in, avg_in, cT_out):
    ctx = ExitStack()
    with ctx:
        r = Room(nc, ctx, "ret")
        wq_s, wk_s, wv_s = (r.sb(n, [P, DC, 512]) for n in ("wq", "wk", "wv"))
        decay = r.sb("decay", [P, HEADS, SPAN])
        own = r.sb("own", [HEADS, 512])
        sel = r.sb("sel", [P, HG, HEADS])
        avg = r.sb("avg", [P, P])
        gnw, gnb = r.sb("gnw", [P, HG]), r.sb("gnb", [P, HG])
        xT = r.sb("xT", [P, DC, T])
        odd_x = r.sb("odd_x", [P, DC, HEADS])
        QT, KT = r.sb("QT", [P, HG, T]), r.sb("KT", [P, HG, T])
        V = r.sb("V", [P, DC, 512])
        v_odd, V_odd = r.sb("v_odd", [HEADS, 512]), r.sb("V_odd", [HEADS, 512])
        K_odd = r.sb("K_odd", [P, HG, HEADS])
        p_odd = r.sb("p_odd", [HEADS, 1])
        PT = r.sb("PT", [P, 2, 2, SPAN])
        cT, cN = r.sb("cT", [P, HG, T]), r.sb("cN", [P, HG, T])
        stats, mv = r.sb("stats", [P, HG, 6]), r.sb("mv", [P, HG, 2])
        d, q, ve, rstd, mh = (r.sb(n, [P, HG]) for n in ("d", "q", "ve", "rstd", "mh"))
        gmean, gscale, gbias = (r.sb(n, [P, HG]) for n in ("gmean", "gscale", "gbias"))
        S = r.ps("S", [P, 2, 2, 512])
        O = r.ps("O", [P, 2, 512])
        proj = r.ps("proj", [P, 2, 512])
        const_in, loaded, x_free = r.sem("const_in"), r.sem("loaded"), r.sem("x_free")
        proj_ready, proj_taken, odd_ready, odd_copied = (r.sem(n) for n in ("proj_ready", "proj_taken", "odd_ready", "odd_x"))
        s_ready, p_ready, av_done = r.sem("s_ready"), r.sem("p_ready"), r.sem("av_done")
        o_ready, o_taken, so_ready, so_taken = (r.sem(n) for n in ("o_ready", "o_taken", "so_ready", "so_taken"))
        chained, means_ready, gm_ready, gv_ready, q_ready = (r.sem(n) for n in ("chained", "means", "gm", "gv", "q"))
        ve_ready, rstd_ready, affine_ready, normed, stored = (r.sem(n) for n in ("ve", "rstd", "affine", "normed", "stored"))
        const_made = r.sem("const_made")
        block = ctx.enter_context(nc.Block())

        @block.sync
        def _(sp):
            for dst, src in ((wq_s, wq), (wk_s, wk), (wv_s, wv)):
                sp.dma_start(dst[:, :, :], src.rearrange("(c p) n -> p c n", p=P)).then_inc(const_in, 16)
            for dst, src in ((own, own_in), (avg, avg_in), (gnw, gnw_in), (gnb, gnb_in)):
                sp.dma_start(dst[:, :], src).then_inc(const_in, 16)
            sp.dma_start(sel[:, :, :], sel_in).then_inc(const_in, 16)
            sp.dma_start(decay[:, :, :], decay_in).then_inc(const_in, 16)
            with sp.Fori(0, B) as b:
                sp.wait_ge(x_free, b + 1)
                sp.dma_start(xT[:, :, :], xT_in[:, bass.ds(b * T, T)].rearrange("(c p) t -> p c t", p=P))\
                  .then_inc(loaded, 16)
                sp.wait_ge(normed, b + 1)
                for s in range(SLOTS):
                    dst = cT_out[:, bass.ds(b * T, T)].rearrange("(g s e) t -> s e g t", g=HG, s=SLOTS)
                    sp.dma_start(dst[s], cN[SLOT * s:SLOT * s + HD, :, :]).then_inc(stored, 16)
            sp.wait_ge(stored, 16 * (SLOTS * B + 1))

        @block.tensor
        def _(pe):
            pe.wait_ge(const_in, 144)
            for s in (s_ready, av_done, x_free):
                pe.sem_inc(s, 1)
            with pe.Fori(0, B) as b:
                pe.wait_ge(loaded, b * 16 + 16)

                def take_bank(n):
                    if n != 1:
                        pe.wait_ge(proj_taken, b * PROJ + 1 + (n - 1 if n else 0))
                    else:
                        pe.wait_ge(affine_ready, b + 1)

                for n in range(2 * HG):
                    take_bank(n)
                    w, g = (wq_s, wk_s)[n // HG], n % HG
                    for c in range(DC):
                        last = nc.tensor.matmul(proj[:, n % 2, 0:T], w[:, c, g * P:g * P + P], xT[:, c, :],
                                                start=c == 0, stop=c == DC - 1)
                    last.then_inc(proj_ready, 1)
                for k in range(DC):
                    n = 2 * HG + k
                    take_bank(n)
                    for c in range(DC):
                        last = nc.tensor.matmul(proj[:, n % 2, :], xT[:, c, k * P:k * P + P], wv_s[:, c, :],
                                                start=c == 0, stop=c == DC - 1)
                    last.then_inc(proj_ready, 1)
                n = PROJ - 1
                take_bank(n)
                pe.wait_ge(odd_copied, b + 1)
                for c in range(DC):
                    last = nc.tensor.matmul(proj[:HEADS, n % 2, :], odd_x[:, c, :], wv_s[:, c, :],
                                            start=c == 0, stop=c == DC - 1)
                last.then_inc(proj_ready, 1)
                pe.wait_ge(proj_taken, b * PROJ + 1 + PROJ)
                pe.sem_inc(x_free, 1)

                def scores(u):
                    pe.wait_ge(p_ready, b * PAIRS_OF_HEADS + u if u else b * PAIRS_OF_HEADS + 1)
                    for i in range(2):
                        g, rows = slot(2 * u + i)
                        nc.tensor.matmul(S[:, u % 2, i, 0:T], KT[rows, g, 0:P], QT[rows, g, :], start=True, stop=True)
                        last = nc.tensor.matmul(S[:, u % 2, i, T:SPAN], KT[rows, g, P:2 * P], QT[rows, g, P:T],
                                                start=True, stop=True)
                    last.then_inc(s_ready, 1)

                pe.wait_ge(odd_ready, 2 * b + 2)
                pe.wait_ge(so_taken, b + 1)
                for g in range(HG):
                    last = nc.tensor.matmul(O[:HEADS, 1, 511:512], K_odd[:, g, :], QT[:, g, ODD:T],
                                            start=g == 0, stop=g == HG - 1)
                last.then_inc(so_ready, 1)
                scores(0)
                for u in range(PAIRS_OF_HEADS):
                    if u + 1 < PAIRS_OF_HEADS:
                        scores(u + 1)
                    g = u // 2
                    pe.wait_ge(p_ready, b * PAIRS_OF_HEADS + u + 2)
                    if u == 1:
                        pe.wait_ge(so_taken, b + 2)
                    if u % 2 == 0:
                        pe.wait_ge(o_taken, b * HG + max(g, 1))
                        pe.wait_ge(o_taken, 1)
                    for i in range(2):
                        rows = slice(SLOT * (2 * (u % 2) + i), SLOT * (2 * (u % 2) + i) + SLOT)
                        at = slice(SLOT * (2 * u + i), SLOT * (2 * u + i) + SLOT)
                        nc.tensor.matmul(O[rows, g % 2, 0:T], V[:, 0, at], PT[:, u % 2, i, 0:T],
                                         start=True, stop=False, skip_group_check=True)
                        last = nc.tensor.matmul(O[rows, g % 2, P:T], V[:, 1, at], PT[:, u % 2, i, T:SPAN],
                                                start=False, stop=False, skip_group_check=True)
                    last.then_inc(av_done, 1)
                    if u % 2:
                        nc.tensor.matmul(O[:, g % 2, ODD:T], V_odd[:, g * P:g * P + P], p_odd[:, :],
                                         start=False, stop=True, skip_group_check=True).then_inc(o_ready, 1)
                pe.wait_ge(means_ready, b + 1)
                nc.tensor.matmul(proj[:, 1, 0:HG], avg[:, :], mv[:, :, 0], start=True, stop=True).then_inc(gm_ready, 1)
                pe.wait_ge(q_ready, b + 1)
                nc.tensor.matmul(proj[:, 1, 0:HG], avg[:, :], q[:, :], start=True, stop=True).then_inc(gv_ready, 1)

        @block.scalar
        def _(act):
            act.sem_inc(proj_taken, 1)
            act.sem_inc(o_taken, 1)
            act.sem_inc(so_taken, 1)
            act.sem_inc(stored, 16)
            with act.Fori(0, B) as b:
                for n in range(PROJ):
                    act.wait_ge(proj_ready, b * PROJ + n + 1)
                    if n < 2 * HG:
                        dst, src = (QT, KT)[n // HG][:, n % HG, :], proj[:, n % 2, 0:T]
                    elif n < PROJ - 1:
                        dst, src = V[:, n - 2 * HG, :], proj[:, n % 2, :]
                    else:
                        dst, src = v_odd[:, :], proj[:HEADS, n % 2, :]
                    nc.scalar.activation(dst, src, ACT.Copy).then_inc(proj_taken, 1)
                act.wait_ge(so_ready, b + 1)
                nc.scalar.activation(p_odd[:, :], O[:HEADS, 1, 511:512], ACT.Copy, scale=SCALE).then_inc(so_taken, 1)
                for g in range(HG):
                    act.wait_ge(o_ready, b * HG + g + 1)
                    nc.scalar.activation(cT[:, g, :], O[:, g % 2, 0:T], ACT.Copy).then_inc(o_taken, 1)
                act.wait_ge(affine_ready, b + 2)
                act.wait_ge(stored, b * 16 * SLOTS + 16)
                for g in range(HG):
                    last = nc.scalar.activation(cN[:, g, :], cT[:, g, :], ACT.Identity, bias=gbias[:, g:g + 1],
                                                scale=gscale[:, g:g + 1])
                last.then_inc(normed, 1)

        @block.vector
        def _(dve):
            v = nc.vector
            dve.wait_ge(const_in, 144)
            dve.sem_inc(p_ready, 1)
            dve.sem_inc(affine_ready, 1)
            with dve.Fori(0, B) as b:
                chain = Chain(dve, chained, 8, b)
                for u in range(PAIRS_OF_HEADS):
                    dve.wait_ge(s_ready, b * PAIRS_OF_HEADS + u + 2)
                    dve.wait_ge(av_done, b * PAIRS_OF_HEADS + max(u, 1))
                    v.tensor_tensor(PT[:, u % 2, :, :], S[:, u % 2, :, 0:SPAN], decay[:, 2 * u:2 * u + 2, :],
                                    ALU.mult).then_inc(p_ready, 1)
                for g in range(HG):
                    dve.wait_ge(o_taken, b * HG + g + 2)
                    last = v.bn_stats(stats[:, g, :], cT[:, g, :])
                chain.link_apart(last)
                for g in range(HG):
                    last = v.bn_aggr(mv[:, g, :], stats[:, g, :])
                last.then_inc(means_ready, 1)
                dve.wait_ge(gm_ready, b + 1)
                dve.wait_ge(means_ready, b + 1)
                v.tensor_copy(gmean[:, :], proj[:, 1, 0:HG])
                chain.link(v.tensor_tensor(d[:, :], mv[:, :, 0], proj[:, 1, 0:HG], ALU.subtract))
                chain.link(v.tensor_tensor(d[:, :], d[:, :], d[:, :], ALU.mult))
                v.tensor_tensor(q[:, :], d[:, :], mv[:, :, 1], ALU.add).then_inc(q_ready, 1)
                dve.wait_ge(gv_ready, b + 1)
                v.tensor_scalar(ve[:, :], proj[:, 1, 0:HG], LN_EPS, None, ALU.add).then_inc(ve_ready, 1)
                dve.wait_ge(rstd_ready, b + 1)
                chain.link(v.tensor_tensor(gscale[:, :], rstd[:, :], gnw[:, :], ALU.mult))
                chain.link(v.tensor_tensor(d[:, :], gmean[:, :], gscale[:, :], ALU.mult))
                chain.link(v.tensor_tensor(gbias[:, :], gnb[:, :], d[:, :], ALU.subtract))
                chain.link(v.tensor_copy(q[:, :], d[:, :]))
                dve.sem_inc(affine_ready, 1)
                chain.done()

        @block.gpsimd
        def _(pool):
            pool.wait_ge(const_in, 144)
            nc.gpsimd.memset(mh[:, :], -0.5).then_inc(const_made, 1)
            pool.wait_ge(const_made, 1)
            with pool.Fori(0, B) as b:
                pool.wait_ge(loaded, b * 16 + 16)
                pool.sem_inc(const_made, 1)
                nc.gpsimd.tensor_copy(odd_x[:, :, :], xT[:, :, ODD:T].broadcast_to([P, DC, HEADS])).then_inc(odd_copied, 1)
                pool.wait_ge(proj_taken, b * PROJ + 1 + 2 * HG)
                nc.gpsimd.tensor_tensor(K_odd[:, :, :], KT[:, :, ODD:T].broadcast_to([P, HG, HEADS]), sel[:, :, :],
                                        ALU.mult).then_inc(odd_ready, 1)
                pool.wait_ge(proj_taken, b * PROJ + 1 + PROJ)
                nc.gpsimd.tensor_tensor(V_odd[:, :], v_odd[:, :], own[:, :], ALU.mult).then_inc(odd_ready, 1)
                pool.wait_ge(ve_ready, b + 1)
                nc.gpsimd.tensor_tensor(rstd[:, :], ve[:, :], mh[:, :], ALU.pow).then_inc(rstd_ready, 1)


N_ODD = 4
DVE_LINKS = {True: 4, False: 6}
BF16 = mybir.dt.bfloat16
VC = HD + 1
BIG = -1e30


def attention(nc, causal, xT_in, wq, wk, wv, bq_in, bk_in, bv_in, own_in, sel_in, aug_in, ident_in, mask_in, aT_out):
    ctx = ExitStack()
    with ctx:
        r = Room(nc, ctx, "soft" if causal else "stable")
        wq_s, wk_s, wv_s = r.sb("wq", [P, DC, 512]), r.sb("wk", [P, DC, 512]), r.sb("wv", [P, DC, D])
        bq, bk = r.sb("bq", [P, HG]), r.sb("bk", [P, HG])
        bv = r.sb("bv", [P, HEADS, HD])
        own = r.sb("own", [HEADS, HEADS, VC])
        sel = r.sb("sel", [P, HG, HEADS])
        aug = r.sb("aug", [HEADS, HG, P])
        ident, ident_b = r.sb("ident", [P, P]), r.sb("ident_b", [P, P], BF16)
        mask = r.sb("mask", [P, 2, P], BF16)
        ones = r.sb("ones", [HEADS, 1])
        xT = r.sb("xT", [P, DC, T])
        odd_x = r.sb("odd_x", [P, DC, HEADS])
        QT, KT = r.sb("QT", [P, HG, T]), r.sb("KT", [P, HG, T])
        V = r.sb("V", [P, 2, HEADS, VC])
        v_odd, V_odd = r.sb("v_odd", [HEADS, HEADS, VC]), r.sb("V_odd", [HEADS, HEADS, VC])
        K_odd, Q_odd = r.sb("K_odd", [P, HG, HEADS]), r.sb("Q_odd", [P, HG, HEADS])
        negmax, negmax_T = r.sb("negmax", [P, 2, HEADS]), r.sb("negmax_T", [HEADS, T])
        W, Yb = r.sb("W", [P, 2, 2, 512]), r.sb("Y", [P, 2, 2, 512])
        w_oq, y_oq = r.sb("w_oq", [P, 2, HEADS]), r.sb("y_oq", [P, 2, HEADS])
        w_ok, y_ok = r.sb("w_ok", [HEADS, T]), r.sb("y_ok", [HEADS, T])
        oq = r.sb("oq", [HEADS, HEADS, VC])
        rsum, rsum_odd = r.sb("rsum", [P, 2, HEADS]), r.sb("rsum_odd", [1, HEADS])
        a, a_odd = r.sb("a", [P, 2, D]), r.sb("a_odd", [1, D])
        aT = r.sb("aT", [P, DC, T])
        S = r.ps("S", [P, 2, 2, 512])
        O = r.ps("O", [P, 2, 512])
        misc = r.ps("misc", [P, 2, 512])
        const_in, loaded, x_free, stored = r.sem("const_in"), r.sem("loaded"), r.sem("x_free"), r.sem("stored")
        ones_made, x_odd_ready, odd_ready, passed = r.sem("ones_made"), r.sem("x_odd"), r.sem("odd"), r.sem("passed")
        max_done = r.sem("max_done")
        misc_ready, taken_act, taken_dve = r.sem("misc_ready"), r.sem("taken_act"), r.sem("taken_dve")
        max_s_ready, max_taken, s_ready, s_taken = (r.sem(n) for n in ("max_s", "max_taken", "s_ready", "s_taken"))
        y_ready, t_ready, w_ready, av_done = r.sem("y"), r.sem("t"), r.sem("w"), r.sem("av")
        oy_ready, ot_ready, ow_ready = r.sem("oy"), r.sem("ot"), r.sem("ow")
        o_ready, o_taken, a_ready, aT_ready = r.sem("o_ready"), r.sem("o_taken"), r.sem("a"), r.sem("aT")
        chained, act_chained = r.sem("chained"), r.sem("act_chained")
        NP_ = PAIRS_OF_HEADS
        nq = 1 if causal else T
        n_const = 11

        units = [(f"q{g}", "act") for g in range(HG)] + [(f"k{g}", "act") for g in range(HG)]
        units += [("v0", "act"), ("v1", "act"), ("v_odd", "act")]
        units += [] if causal else [("odd_key_max", "dve")]
        units += [("odd_query_max", "dve"), ("negmax_T", "dve")] + [(f"aug{g}", "dve") for g in range(HG)]
        taker = "act" if causal else "dve"
        units += [("odd_query", taker), ("odd_key", taker), ("odd_out", "dve"), ("odd_row", "dve")]
        units += [("aT0", "act"), ("aT1", "act")]
        index = {name: n for n, (name, _) in enumerate(units)}
        per_taker = {who: sum(w == who for _, w in units) for who in ("act", "dve")}
        taken = {"act": taken_act, "dve": taken_dve}

        def taken_count(n):
            return sum(w == units[n][1] for _, w in units[:n + 1])

        def wait_taken(engine, b, name):
            n = index[name]
            engine.wait_ge(taken[units[n][1]], b * per_taker[units[n][1]] + taken_count(n) + 1)

        def wait_misc(engine, b, name):
            engine.wait_ge(misc_ready, b * len(units) + index[name] + 1)
            return misc[:, index[name] % 2, :]

        block = ctx.enter_context(nc.Block())

        @block.sync
        def _(sp):
            for dst, src in ((wq_s, wq), (wk_s, wk), (wv_s, wv)):
                sp.dma_start(dst[:, :, :], src.rearrange("(c p) n -> p c n", p=P)).then_inc(const_in, 16)
            for dst, src in ((bq, bq_in), (bk, bk_in), (ident, ident_in)):
                sp.dma_start(dst[:, :], src).then_inc(const_in, 16)
            sp.dma_start(bv[:, :, :].rearrange("p h e -> p (h e)"), bv_in.broadcast_to([P, D])).then_inc(const_in, 16)
            for dst, src in ((own, own_in), (sel, sel_in), (aug, aug_in), (mask, mask_in)):
                sp.dma_start(dst[:, :, :], src).then_inc(const_in, 16)
            with sp.Fori(0, B) as b:
                sp.wait_ge(x_free, b + 1)
                sp.dma_start(xT[:, :, :], xT_in[:, bass.ds(b * T, T)].rearrange("(c p) t -> p c t", p=P))\
                  .then_inc(loaded, 16)
                wait_taken(sp, b, "aT1")
                sp.dma_start(aT_out[:, bass.ds(b * T, T)].rearrange("(c p) t -> p c t", p=P), aT[:, :, :])\
                  .then_inc(stored, 16)
            sp.wait_ge(stored, 16 * B + 16)

        @block.tensor
        def _(pe):
            mm = nc.tensor.matmul
            pe.wait_ge(const_in, 16 * n_const)
            pe.wait_ge(ones_made, 4)
            pe.sem_inc(x_free, 1)
            pe.sem_inc(av_done, 1)
            with pe.Fori(0, B) as b:
                pe.wait_ge(loaded, b * 16 + 16)

                def stand():
                    pe.sem_inc(passed, 1)

                def bank(name):
                    n = index[name]
                    if n >= 2:
                        wait_taken(pe, b, units[n - 2][0])
                    else:
                        pe.wait_ge(taken_act, b * per_taker["act"] + 1)
                        pe.wait_ge(taken_dve, b * per_taker["dve"] + 1)
                    stand()
                    return misc[:, n % 2, :]

                for w, what in ((wq_s, "q"), (wk_s, "k")):
                    for g in range(HG):
                        out = bank(f"{what}{g}")
                        for c in range(DC):
                            last = mm(out[:, 0:T], w[:, c, g * P:g * P + P], xT[:, c, :], start=c == 0, stop=c == DC - 1)
                        last.then_inc(misc_ready, 1)
                for k in range(2):
                    out = bank(f"v{k}")
                    for c in range(DC):
                        last = mm(out[:, 0:D], xT[:, c, k * P:k * P + P], wv_s[:, c, :], start=c == 0, stop=c == DC - 1)
                    last.then_inc(misc_ready, 1)
                pe.wait_ge(x_odd_ready, b + 1)
                out = bank("v_odd")
                for c in range(DC):
                    last = mm(out[:HEADS, 0:D], odd_x[:, c, :], wv_s[:, c, :], start=c == 0, stop=c == DC - 1)
                last.then_inc(misc_ready, 1)
                wait_taken(pe, b, "v_odd")
                pe.sem_inc(x_free, 1)

                for u in range(NP_):
                    pe.wait_ge(max_taken, b * NP_ + max(u, 1))
                    pe.wait_ge(s_taken, b * NP_ + 1)
                    stand()
                    for i in range(2):
                        g, rows = slot(2 * u + i)
                        out = S[:, u % 2, i, :]
                        if causal:
                            mm(out[:, 0:P], QT[rows, g, 0:P], KT[rows, g, 0:P], start=True, stop=True,
                               skip_group_check=True)
                            last = mm(out[:, P:3 * P], QT[rows, g, P:2 * P], KT[rows, g, 0:2 * P], start=False, stop=True,
                                      skip_group_check=True)
                        else:
                            for k in range(2):
                                last = mm(out[:, k * D:k * D + D], QT[rows, g, k * P:k * P + P], KT[rows, g, 0:D],
                                          start=True, stop=True)
                    if causal:
                        for i in range(2):
                            for at in (0, 2 * P):
                                last = mm(S[:, u % 2, i, at:at + P], ident_b[:, :], mask[:, 0, :], start=False, stop=True,
                                          skip_group_check=True)
                    last.then_inc(max_s_ready, 1)
                if not causal:
                    out = bank("odd_key_max")
                    pe.wait_ge(odd_ready, b * N_ODD + 3)
                    stand()
                    for k in range(2):
                        for g in range(HG):
                            last = mm(out[:, k * HEADS:k * HEADS + HEADS], QT[:, g, k * P:k * P + P], K_odd[:, g, :],
                                      start=g == 0, stop=g == HG - 1)
                    last.then_inc(misc_ready, 1)
                out = bank("odd_query_max")
                pe.wait_ge(odd_ready, b * N_ODD + 3)
                stand()
                for g in range(HG):
                    last = mm(out[:HEADS, 0:T], Q_odd[:, g, :], KT[:, g, :], start=g == 0, stop=g == HG - 1)
                last.then_inc(misc_ready, 1)
                out = bank("negmax_T")
                pe.wait_ge(max_done, b + 1)
                stand()
                for k in range(2):
                    last = nc.tensor.transpose(out[:HEADS, k * P:k * P + P], negmax[:, k, :], ident[:, :])
                last.then_inc(misc_ready, 1)
                for g in range(HG):
                    out = bank(f"aug{g}")
                    wait_taken(pe, b, "negmax_T")
                    stand()
                    mm(out[:, 0:T], aug[:, g, :], negmax_T[:, :], start=True, stop=True).then_inc(misc_ready, 1)

                out = bank("odd_query")
                pe.wait_ge(odd_ready, b * N_ODD + 4)
                stand()
                for k in range(2):
                    for g in range(HG):
                        last = mm(out[:, k * HEADS:k * HEADS + HEADS], KT[:, g, k * P:k * P + P], Q_odd[:, g, :],
                                  start=g == 0, stop=g == HG - 1)
                last.then_inc(misc_ready, 1)
                out = bank("odd_key")
                for g in range(HG):
                    last = mm(out[:HEADS, 0:nq], K_odd[:, g, :], QT[:, g, T - nq:T], start=g == 0, stop=g == HG - 1)
                last.then_inc(misc_ready, 1)

                def scores(u):
                    pe.wait_ge(s_taken, b * NP_ + max(u, 1))
                    pe.wait_ge(max_taken, b * NP_ + 1 + NP_)
                    stand()
                    for i in range(2):
                        h = 2 * u + i
                        g, rows = h // SLOTS, slice(SLOT * (h % SLOTS), SLOT * (h % SLOTS) + HD + 1)
                        out = S[:, u % 2, i, :]
                        if causal:
                            mm(out[:, 0:2 * P], KT[rows, g, 0:P], QT[rows, g, 0:2 * P], start=True, stop=True,
                               skip_group_check=True)
                            last = mm(out[:, 2 * P:3 * P], KT[rows, g, P:2 * P], QT[rows, g, P:2 * P], start=False,
                                      stop=True, skip_group_check=True)
                        else:
                            for k in range(2):
                                last = mm(out[:, k * D:k * D + D], KT[rows, g, k * P:k * P + P], QT[rows, g, 0:D],
                                          start=True, stop=True)
                    if causal:
                        for i in range(2):
                            for at in (0, 2 * P):
                                last = mm(S[:, u % 2, i, at:at + P], ident_b[:, :], mask[:, 1, :], start=False, stop=True,
                                          skip_group_check=True)
                    last.then_inc(s_ready, 1)

                def products(u):
                    pe.wait_ge(w_ready, b * NP_ + u + 1)
                    stand()
                    for i in range(2):
                        h = 2 * u + i
                        for k in range(2):
                            if causal:
                                blocks = [(0, 0)] if k == 0 else [(0, P), (1, 2 * P)]
                            else:
                                blocks = [(0, k * P), (1, D + k * P)]
                            for n, (kb, at) in enumerate(blocks):
                                last = mm(O[:, k, h * VC:h * VC + VC], W[:, u % 2, i, at:at + P], V[:, kb, h, :],
                                          start=causal and n == 0, stop=n == len(blocks) - 1, skip_group_check=True)
                    last.then_inc(av_done, 1)
                    return last

                scores(0)
                pe.wait_ge(o_taken, b + 1)
                if not causal:
                    pe.wait_ge(ow_ready, 2 * b + 2)
                    pe.wait_ge(odd_ready, b * N_ODD + 3)
                    stand()
                    for k in range(2):
                        mm(O[:, k, 0:HEADS * VC], w_ok[:, k * P:k * P + P], V_odd[:, :, :].rearrange("k h e -> k (h e)"),
                           start=True, stop=False, skip_group_check=True)
                for u in range(NP_):
                    if u + 1 < NP_:
                        scores(u + 1)
                    products(u)
                pe.sem_inc(o_ready, 1)

                out = bank("odd_out")
                pe.wait_ge(ow_ready, 2 * b + 2)
                pe.wait_ge(odd_ready, b * N_ODD + 3)
                stand()
                for k in range(2):
                    last = mm(out[:HEADS, 0:HEADS * VC], w_oq[:, k, :], V[:, k, :, :].rearrange("k h e -> k (h e)"),
                              start=k == 0, stop=k == 1)
                last.then_inc(misc_ready, 1)
                out = bank("odd_row")
                wait_taken(pe, b, "odd_out")
                stand()
                mm(out[0:1, 0:HEADS * VC], ones[:, :], oq[:, :, :].rearrange("k h e -> k (h e)"), start=True, stop=False)
                mm(out[0:1, 0:HEADS * VC], w_ok[:, nq - 1:nq], V_odd[:, :, :].rearrange("k h e -> k (h e)"),
                   start=False, stop=True).then_inc(misc_ready, 1)
                for c in range(DC):
                    out = bank(f"aT{c}")
                    pe.wait_ge(a_ready, b + 1)
                    stand()
                    for k in range(2):
                        nc.tensor.transpose(out[:, k * P:k * P + P], a[:, k, c * P:c * P + P], ident[:, :])
                    nc.tensor.transpose(out[:, ODD:T], a_odd[:, c * P:c * P + P], ident[0:1, 0:1]).then_inc(misc_ready, 1)

        @block.scalar
        def _(act):
            A = nc.scalar.activation
            act.wait_ge(const_in, 16 * n_const)
            act.sem_inc(taken_act, 1)
            act.sem_inc(stored, 16)
            if causal:
                act.sem_inc(s_taken, 1)
            act.wait_ge(ones_made, 3)
            with act.Fori(0, B) as b:
                for what, dst, bias in (("q", QT, bq), ("k", KT, bk)):
                    for g in range(HG):
                        src = wait_misc(act, b, f"{what}{g}")
                        A(dst[:, g, :], src[:, 0:T], ACT.Identity, bias=bias[:, g:g + 1]).then_inc(taken_act, 1)
                for k in range(2):
                    src = wait_misc(act, b, f"v{k}")
                    A(V[:, k, :, 0:HD], src[:, 0:D].rearrange("p (h e) -> p h e", e=HD), ACT.Copy).then_inc(taken_act, 1)
                src = wait_misc(act, b, "v_odd")
                A(v_odd[:, :, 0:HD], src[:HEADS, 0:D].rearrange("p (h e) -> p h e", e=HD), ACT.Copy).then_inc(taken_act, 1)
                if causal:
                    src = wait_misc(act, b, "odd_query")
                    A(w_oq[:, :, :].rearrange("p k h -> p (k h)"), src[:, 0:2 * HEADS], ACT.Exp, scale=SCALE)\
                        .then_inc(taken_act, 1)
                    src = wait_misc(act, b, "odd_key")
                    A(w_ok[:, 0:nq], src[:HEADS, 0:nq], ACT.Exp, scale=SCALE).then_inc(taken_act, 1)
                    act.wait_ge(taken_act, b * per_taker["act"] + taken_count(index["odd_key"]) + 1)
                    act.sem_inc(ow_ready, 2)
                    for u in range(NP_):
                        act.wait_ge(s_ready, b * NP_ + u + 1)
                        act.wait_ge(av_done, b * NP_ + max(u, 1))
                        A(W[:, u % 2, :, 0:3 * P], S[:, u % 2, :, 0:3 * P], ACT.Exp, scale=SCALE).then_inc(w_ready, 1)
                        act.wait_ge(w_ready, b * NP_ + u + 1)
                        act.sem_inc(s_taken, 1)
                else:
                    chain = Chain(act, act_chained, NP_ + 2, b)
                    act.wait_ge(ot_ready, 2 * b + 1)
                    A(y_oq[:, :, :], w_oq[:, :, :], ACT.Square).then_inc(oy_ready, 1)
                    act.wait_ge(ot_ready, 2 * b + 1)
                    A(y_ok[:, :], w_ok[:, :], ACT.Square).then_inc(oy_ready, 1)
                    act.wait_ge(ot_ready, 2 * b + 2)
                    A(y_oq[:, :, :], w_oq[:, :, :], ACT.Ln, bias=2.0)
                    chain.link(A(y_ok[:, :], w_ok[:, :], ACT.Ln, bias=2.0))
                    A(w_oq[:, :, :], y_oq[:, :, :], ACT.Exp, scale=-1.0).then_inc(ow_ready, 1)
                    A(w_ok[:, :], y_ok[:, :], ACT.Exp, scale=-1.0).then_inc(ow_ready, 1)

                    def square(u):
                        act.wait_ge(s_taken, b * NP_ + u + 2)
                        A(Yb[:, u % 2, :, :], W[:, u % 2, :, :], ACT.Square).then_inc(y_ready, 1)
                    square(0)
                    for u in range(NP_):
                        if u + 1 < NP_:
                            square(u + 1)
                        act.wait_ge(t_ready, b * NP_ + u + 1)
                        chain.link(A(Yb[:, u % 2, :, :], W[:, u % 2, :, :], ACT.Ln, bias=2.0))
                        A(W[:, u % 2, :, :], Yb[:, u % 2, :, :], ACT.Exp, scale=-1.0).then_inc(w_ready, 1)
                    act.sem_inc(act_chained, 1)
                    chain.count += 1
                    chain.done()
                act.wait_ge(stored, b * 16 + 16)
                for c in range(DC):
                    src = wait_misc(act, b, f"aT{c}")
                    A(aT[:, c, :], src[:, 0:T], ACT.Copy).then_inc(taken_act, 1)

        @block.vector
        def _(dve):
            v = nc.vector
            dve.wait_ge(const_in, 16 * n_const)
            dve.sem_inc(taken_dve, 1)
            dve.sem_inc(max_taken, 1)
            dve.sem_inc(o_taken, 1)
            if not causal:
                dve.sem_inc(s_taken, 1)
            with dve.Fori(0, B) as b:
                chain = Chain(dve, chained, DVE_LINKS[causal], b)
                link = chain.link
                for u in range(NP_):
                    dve.wait_ge(max_s_ready, b * NP_ + u + 1)
                    at = slice(2 * u, 2 * u + 2)
                    if causal:
                        v.tensor_reduce(negmax[:, 0, at], S[:, u % 2, :, 0:P], AX.X, ALU.max, negate=True)
                        v.tensor_reduce(negmax[:, 1, at], S[:, u % 2, :, P:3 * P], AX.X, ALU.max, negate=True)\
                            .then_inc(max_taken, 1)
                    else:
                        v.tensor_reduce(negmax[:, :, at].rearrange("p k h -> p h k"),
                                        S[:, u % 2, :, :].rearrange("p h (k n) -> p h k n", k=2), AX.X, ALU.max,
                                        negate=True).then_inc(max_taken, 1)
                if not causal:
                    src = wait_misc(dve, b, "odd_key_max")
                    dve.wait_ge(max_taken, b * NP_ + NP_ + 1)
                    link(v.scalar_tensor_tensor(negmax[:, :, :].rearrange("p k h -> p (k h)"), src[:, 0:2 * HEADS], -1.0,
                                                negmax[:, :, :].rearrange("p k h -> p (k h)"), ALU.mult, ALU.min))
                    dve.sem_inc(taken_dve, 1)
                else:
                    dve.wait_ge(max_taken, b * NP_ + NP_ + 1)
                dve.sem_inc(max_done, 1)
                src = wait_misc(dve, b, "odd_query_max")
                v.tensor_reduce(negmax_T[:, ODD:T], src[:HEADS, 0:T], AX.X, ALU.max, negate=True).then_inc(taken_dve, 1)
                src = wait_misc(dve, b, "negmax_T")
                v.tensor_copy(negmax_T[:, 0:2 * P], src[:HEADS, 0:2 * P]).then_inc(taken_dve, 1)
                for g in range(HG):
                    src = wait_misc(dve, b, f"aug{g}")
                    v.tensor_tensor(QT[:, g, :], QT[:, g, :], src[:, 0:T], ALU.add).then_inc(taken_dve, 1)
                if not causal:
                    src = wait_misc(dve, b, "odd_query")
                    v.tensor_scalar(w_oq[:, :, :].rearrange("p k h -> p (k h)"), src[:, 0:2 * HEADS], -SCALE, 1.0,
                                    ALU.mult, ALU.add).then_inc(taken_dve, 1)
                    src = wait_misc(dve, b, "odd_key")
                    v.tensor_scalar(w_ok[:, :], src[:HEADS, 0:T], -SCALE, 1.0, ALU.mult, ALU.add).then_inc(taken_dve, 1)
                    wait_taken(dve, b, "odd_key")
                    dve.sem_inc(ot_ready, 1)

                    def shifted(u):
                        dve.wait_ge(s_ready, b * NP_ + u + 1)
                        dve.wait_ge(av_done, b * NP_ + max(u, 1))
                        v.tensor_scalar(W[:, u % 2, :, :], S[:, u % 2, :, :], -SCALE, 1.0, ALU.mult, ALU.add)\
                            .then_inc(s_taken, 1)
                    shifted(0)
                    dve.wait_ge(oy_ready, 2 * b + 2)
                    v.scalar_tensor_tensor(w_oq[:, :, :], y_oq[:, :, :], 3.0, w_oq[:, :, :], ALU.add, ALU.mult)
                    link(v.scalar_tensor_tensor(w_ok[:, :], y_ok[:, :], 3.0, w_ok[:, :], ALU.add, ALU.mult))
                    dve.sem_inc(ot_ready, 1)
                    for u in range(NP_):
                        if u + 1 < NP_:
                            shifted(u + 1)
                        dve.wait_ge(y_ready, b * NP_ + u + 1)
                        v.scalar_tensor_tensor(W[:, u % 2, :, :], Yb[:, u % 2, :, :], 3.0, W[:, u % 2, :, :],
                                               ALU.add, ALU.mult).then_inc(t_ready, 1)
                src = wait_misc(dve, b, "odd_out")
                v.tensor_tensor(oq[:, :, :], src[:HEADS, 0:HEADS * VC].rearrange("k (h e) -> k h e", e=VC), own[:, :, :],
                                ALU.mult).then_inc(taken_dve, 1)
                dve.wait_ge(o_ready, b + 1)
                dve.wait_ge(av_done, b * NP_ + NP_ + 1)
                wait_taken_last = b * per_taker["act"] + 1
                dve.wait_ge(taken_act, wait_taken_last)
                o = O[:, :, 0:HEADS * VC].rearrange("p k (h e) -> p k h e", e=VC)
                link(v.reciprocal(rsum[:, :, :], o[:, :, :, HD]))
                last = None
                for k in range(2):
                    last = v.tensor_tensor(a[:, k, :].rearrange("p (h e) -> p h e", e=HD), o[:, k, :, 0:HD],
                                           rsum[:, k, :].rearrange("p (h e) -> p h e", e=1).broadcast_to([P, HEADS, HD]), ALU.mult)
                link(last)
                dve.sem_inc(o_taken, 1)
                src = wait_misc(dve, b, "odd_row")
                row = src[0:1, 0:HEADS * VC].rearrange("k (h e) -> k h e", e=VC)
                link(v.reciprocal(rsum_odd[:, :], row[:, :, HD]))
                link(v.tensor_tensor(a_odd[:, :].rearrange("k (h e) -> k h e", e=HD), row[:, :, 0:HD],
                                     rsum_odd[:, :].rearrange("k (h e) -> k h e", e=1).broadcast_to([1, HEADS, HD]), ALU.mult))
                dve.sem_inc(taken_dve, 1)
                dve.sem_inc(a_ready, 1)
                chain.done()

        @block.gpsimd
        def _(pool):
            g_ = nc.gpsimd
            g_.memset(ones[:, :], 1.0).then_inc(ones_made, 1)
            g_.memset(V[:, :, :, HD:VC], 1.0).then_inc(ones_made, 1)
            g_.memset(v_odd[:, :, HD:VC], 1.0).then_inc(ones_made, 1)
            pool.wait_ge(const_in, 16 * n_const)
            g_.tensor_copy(ident_b[:, :], ident[:, :]).then_inc(ones_made, 1)
            pool.wait_ge(ones_made, 4)
            with pool.Fori(0, B) as b:
                pool.wait_ge(loaded, b * 16 + 16)
                pool.sem_inc(ones_made, 1)
                g_.tensor_copy(odd_x[:, :, :], xT[:, :, ODD:T].broadcast_to([P, DC, HEADS])).then_inc(x_odd_ready, 1)
                wait_taken(pool, b, "v_odd")
                g_.tensor_tensor(K_odd[:, :, :], KT[:, :, ODD:T].broadcast_to([P, HG, HEADS]), sel[:, :, :], ALU.mult)
                g_.tensor_tensor(Q_odd[:, :, :], QT[:, :, ODD:T].broadcast_to([P, HG, HEADS]), sel[:, :, :],
                                 ALU.mult).then_inc(odd_ready, 1)
                if causal:
                    for k in range(2):
                        g_.tensor_tensor(V[:, k, :, 0:HD], V[:, k, :, 0:HD], bv[:, :, :], ALU.add)
                    g_.tensor_tensor(v_odd[:, :, 0:HD], v_odd[:, :, 0:HD], bv[:HEADS, :, :], ALU.add)\
                        .then_inc(odd_ready, 1)
                else:
                    pool.sem_inc(odd_ready, 1)
                pool.wait_ge(odd_ready, b * N_ODD + 2)
                g_.tensor_tensor(V_odd[:, :, :], v_odd[:, :, :], own[:, :, :], ALU.mult).then_inc(odd_ready, 1)
                wait_taken(pool, b, "aug3")
                g_.tensor_tensor(Q_odd[:, :, :], QT[:, :, ODD:T].broadcast_to([P, HG, HEADS]), sel[:, :, :],
                                 ALU.mult).then_inc(odd_ready, 1)


def enter_attention(nc, cT_in, h_in, wout_in, gamma_in, beta_in, ident_in, hx_out, x_out, xT_out):
    ctx = ExitStack()
    with ctx:
        r = Room(nc, ctx, "mid")
        ident, wout = r.sb("ident", [P, P]), r.sb("wout", [P, DC, D])
        gamma, beta = r.sb("gamma", [P, DC]), r.sb("beta", [P, DC])
        cT, h = r.sb("cT", [P, DC, GROUP]), r.sb("h", [P, 4, D])
        h1, x, hx, xn = (r.sb(n, [P, 4, D]) for n in ("h1", "x", "hx", "xn"))
        xt = r.sb("xt", [P, DC, GROUP])
        stats, mv = r.sb("stats", [P, 4, 6]), r.sb("mv", [P, 4, 2])
        ve, rstd, minus_half = r.sb("ve", [P, 4]), r.sb("rstd", [P, 4]), r.sb("mh", [P, 4])
        out_ps = r.ps("out", [P, 4, D])
        tp = r.ps("tp", [P, DC, GROUP])
        const_in, loaded, inputs_free = r.sem("const_in"), r.sem("loaded"), r.sem("inputs_free")
        const_made, chained, var_ready, rstd_ready = r.sem("const_made"), r.sem("chained"), r.sem("var"), r.sem("rstds")
        out_ready, out_taken = r.sem("out_ready"), r.sem("out_taken")
        xn_ready, tp_ready, xt_ready = r.sem("xn_ready"), r.sem("tp_ready"), r.sem("xt_ready")
        rows_ready, rows_stored, stored = r.sem("rows_ready"), r.sem("rows_stored"), r.sem("stored")
        block = ctx.enter_context(nc.Block())

        @block.sync
        def _(sp):
            sp.dma_start(ident[:, :], ident_in).then_inc(const_in, 16)
            sp.dma_start(wout[:, :, :], wout_in.rearrange("(c p) n -> p c n", p=P)).then_inc(const_in, 16)
            sp.dma_start(gamma[:, :], gamma_in).then_inc(const_in, 16)
            sp.dma_start(beta[:, :], beta_in).then_inc(const_in, 16)

            def step(t0, g, tiles, rows):
                sp.wait_ge(inputs_free, g + 1)
                sp.wait_ge(out_ready, g + 1)
                sp.dma_start(cT[:, :, 0:tiles * rows], cT_in[:, bass.ds(t0, tiles * rows)]
                             .rearrange("(c p) t -> p c t", p=P)).then_inc(loaded, 16)
                sp.dma_start(h[:rows, 0:tiles, :], tokens(h_in, t0, tiles, rows)).then_inc(loaded, 16)
            groups(sp, step)

        @block.tensor
        def _(pe):
            pe.sem_inc(tp_ready, 1)
            pe.sem_inc(out_ready, 1)
            pe.wait_ge(const_in, 64)

            def step(t0, g, tiles, rows):
                pe.wait_ge(loaded, g * 32 + 32)
                pe.wait_ge(out_taken, g + 1)
                for j in range(tiles):
                    for c in range(DC):
                        last = nc.tensor.matmul(out_ps[:rows, j, :], cT[:, c, j * P:j * P + rows], wout[:, c, :],
                                                start=c == 0, stop=c == DC - 1)
                last.then_inc(out_ready, 1)
                pe.wait_ge(xt_ready, g + 1)
                pe.wait_ge(xn_ready, g + 1)
                transposed(nc, tp, xn, ident, tiles, rows).then_inc(tp_ready, 1)
            groups(pe, step)

        @block.vector
        def _(dve):
            v = nc.vector
            dve.sem_inc(inputs_free, 1)
            dve.sem_inc(out_taken, 1)

            def step(t0, g, tiles, rows):
                chain = Chain(dve, chained, 8, g)
                dve.wait_ge(out_ready, g + 2)
                dve.wait_ge(rows_stored, g * 32 + 32)
                v.tensor_tensor(h1[:rows, 0:tiles, :], h[:rows, 0:tiles, :], out_ps[:rows, 0:tiles, :], ALU.add)\
                    .then_inc(out_taken, 1)
                dve.wait_ge(out_taken, g + 2)
                dve.sem_inc(inputs_free, 1)
                statistics(v, chain, h1, stats, mv, ve, tiles, rows, LN_EPS).then_inc(var_ready, 1)
                dve.wait_ge(rstd_ready, 2 * g + 1)
                dve.wait_ge(var_ready, 2 * g + 1)
                chain.link_apart(normalise(v, h1, x, mv, rstd, tiles, rows))
                statistics(v, chain, x, stats, mv, ve, tiles, rows, LN_EPS).then_inc(var_ready, 1)
                v.tensor_tensor(hx[:rows, 0:tiles, :], h1[:rows, 0:tiles, :], x[:rows, 0:tiles, :], ALU.add)\
                    .then_inc(rows_ready, 1)
                dve.wait_ge(rstd_ready, 2 * g + 2)
                dve.wait_ge(var_ready, 2 * g + 2)
                dve.wait_ge(tp_ready, g + 1)
                normalise(v, x, xn, mv, rstd, tiles, rows).then_inc(xn_ready, 1)
                chain.done()
            groups(dve, step)

        @block.gpsimd
        def _(pool):
            nc.gpsimd.memset(minus_half[:, :], -0.5).then_inc(const_made, 1)
            pool.wait_ge(const_made, 1)

            def step(t0, g, tiles, rows):
                for n in range(2):
                    pool.wait_ge(var_ready, 2 * g + n + 1)
                    nc.gpsimd.tensor_tensor(rstd[:rows, 0:tiles], ve[:rows, 0:tiles], minus_half[:rows, 0:tiles],
                                            ALU.pow).then_inc(rstd_ready, 1)
            groups(pool, step)

        @block.scalar
        def _(act):
            act.sem_inc(xt_ready, 1)
            act.sem_inc(stored, 16)
            act.sem_inc(rows_stored, 32)
            act.wait_ge(const_in, 64)

            def step(t0, g, tiles, rows):
                act.wait_ge(stored, g * 16 + 16)
                act.wait_ge(tp_ready, g + 2)
                n = tiles * rows
                for c in range(DC):
                    last = nc.scalar.activation(xt[:, c, 0:n], tp[:, c, 0:n], ACT.Identity, bias=beta[:, c:c + 1],
                                                scale=gamma[:, c:c + 1])
                last.then_inc(xt_ready, 1)
                act.wait_ge(xt_ready, g + 2)
                act.dma_start(xT_out[:, bass.ds(t0, n)].rearrange("(c p) t -> p c t", p=P),
                              xt[:, :, 0:n]).then_inc(stored, 16)
                act.wait_ge(rows_ready, g + 1)
                act.dma_start(tokens(hx_out, t0, tiles, rows), hx[:rows, 0:tiles, :]).then_inc(rows_stored, 16)
                act.dma_start(tokens(x_out, t0, tiles, rows), x[:rows, 0:tiles, :]).then_inc(rows_stored, 16)
            groups(act, step)
            act.wait_ge(rows_stored, 32 * (NGROUPS + 2))
            act.wait_ge(stored, 16 * (NGROUPS + 2))


EXPERTS, HIDDEN = 8, 4 * D
MOE_LINKS = 20
HB = HIDDEN // P


def experts(nc, aT_in, x_in, hx_in, wp_in, bp_in, gamma_in, beta_in, gate_w_in, gate_b_in, w1_in, b1_in, w2_in, b2_in,
            ident_in, h_out, xT_out):
    ctx = ExitStack()
    with ctx:
        r = Room(nc, ctx, "moe")
        ident, wp, bp = r.sb("ident", [P, P]), r.sb("wp", [P, DC, D]), r.sb("bp", [P, D])
        gamma, beta = r.sb("gamma", [P, DC]), r.sb("beta", [P, DC])
        gate_w, gate_b = r.sb("gate_w", [P, DC, EXPERTS]), r.sb("gate_b", [P, EXPERTS])
        w1, w2 = r.sb("w1", [P, EXPERTS, DC, HIDDEN]), r.sb("w2", [P, EXPERTS, HB, D])
        b1, b2 = r.sb("b1", [P, EXPERTS, HB]), r.sb("b2", [EXPERTS, D])
        aT = r.sb("aT", [P, DC, GROUP])
        x, acc = r.sb("x", [P, 4, D]), r.sb("acc", [P, 4, D])
        xn = r.sb("xn", [P, 4, D])
        mT = r.sb("mT", [P, DC, GROUP])
        mid = r.sb("mid", [P, 2, HB, GROUP])
        xt = aT
        stats, mv = r.sb("stats", [P, 4, 6]), r.sb("mv", [P, 4, 2])
        ve, rstd, minus_half = r.sb("ve", [P, 4]), r.sb("rstd", [P, 4]), r.sb("mh", [P, 4])
        logits, top, index = r.sb("logits", [P, 4, EXPERTS]), r.sb("top", [P, 4, 8]), r.sb("index", [P, 4, 8], U32)
        index_f, iota = r.sb("index_f", [P, 4, 8]), r.sb("iota", [P, EXPERTS])
        gap, second, total = r.sb("gap", [P, 4]), r.sb("second", [P, 4]), r.sb("total", [P, 4])
        wa, wb, one_hot, w_full = r.sb("wa", [P, 4]), r.sb("wb", [P, 4]), r.sb("one_hot", [P, 4, EXPERTS]), r.sb("w_full", [P, 4, EXPERTS])
        wT = r.sb("wT", [EXPERTS, GROUP])
        hid = r.ps("hid", [P, 2, GROUP])
        y = r.ps("y", [P, 2, 2, 2, D])
        tp = r.ps("tp", [P, DC, GROUP])
        const_in, const_made, loaded, loaded_hx = r.sem("const_in"), r.sem("const_made"), r.sem("loaded"), r.sem("loaded_hx")
        x_free, acc_free, proj_ready, proj_taken = r.sem("x_free"), r.sem("acc_free"), r.sem("proj_ready"), r.sem("proj_taken")
        chained, var_ready, rstd_ready, xn_ready = r.sem("chained"), r.sem("var"), r.sem("rstds"), r.sem("xn")
        tp_ready, tp_taken, gate_ready, gap_ready, exp_ready = (r.sem(n) for n in ("tp_ready", "tp_taken", "gate", "gap", "exp"))
        w_ready, wT_ready, wT_taken = r.sem("w_ready"), r.sem("wT_ready"), r.sem("wT_taken")
        hid_ready, mid_ready, y_ready, y_taken = r.sem("hid_ready"), r.sem("mid_ready"), r.sem("y_ready"), r.sem("y_taken")
        h_stored, stored, passed = r.sem("h_stored"), r.sem("stored"), r.sem("passed")
        h_ready, sp_passed = r.sem("h_ready"), r.sem("sp_passed")
        YU = 2 * (EXPERTS + 1)
        block = ctx.enter_context(nc.Block())

        @block.sync
        def _(sp):
            for dst, src in ((wp, wp_in), (gate_w, gate_w_in)):
                sp.dma_start(dst[:, :, :], src.rearrange("(c p) n -> p c n", p=P)).then_inc(const_in, 16)
            for dst, src in ((ident, ident_in), (gamma, gamma_in), (beta, beta_in), (b2, b2_in)):
                sp.dma_start(dst[:, :], src).then_inc(const_in, 16)
            sp.dma_start(bp[:, :], bp_in.broadcast_to([P, D])).then_inc(const_in, 16)
            sp.dma_start(gate_b[:, :], gate_b_in.broadcast_to([P, EXPERTS])).then_inc(const_in, 16)
            sp.dma_start(b1[:, :, :], b1_in).then_inc(const_in, 16)
            for e in range(EXPERTS):
                sp.dma_start(w1[:, e, :, :], w1_in[:, e, :, :]).then_inc(const_in, 16)
                sp.dma_start(w2[:, e, :, :], w2_in[:, e, :, :]).then_inc(const_in, 16)

            def step(t0, g, tiles, rows):
                n = tiles * rows
                sp.wait_ge(stored, g * 16 + 16)
                sp.sem_inc(sp_passed, 1)
                sp.wait_ge(x_free, g + 1)
                sp.sem_inc(sp_passed, 1)
                sp.dma_start(aT[:, :, 0:n], aT_in[:, bass.ds(t0, n)].rearrange("(c p) t -> p c t", p=P)).then_inc(loaded, 16)
                sp.dma_start(x[:rows, 0:tiles, :], tokens(x_in, t0, tiles, rows)).then_inc(loaded, 16)
                sp.wait_ge(h_stored, g * 16 + 16)
                sp.sem_inc(sp_passed, 1)
                sp.dma_start(acc[:rows, 0:tiles, :], tokens(hx_in, t0, tiles, rows)).then_inc(loaded_hx, 16)
            groups(sp, step)

        @block.tensor
        def _(pe):
            mm = nc.tensor.matmul
            pe.sem_inc(y_ready, 2)
            pe.wait_ge(const_in, 16 * (9 + 2 * EXPERTS))

            def step(t0, g, tiles, rows):
                n = tiles * rows
                pairs = (tiles + 1) // 2

                def stand():
                    pe.sem_inc(passed, 1)

                pe.wait_ge(loaded, g * 32 + 32)
                pe.wait_ge(tp_taken, 3 * g + 1)
                for j in range(tiles):
                    for c in range(DC):
                        last = mm(tp[:rows, j // 2, (j % 2) * D:(j % 2) * D + D], aT[:, c, j * P:j * P + rows], wp[:, c, :],
                                  start=c == 0, stop=c == DC - 1)
                last.then_inc(proj_ready, 1)
                pe.wait_ge(proj_taken, g + 1)
                pe.wait_ge(xn_ready, 2 * g + 1)
                transposed(nc, tp, xn, ident, tiles, rows).then_inc(tp_ready, 1)
                pe.wait_ge(tp_taken, 3 * g + 2)
                stand()
                for j in range(tiles):
                    for c in range(DC):
                        last = mm(tp[:rows, 0, j * EXPERTS:(j + 1) * EXPERTS], mT[:, c, j * P:j * P + rows],
                                  gate_w[:, c, :], start=c == 0, stop=c == DC - 1)
                last.then_inc(gate_ready, 1)

                def hidden(e, hb):
                    u = e * HB + hb
                    pe.wait_ge(mid_ready, g * EXPERTS * HB + u + 1)
                    for c in range(DC):
                        last = mm(hid[:, u % 2, 0:n], w1[:, e, c, hb * P:hb * P + P], mT[:, c, 0:n], start=c == 0,
                                  stop=c == DC - 1)
                    last.then_inc(hid_ready, 1)

                def out(e):
                    pe.wait_ge(mid_ready, g * EXPERTS * HB + (e + 1) * HB + 2)
                    for k in range(pairs):
                        pe.wait_ge(y_taken, g * YU + 4 + max(0, pairs * (e - 1) + k + 1))
                        for j in range(2 * k, min(2 * k + 2, tiles)):
                            for hb in range(HB):
                                last = mm(y[:rows, (e + 1) % 2, k, j % 2, :], mid[:, e % 2, hb, j * P:j * P + rows],
                                          w2[:, e, hb, :], start=hb == 0, stop=hb == HB - 1)
                        last.then_inc(y_ready, 1)

                for hb in range(HB):
                    hidden(0, hb)
                pe.wait_ge(w_ready, g + 1)
                stand()
                for j in range(tiles):
                    last = nc.tensor.transpose(tp[:EXPERTS, 1, j * P:j * P + rows], w_full[:rows, j, :], ident[:rows, :rows])
                last.then_inc(wT_ready, 1)
                pe.wait_ge(wT_taken, g + 1)
                pe.wait_ge(y_taken, g * YU + 4)
                for k in range(pairs):
                    stand()
                    for j in range(2 * k, min(2 * k + 2, tiles)):
                        last = mm(y[:rows, 0, k, j % 2, :], wT[:, j * P:j * P + rows], b2[:, :], start=True, stop=True)
                    last.then_inc(y_ready, 1)
                for e in range(EXPERTS):
                    if e + 1 < EXPERTS:
                        for hb in range(HB):
                            hidden(e + 1, hb)
                    out(e)
                pe.wait_ge(xn_ready, 2 * g + 2)
                transposed(nc, tp, xn, ident, tiles, rows).then_inc(tp_ready, 1)
            groups(pe, step)

        @block.scalar
        def _(act):
            A = nc.scalar.activation
            act.sem_inc(tp_taken, 1)
            act.sem_inc(mid_ready, 2)
            act.sem_inc(stored, 16)
            act.wait_ge(const_in, 16 * (9 + 2 * EXPERTS))

            def step(t0, g, tiles, rows):
                n = tiles * rows
                pairs = (tiles + 1) // 2
                act.wait_ge(tp_ready, 2 * g + 1)
                for c in range(DC):
                    last = A(mT[:, c, 0:n], tp[:, c, 0:n], ACT.Identity, bias=beta[:, c:c + 1], scale=gamma[:, c:c + 1])
                last.then_inc(tp_taken, 1)
                act.wait_ge(gap_ready, g + 1)
                A(second[:rows, 0:tiles], gap[:rows, 0:tiles], ACT.Exp).then_inc(exp_ready, 1)
                for e in range(EXPERTS):
                    act.wait_ge(y_ready, g * YU + 2 + (pairs * e if e >= 2 else 0))
                    for hb in range(HB):
                        u = e * HB + hb
                        act.wait_ge(hid_ready, g * EXPERTS * HB + u + 1)
                        A(mid[:, e % 2, hb, 0:n], hid[:, u % 2, 0:n], ACT.Gelu, bias=b1[:, e, hb:hb + 1])\
                            .then_inc(mid_ready, 1)
                    if e == 0:
                        act.wait_ge(wT_ready, g + 1)
                        A(wT[:, 0:n], tp[:EXPERTS, 1, 0:n], ACT.Copy).then_inc(wT_taken, 1)
                act.wait_ge(tp_ready, 2 * g + 2)
                A(xt[:, :, 0:n], tp[:, :, 0:n], ACT.Copy).then_inc(tp_taken, 1)
                act.sem_inc(tp_taken, 1)
                act.wait_ge(tp_taken, 3 * g + 4)
                act.dma_start(xT_out[:, bass.ds(t0, n)].rearrange("(c p) t -> p c t", p=P),
                              xt[:, :, 0:n]).then_inc(stored, 16)
                act.wait_ge(h_ready, g + 1)
                act.dma_start(tokens(h_out, t0, tiles, rows), acc[:rows, 0:tiles, :]).then_inc(h_stored, 16)
            groups(act, step)
            act.wait_ge(stored, 16 * (NGROUPS + 2))
            act.wait_ge(h_stored, 16 * (NGROUPS + 2))

        @block.vector
        def _(dve):
            v = nc.vector
            dve.sem_inc(x_free, 1)
            dve.sem_inc(y_taken, 4)
            dve.wait_ge(const_made, 3)
            dve.wait_ge(const_in, 16 * (9 + 2 * EXPERTS))

            def step(t0, g, tiles, rows):
                chain = Chain(dve, chained, MOE_LINKS, g)
                link = chain.link
                t_ = slice(0, tiles)
                pairs = (tiles + 1) // 2
                dve.wait_ge(loaded_hx, g * 16 + 16)
                dve.wait_ge(proj_ready, g + 1)
                proj = tp[:rows, :, :].rearrange("p c (k d) -> p (c k) d", k=2)[:, t_, :]
                bias = bp[:rows, :].rearrange("p (a d) -> p a d", a=1).broadcast_to([rows, tiles, D])
                link(v.tensor_tensor(xn[:rows, t_, :], proj, bias, ALU.add))
                dve.sem_inc(proj_taken, 1)
                v.tensor_tensor(acc[:rows, t_, :], acc[:rows, t_, :], xn[:rows, t_, :], ALU.add)
                chain.link_apart(v.tensor_tensor(x[:rows, t_, :], x[:rows, t_, :], xn[:rows, t_, :], ALU.add))
                statistics(v, chain, x, stats, mv, ve, tiles, rows, LN_EPS).then_inc(var_ready, 1)
                dve.wait_ge(rstd_ready, 2 * g + 1)
                normalise(v, x, xn, mv, rstd, tiles, rows).then_inc(xn_ready, 1)
                dve.wait_ge(xn_ready, 2 * g + 1)
                dve.sem_inc(x_free, 1)
                dve.wait_ge(gate_ready, g + 1)
                bias = gate_b[:rows, :].rearrange("p (a d) -> p a d", a=1).broadcast_to([rows, tiles, EXPERTS])
                chain.link_apart(v.tensor_tensor(logits[:rows, t_, :], tp[:rows, 0, 0:tiles * EXPERTS]
                                                 .rearrange("p (j e) -> p j e", e=EXPERTS), bias, ALU.add))
                for j in range(tiles):
                    last = v.max(top[:rows, j, :], logits[:rows, j, :])
                chain.link_apart(last)
                for j in range(tiles):
                    last = v.max_index(index[:rows, j, :], top[:rows, j, :], logits[:rows, j, :])
                v.tensor_tensor(gap[:rows, t_], top[:rows, t_, 1], top[:rows, t_, 0], ALU.subtract).then_inc(gap_ready, 1)
                link(last)
                link(v.tensor_copy(index_f[:rows, t_, :], index[:rows, t_, :]))
                dve.wait_ge(exp_ready, g + 1)
                link(v.tensor_scalar(total[:rows, t_], second[:rows, t_], 1.0, None, ALU.add))
                link(v.reciprocal(wa[:rows, t_], total[:rows, t_]))
                link(v.tensor_tensor(wb[:rows, t_], wa[:rows, t_], second[:rows, t_], ALU.mult))
                for j in range(tiles):
                    last = v.tensor_scalar(one_hot[:rows, j, :], iota[:rows, :], index_f[:rows, j, 1:2], wb[:rows, j:j + 1],
                                           ALU.is_equal, ALU.mult)
                    v.tensor_scalar(w_full[:rows, j, :], iota[:rows, :], index_f[:rows, j, 0:1], wa[:rows, j:j + 1],
                                    ALU.is_equal, ALU.mult)
                link(v.tensor_copy(total[:rows, t_], wb[:rows, t_]))
                link(v.tensor_tensor(w_full[:rows, t_, :], w_full[:rows, t_, :], one_hot[:rows, t_, :], ALU.add))
                dve.sem_inc(w_ready, 1)
                for e in range(-1, EXPERTS):
                    for k in range(pairs):
                        dve.wait_ge(y_ready, g * YU + 2 + pairs * (e + 1) + k + 1)
                        for j in range(2 * k, min(2 * k + 2, tiles)):
                            src = y[:rows, (e + 1) % 2, k, j % 2, :]
                            if e < 0:
                                last = v.tensor_tensor(acc[:rows, j, :], acc[:rows, j, :], src, ALU.add)
                            else:
                                last = v.scalar_tensor_tensor(acc[:rows, j, :], src, w_full[:rows, j, e:e + 1],
                                                              acc[:rows, j, :], ALU.mult, ALU.add)
                        last.then_inc(y_taken, 1)
                        dve.wait_ge(y_taken, g * YU + 4 + pairs * (e + 1) + k + 1)
                dve.sem_inc(h_ready, 1)
                statistics(v, chain, acc, stats, mv, ve, tiles, rows, LN_EPS).then_inc(var_ready, 1)
                dve.wait_ge(rstd_ready, 2 * g + 2)
                normalise(v, acc, xn, mv, rstd, tiles, rows).then_inc(xn_ready, 1)
                chain.done()
            groups(dve, step)

        @block.gpsimd
        def _(pool):
            nc.gpsimd.memset(minus_half[:, :], -0.5).then_inc(const_made, 1)
            nc.gpsimd.iota(iota[:, :], [[1, EXPERTS]], base=0, channel_multiplier=0, allow_small_or_imprecise_dtypes=True)\
                .then_inc(const_made, 1)
            pool.wait_ge(const_made, 2)
            pool.sem_inc(const_made, 1)
            pool.sem_inc(h_stored, 16)

            def step(t0, g, tiles, rows):
                for n in range(2):
                    pool.wait_ge(var_ready, 2 * g + n + 1)
                    nc.gpsimd.tensor_tensor(rstd[:rows, 0:tiles], ve[:rows, 0:tiles], minus_half[:rows, 0:tiles],
                                            ALU.pow).then_inc(rstd_ready, 1)
            groups(pool, step)

PH, PK = 8, 8
NKEYS = 64
JB = NKEYS // 2
SUB = 16
EG = 2 * P
EGROUPS = NTOK // EG
LAG = 2
ROUTE_LINKS = 69
PE_AT = {"proj": 0, "tp": 4, "sims": (5, 15), "fields": (13, 26), "scatter": (16, 28)}
DVE_AT = {"h": 1, "x": 2, "xn": 3, "pick": (6, 19), "one_hot": (15, 27)}


def product_keys(nc, aT_in, h_in, wout_in, bout_in, norm_w_in, w_q_in, keys_in, down_in, up_in, ident_in, h_out):
    ctx = ExitStack()
    with ctx:
        r = Room(nc, ctx, "peer")
        ident, wout, bout = r.sb("ident", [P, P]), r.sb("wout", [P, DC, D]), r.sb("bout", [P, D])
        norm_w = r.sb("norm_w", [P, DC])
        down, up = r.sb("down", [P, DC, JB, P]), r.sb("up", [P, JB, D])
        simw = r.sb("simw", [P, DC, 2 * PH * NKEYS])
        G = r.sb("G", [P, 2, JB, EG])
        G_flat = G[:, :, :, :].rearrange("p g a b -> p (g a b)")
        w_q = G_flat[:, 0:16 * D].rearrange("p (a b) -> p a b", a=16)
        keys = G_flat[:, 16 * D:16 * D + 16 * NKEYS].rearrange("p (a b) -> p a b", a=16)
        aT, xnT = r.sb("aT", [P, DC, EG]), r.sb("xnT", [P, 2, DC, EG])
        h, x = r.sb("h", [P, 2, 2, D]), r.sb("x", [P, 2, D])
        stats, mv = r.sb("stats", [P, 2, 6]), r.sb("mv", [P, 2, 2])
        ve, rstd, minus_half, m2 = (r.sb(n, [P, 2]) for n in ("ve", "rstd", "mh", "m2"))
        best, best_i = r.sb("best", [P, 2 * PH, 8]), r.sb("best_i", [P, 2 * PH, 8], U32)
        best_if = r.sb("best_if", [P, 2 * PH, 8])
        sums = r.sb("sums", [P, PH, 8, 8])
        fs, pk = r.sb("fs", [P, PH, PK]), r.sb("pk", [P, PH * PK], U32)
        pk_u, pk_f = r.sb("pk_u", [P, 2, PH * PK], U32), r.sb("pk_f", [P, 2, PH * PK])
        picked = r.sb("picked", [P, PH, PK, 8])
        j_f, j_u, j_parts, par = r.sb("j_f", [P, 64]), r.sb("j_u", [P, 64], U32), r.sb("j_parts", [P, 2, 64], U32), r.sb("par", [P, 64])
        fields = r.sb("fields", [P, 4, 64])
        FT = r.sb("FT", [P, 4, 64])
        iota = r.sb("iota", [P, NKEYS])
        eq = r.sb("eq", [P, SUB, NKEYS])
        one_i, one_j = r.sb("one_i", [P, 2, SUB, 2, NKEYS]), r.sb("one_j", [P, 2, SUB, JB])
        hid = r.sb("hid", [P, 4, EG])
        route = r.ps("route", [P, 2, 512])
        work = r.ps("work", [P, 2, 512])
        total = r.ps("total", [P, 2, D])
        scat = r.ps("scat", [P, 2, SUB, JB])
        const_in, const_made, loaded, a_free, h_stored = (r.sem(n) for n in ("const_in", "const_made", "loaded", "a_free", "h_stored"))
        simw_ready, simw_taken = r.sem("simw_ready"), r.sem("simw_taken")
        proj_ready, proj_taken, chained, var_ready, rstd_ready = (r.sem(n) for n in ("proj", "proj_taken", "chained", "var", "rstds"))
        xn_ready, tp_ready, tp_taken = r.sem("xn"), r.sem("tp"), r.sem("tp_taken")
        sims_ready, sims_taken, fields_ready, f_ready, f_taken = (r.sem(n) for n in ("sims", "sims_taken", "fields_r", "f", "f_taken"))
        one_ready, scat_ready, scat_taken = r.sem("one"), r.sem("scat_r"), r.sem("scat_taken")
        hid_ready, gelu_ready, gated, up_done = r.sem("hid_r"), r.sem("gelu"), r.sem("gated"), r.sem("up_done")
        out_taken, passed, sp_passed = r.sem("out_taken"), r.sem("passed"), r.sem("sp_passed")
        dve_passed = r.sem("dve_passed")
        N_CONST = 9
        block = ctx.enter_context(nc.Block())

        def shape_of(is_tail):
            return (1, TAIL, 1, TAIL) if is_tail else (2, P, 2, P // 2)

        def turns(engine, turn):
            turn(-1, None, "full", 1)
            with engine.Fori(0, EGROUPS - 2, 2) as g:
                turn(g, "full", "full", 0)
                turn(g + 1, "full", "full", 1)
            turn(EGROUPS - 2, "full", "full", 0)
            turn(EGROUPS - 1, "full", "tail", 1)
            turn(EGROUPS, "tail", None, 0)

        @block.sync
        def _(sp):
            sp.dma_start(w_q, w_q_in).then_inc(const_in, 16)
            sp.dma_start(keys, keys_in).then_inc(const_in, 16)
            sp.dma_start(wout[:, :, :], wout_in.rearrange("(c p) n -> p c n", p=P)).then_inc(const_in, 16)
            sp.dma_start(ident[:, :], ident_in).then_inc(const_in, 16)
            sp.dma_start(bout[:, :], bout_in.broadcast_to([P, D])).then_inc(const_in, 16)
            sp.dma_start(norm_w[:, :], norm_w_in).then_inc(const_in, 16)
            for c in range(DC):
                sp.dma_start(down[:, c, :, :], down_in[:, c, :, :]).then_inc(const_in, 16)
            sp.dma_start(up[:, :, :], up_in).then_inc(const_in, 16)

            def turn(g, blocks, routing, q):
                if routing is None:
                    return
                tiles, rows, _, _ = shape_of(routing == "tail")
                ga, n = g + 1, tiles * rows
                sp.wait_ge(a_free, ga + 1)
                sp.sem_inc(sp_passed, 1)
                sp.wait_ge(h_stored, ga * 16 + 16)
                sp.sem_inc(sp_passed, 1)
                sp.dma_start(aT[:, :, 0:n], aT_in[:, bass.ds(ga * EG, n)].rearrange("(c p) t -> p c t", p=P))\
                  .then_inc(loaded, 16)
                sp.dma_start(h[:rows, 1 - q, 0:tiles, :], tokens(h_in, ga * EG, tiles, rows)).then_inc(loaded, 16)
            turns(sp, turn)

        @block.tensor
        def _(pe):
            mm = nc.tensor.matmul
            pe.sem_inc(a_free, 1)
            pe.sem_inc(scat_ready, 2)
            pe.sem_inc(up_done, 4)
            pe.wait_ge(const_in, 16 * N_CONST)
            for c in range(DC):
                for half in range(2):
                    for n in range(PH):
                        s = half * PH + n
                        last = mm(route[:, half, n * NKEYS:(n + 1) * NKEYS], w_q[:, s, c * P:c * P + P], keys[:, s, :],
                                  start=True, stop=True)
                last.then_inc(simw_ready, 1)
                pe.wait_ge(simw_taken, c + 1)

            def stand():
                pe.sem_inc(passed, 1)

            def turn(g, blocks, routing, q):
                tiles, rows, halves, tt = shape_of(routing == "tail")
                b_tiles, b_rows, _, _ = shape_of(blocks == "tail")
                nb = b_tiles * b_rows
                ga, b = g + 1, 1 - q
                for jj in range(JB + LAG):
                    if blocks and jj < JB:
                        pe.wait_ge(gelu_ready, g * JB + jj + 1)
                        if jj == 0:
                            pe.wait_ge(tp_taken, g + 1)
                            stand()
                        for c in range(DC):
                            last = mm(work[:, jj % 2, 0:nb], down[:, c, jj, :], xnT[:, q, c, 0:nb], start=c == 0,
                                      stop=c == DC - 1)
                        last.then_inc(hid_ready, 1)
                    if routing and jj == PE_AT["proj"]:
                        pe.wait_ge(loaded, ga * 32 + 32)
                        pe.wait_ge(f_taken, ga * 2 + 1)
                        stand()
                        for j in range(tiles):
                            for c in range(DC):
                                last = mm(route[:rows, 0, j * D:j * D + D], aT[:, c, j * P:j * P + rows],
                                          wout[:, c, :], start=c == 0, stop=c == DC - 1)
                        last.then_inc(proj_ready, 1)
                        pe.wait_ge(proj_ready, ga + 1)
                        pe.sem_inc(a_free, 1)
                    if routing and jj == PE_AT["tp"]:
                        pe.wait_ge(proj_taken, ga + 1)
                        pe.wait_ge(xn_ready, ga + 1)
                        for c in range(DC):
                            for j in range(tiles):
                                last = nc.tensor.transpose(route[:, 0, c * EG + j * P:c * EG + j * P + rows],
                                                           x[:rows, j, c * P:c * P + P], ident[:rows, :rows])
                        last.then_inc(tp_ready, 1)
                        pe.wait_ge(tp_taken, ga + 1)
                    for j in range(tiles if routing else 0):
                        t = ga * 2 + j
                        if jj == PE_AT["sims"][j]:
                            pe.wait_ge(sims_taken, t + 1)
                            pe.wait_ge(f_taken, t + 1)
                            for half in range(2):
                                for c in range(DC):
                                    last = mm(route[:rows, half, :], xnT[:, b, c, j * P:j * P + rows],
                                              simw[:, c, half * 512:half * 512 + 512], start=c == 0, stop=c == DC - 1)
                            last.then_inc(sims_ready, 1)
                        if jj == PE_AT["fields"][j]:
                            pe.wait_ge(fields_ready, t + 1)
                            stand()
                            for half in range(halves):
                                part = slice(64 * half, 64 * half + tt)
                                for f in range(4):
                                    last = mm(route[64 * half:64 * half + 64, 0, f * 64:f * 64 + tt], fields[part, f, :],
                                              ident[part, part], start=True, stop=True)
                            last.then_inc(f_ready, 1)
                        s = jj - PE_AT["scatter"][j]
                        if 0 <= s < tt // SUB:
                            u = t * 4 + s
                            pe.wait_ge(one_ready, u + 1)
                            pe.wait_ge(scat_taken, u + 1)
                            stand()
                            for half in range(halves):
                                part = slice(64 * half, 64 * half + 64)
                                for k in range(SUB):
                                    last = mm(scat[:, half, k, :], one_i[part, s % 2, k, :, :].rearrange("p a i -> p (a i)"),
                                              one_j[part, s % 2, k, :], start=True, stop=True)
                            last.then_inc(scat_ready, 1)
                    if blocks and jj >= LAG:
                        e = jj - LAG
                        pe.wait_ge(gated, g * JB + e + 1)
                        if e == 0:
                            pe.wait_ge(out_taken, g + 1)
                            stand()
                        for j in range(b_tiles):
                            last = mm(total[:b_rows, j, :], hid[:, e % 4, j * P:j * P + b_rows], up[:, e, :],
                                      start=e == 0 and j == 0, stop=e == JB - 1, skip_group_check=True)
                        last.then_inc(up_done, 1)
            turns(pe, turn)

        @block.scalar
        def _(act):
            A = nc.scalar.activation
            act.sem_inc(gelu_ready, 2)
            act.sem_inc(f_taken, 1)
            act.sem_inc(scat_taken, 1)
            act.sem_inc(h_stored, 32)
            act.wait_ge(const_in, 16 * N_CONST)
            for c in range(DC):
                act.wait_ge(simw_ready, c + 1)
                A(simw[:, c, :].rearrange("p (a b) -> p a b", a=2), route[:, :, :], ACT.Copy).then_inc(simw_taken, 1)

            def turn(g, blocks, routing, q):
                tiles, rows, halves, tt = shape_of(routing == "tail")
                b_tiles, b_rows, _, _ = shape_of(blocks == "tail")
                nb, n = b_tiles * b_rows, tiles * rows
                ga, b = g + 1, 1 - q
                for jj in range(JB):
                    if blocks:
                        act.wait_ge(hid_ready, g * JB + jj + 1)
                        act.wait_ge(up_done, g * JB + jj + 1)
                        A(hid[:, jj % 4, 0:nb], work[:, jj % 2, 0:nb], ACT.Gelu).then_inc(gelu_ready, 1)
                    if routing and jj == PE_AT["tp"]:
                        act.wait_ge(tp_ready, ga + 1)
                        for c in range(DC):
                            last = A(xnT[:, b, c, 0:n], route[:, 0, c * EG:c * EG + n], ACT.Copy, scale=norm_w[:, c:c + 1])
                        last.then_inc(tp_taken, 1)
                    for j in range(tiles if routing else 0):
                        t = ga * 2 + j
                        if jj == PE_AT["fields"][j]:
                            act.wait_ge(f_ready, t + 1)
                            src = route[:64 * halves, 0, 0:256].rearrange("p (f t) -> p f t", f=4)[:, :, 0:tt]
                            A(FT[:64 * halves, :, 0:tt], src, ACT.Copy).then_inc(f_taken, 1)
                        s = jj - PE_AT["scatter"][j]
                        if 0 <= s < tt // SUB:
                            act.wait_ge(scat_ready, t * 4 + s + 3)
                            for half in range(halves):
                                at = j * P + half * 64 + s * SUB
                                last = A(G[:, b, :, at:at + SUB].rearrange("p j t -> p t j"), scat[:, half, :, :], ACT.Copy)
                            last.then_inc(scat_taken, 1)
                if blocks:
                    act.wait_ge(out_taken, g + 2)
                    act.dma_start(tokens(h_out, g * EG, b_tiles, b_rows), h[:b_rows, q, 0:b_tiles, :]).then_inc(h_stored, 16)
            turns(act, turn)
            act.wait_ge(h_stored, 16 * (EGROUPS + 3))

        @block.vector
        def _(dve):
            v = nc.vector
            dve.sem_inc(sims_taken, 1)
            dve.sem_inc(out_taken, 1)
            dve.wait_ge(const_made, 3)
            dve.wait_ge(const_in, 16 * N_CONST)

            def pick(step, t, link, link_apart, rows):
                R = slice(0, rows)
                flat = sums[R].rearrange("p h a b -> p h (a b)")
                sims = route[R, :, :].rearrange("p a (h s k) -> p (a h s) k", s=2, k=NKEYS)
                eight = iota[R, 0:8].rearrange("p (o a) -> p o a", o=1).broadcast_to([rows, 64, 8])
                num = best_if[R, :, :].rearrange("p (h s) k -> p h s k", s=2)

                def number(side, dst):
                    where = pk_f[R, side, :].rearrange("p (k o) -> p k o", o=1).broadcast_to([rows, 64, 8])
                    link(v.tensor_tensor(picked[R].rearrange("p h k a -> p (h k) a"), where, eight, ALU.is_equal))
                    link(v.tensor_tensor(picked[R], picked[R], num[:, :, side, :].rearrange("p h (o a) -> p h o a", o=1)
                                         .broadcast_to([rows, PH, PK, 8]), ALU.mult))
                    link(v.tensor_reduce(dst, picked[R].rearrange("p h k a -> p (h k) a"), AX.X, ALU.add))

                if step == 0:
                    dve.wait_ge(sims_ready, t + 1)
                    dve.sem_inc(dve_passed, 1)
                    for s in range(2 * PH):
                        last = v.max(best[R, s, :], sims[:, s, :])
                    link_apart(last)
                elif step == 1:
                    for s in range(2 * PH):
                        last = v.max_index(best_i[R, s, :], best[R, s, :], sims[:, s, :])
                    link(last)
                    dve.sem_inc(sims_taken, 1)
                    v.tensor_copy(best_if[R], best_i[R])
                elif step == 2:
                    s1 = best[R, :, :].rearrange("p (h s) k -> p h s k", s=2)
                    b1 = s1[:, :, 0, :].rearrange("p h (k o) -> p h k o", o=1).broadcast_to([rows, PH, 8, 8])
                    b2 = s1[:, :, 1, :].rearrange("p h (o k) -> p h o k", o=1).broadcast_to([rows, PH, 8, 8])
                    link_apart(v.tensor_tensor(sums[R], b1, b2, ALU.add))
                    for h_ in range(PH):
                        last = v.max(fs[R, h_, :], flat[:, h_, :])
                    link_apart(last)
                elif step == 3:
                    for h_ in range(PH):
                        last = v.max_index(pk[R, h_ * PK:(h_ + 1) * PK], fs[R, h_, :], flat[:, h_, :])
                    link(last)
                    v.tensor_scalar(pk_u[R, 0, :], pk[R, :], 3, None, ALU.logical_shift_right)
                    link(v.tensor_scalar(pk_u[R, 1, :], pk[R, :], 7, None, ALU.bitwise_and))
                    link(v.tensor_copy(pk_f[R], pk_u[R]))
                elif step == 4:
                    number(0, fields[R, 0, :])
                elif step == 5:
                    number(1, j_f[R, :])
                else:
                    link(v.tensor_copy(j_u[R, :], j_f[R, :]))
                    v.tensor_scalar(j_parts[R, 0, :], j_u[R, :], 1, None, ALU.logical_shift_right)
                    link(v.tensor_scalar(j_parts[R, 1, :], j_u[R, :], 1, None, ALU.bitwise_and))
                    v.tensor_copy(fields[R, 1, :], j_parts[R, 0, :])
                    link(v.tensor_copy(par[R, :], j_parts[R, 1, :]))
                    weight = fs[R].rearrange("p h k -> p (h k)")
                    link(v.scalar_tensor_tensor(fields[R, 3, :], weight, 0.0, par[R, :], ALU.max, ALU.mult))
                    v.scalar_tensor_tensor(fields[R, 2, :], weight, 0.0, fields[R, 3, :], ALU.max, ALU.subtract)\
                        .then_inc(fields_ready, 1)

            def one_hot(s, t, link, halves):
                q = 64 * halves
                at = slice(s * SUB, (s + 1) * SUB)

                def wide(f, n):
                    return FT[:q, f, at].rearrange("p (t o) -> p t o", o=1).broadcast_to([q, SUB, n])

                def numbers(n):
                    return iota[:q, 0:n].rearrange("p (o i) -> p o i", o=1).broadcast_to([q, SUB, n])
                if s == 0:
                    dve.wait_ge(f_taken, t + 2)
                dve.wait_ge(scat_ready, t * 4 + s + 1)
                link(v.tensor_tensor(eq[:q], wide(0, NKEYS), numbers(NKEYS), ALU.is_equal))
                for parity in range(2):
                    v.tensor_tensor(one_i[:q, s % 2, :, parity, :], eq[:q], wide(2 + parity, NKEYS), ALU.mult)
                link(v.tensor_tensor(one_j[:q, s % 2, :, :], wide(1, JB), numbers(JB), ALU.is_equal))
                dve.sem_inc(one_ready, 1)

            def turn(g, blocks, routing, q):
                tiles, rows, halves, tt = shape_of(routing == "tail")
                b_tiles, b_rows, _, _ = shape_of(blocks == "tail")
                nb = b_tiles * b_rows
                ga, b = g + 1, 1 - q
                chain = Chain(dve, chained, ROUTE_LINKS, ga)
                link = chain.link
                R, t_ = slice(0, rows), slice(0, tiles)
                for jj in range(JB):
                    if blocks:
                        dve.wait_ge(gelu_ready, g * JB + jj + 3)
                        if jj == 0:
                            dve.wait_ge(scat_taken, g * 8 + (9 if blocks == "full" else 2))
                        v.tensor_tensor(hid[:, jj % 4, 0:nb], hid[:, jj % 4, 0:nb], G[:, q, jj, 0:nb], ALU.mult)\
                            .then_inc(gated, 1)
                    if not routing:
                        continue
                    if jj == DVE_AT["h"]:
                        dve.wait_ge(loaded, ga * 32 + 32)
                        bias = bout[R, :].rearrange("p (a d) -> p a d", a=1).broadcast_to([rows, tiles, D])
                        hb = h[:, b]
                        link(v.tensor_tensor(hb[R, t_, :], hb[R, t_, :], bias, ALU.add))
                        dve.wait_ge(proj_ready, ga + 1)
                        proj = route[R, 0, :].rearrange("p (k d) -> p k d", k=2)[:, t_, :]
                        chain.link_apart(v.tensor_tensor(hb[R, t_, :], hb[R, t_, :], proj, ALU.add))
                        dve.sem_inc(proj_taken, 1)
                        statistics(v, chain, hb, stats, mv, ve, tiles, rows, LN_EPS).then_inc(var_ready, 1)
                    if jj == DVE_AT["x"]:
                        dve.wait_ge(rstd_ready, 2 * ga + 1)
                        chain.link_apart(normalise(v, h[:, b], x, mv, rstd, tiles, rows))
                        link(statistics(v, chain, x, stats, mv, ve, tiles, rows, RMS_EPS))
                        link(v.tensor_tensor(m2[R, t_], mv[R, t_, 0], mv[R, t_, 0], ALU.mult))
                        v.tensor_tensor(ve[R, t_], ve[R, t_], m2[R, t_], ALU.add).then_inc(var_ready, 1)
                    if jj == DVE_AT["xn"]:
                        dve.wait_ge(rstd_ready, 2 * ga + 2)
                        for j in range(tiles):
                            last = v.tensor_scalar(x[R, j, :], x[R, j, :], rstd[R, j:j + 1], None, ALU.mult)
                        last.then_inc(xn_ready, 1)
                    for j in range(tiles):
                        t = ga * 2 + j
                        step = jj - DVE_AT["pick"][j]
                        if 0 <= step < 7:
                            pick(step, t, link, chain.link_apart, rows)
                        s = jj - DVE_AT["one_hot"][j]
                        if 0 <= s < tt // SUB:
                            one_hot(s, t, link, halves)
                if blocks:
                    dve.wait_ge(up_done, g * JB + JB + 4)
                    v.tensor_tensor(h[:b_rows, q, 0:b_tiles, :], h[:b_rows, q, 0:b_tiles, :], total[:b_rows, 0:b_tiles, :],
                                    ALU.add).then_inc(out_taken, 1)
                assert routing != "full" or chain.count == ROUTE_LINKS, chain.count
            turns(dve, turn)

        @block.gpsimd
        def _(pool):
            nc.gpsimd.memset(minus_half[:, :], -0.5).then_inc(const_made, 1)
            nc.gpsimd.iota(iota[:, :], [[1, NKEYS]], base=0, channel_multiplier=0, allow_small_or_imprecise_dtypes=True)\
                .then_inc(const_made, 1)
            pool.wait_ge(const_made, 2)
            pool.sem_inc(const_made, 1)

            def turn(g, blocks, routing, q):
                if routing is None:
                    return
                tiles, rows, _, _ = shape_of(routing == "tail")
                for n in range(2):
                    pool.wait_ge(var_ready, 2 * (g + 1) + n + 1)
                    nc.gpsimd.tensor_tensor(rstd[:rows, 0:tiles], ve[:rows, 0:tiles], minus_half[:rows, 0:tiles],
                                            ALU.pow).then_inc(rstd_ready, 1)
            turns(pool, turn)


def padded_heads(w, axis):
    w = np.moveaxis(np.asarray(w), axis, 0)
    out = np.zeros((HEADS, SLOT) + w.shape[1:], w.dtype)
    out[:, :HD] = w.reshape((HEADS, HD) + w.shape[1:])
    return np.ascontiguousarray(np.moveaxis(out.reshape((HEADS * SLOT,) + w.shape[1:]), 0, axis))


def on_slots(vec):
    return np.ascontiguousarray(vec.reshape(HG, P).T)


def constants():
    p = np.arange(P)
    head = np.arange(HEADS)
    gamma = np.array([1.0 - 2.0 ** (-5 - 8 * i // HEADS) for i in range(HEADS)], np.float32)
    query = np.concatenate([np.arange(T), np.arange(P, T)])
    key = np.concatenate([np.zeros(T, np.int64), np.full(T - P, P)])[None, :] + p[:, None]
    diff = query[None, :] - key
    power = gamma[None, :, None] ** np.maximum(diff, 0).astype(np.float32)[:, None, :]
    decay = np.where(diff[:, None, :] >= 0, power * np.float32(SCALE), np.float32(0)).astype(np.float32)
    col = np.arange(HEADS * SLOT)
    own = (col[None, :] // SLOT == head[:, None]).astype(np.float32)
    sel = (head[None, None, :] == SLOTS * np.arange(HG)[None, :, None] + (p // SLOT)[:, None, None]).astype(np.float32)
    avg = ((p[:, None] // SLOT == p[None, :] // SLOT) & (p[:, None] % SLOT < HD)).astype(np.float32) / HD
    valid = p[None, :] <= p[:, None]
    mask = np.where(np.stack([valid, valid.T], 1), 0.0, BIG).astype(mybir.dt.np(BF16))
    own17 = np.repeat(np.eye(HEADS, dtype=np.float32)[:, :, None], VC, 2)
    aug = np.zeros((HEADS, HG, P), np.float32)
    aug[head, head // SLOTS, SLOT * (head % SLOTS) + HD] = 1
    ones_row = np.zeros((HEADS, SLOT), np.float32)
    ones_row[:, HD] = 1
    return {"mask": mask, "own17": own17, "aug": aug, "ones_row": ones_row.reshape(-1), "ident": np.eye(P, dtype=np.float32), "decay": decay, "own": own, "sel": sel, "avg": avg.astype(np.float32)}


def laid_out(inputs):
    a = {k: np.asarray(v) for k, v in inputs.items()}
    c = constants()
    tight = np.ascontiguousarray

    def by_state(m):
        return m.reshape(PAIRS, 2, 64).transpose(1, 2, 0).reshape(P, PAIRS)

    def column(vec):
        return tight(vec.reshape(DC, P).T)

    def head_weight(w):
        return padded_heads(w.transpose(1, 0, 2).reshape(D, D), 1)

    def slots(vec):
        return on_slots(padded_heads(vec, 0))

    b_ri, qkv, zero = a["L0_tok_B_ri"], a["L1_attn_w_qkv"], np.zeros(D, np.float32)
    down = a["L1_ffn_expert_down"].reshape(NKEYS, JB, 2, DC, P)
    up = a["L1_ffn_expert_up"].reshape(NKEYS, JB, 2, D)
    return {
        "cls_tok": a["cls_tok"].reshape(1, D),
        "log_dt": tight(a["L0_tok_log_dt"].reshape(PAIRS, 2).T),
        "inv_A_real": tight(by_state(a["L0_tok_inv_A_real"])),
        "A_imag": tight(by_state(a["L0_tok_A_imag"])),
        "B_ri": tight(np.stack([by_state(b_ri[..., 0]), by_state(b_ri[..., 1])], 1)),
        "C_ri": tight(a["x"].reshape(B, PAIRS, 2, 64, 2).transpose(2, 3, 4, 1, 0).reshape(P, 2, PAIRS, B)),
        "ret_wq": head_weight(a["L0_attn_Wq"]), "ret_wk": head_weight(a["L0_attn_Wk"]),
        "ret_wv": head_weight(a["L0_attn_Wv"]),
        "ret_gnw": slots(a["L0_attn_gn_weight"]), "ret_gnb": slots(a["L0_attn_gn_bias"]),
        "ret_wout": a["L0_attn_Wout"],
        "ln1_g": column(a["L0_ffn_ln1_g"]), "ln1_b": column(a["L0_ffn_ln1_b"]),
        "ln2_g": column(a["L0_ffn_ln2_g"]), "ln2_b": column(a["L0_ffn_ln2_b"]),
        "soft_wq": padded_heads(a["L0_ffn_Wq"], 1), "soft_wk": padded_heads(a["L0_ffn_Wk"], 1),
        "soft_wv": a["L0_ffn_Wv"], "soft_bq": slots(a["L0_ffn_bq"]),
        "soft_bk": on_slots(np.where(c["ones_row"] > 0, c["ones_row"], padded_heads(a["L0_ffn_bk"], 0))),
        "soft_bv": a["L0_ffn_bv"].reshape(1, D), "soft_wp": a["L0_ffn_Wp"], "soft_bp": a["L0_ffn_bp"].reshape(1, D),
        "gate_w": a["L0_ffn_gate_W"], "gate_b": a["L0_ffn_gate_b"].reshape(1, EXPERTS),
        "moe_w1": tight(a["L0_ffn_exp_W1"].reshape(EXPERTS, DC, P, HIDDEN).transpose(2, 0, 1, 3)),
        "moe_b1": tight(a["L0_ffn_exp_b1"].reshape(EXPERTS, HB, P).transpose(2, 0, 1)),
        "moe_w2": tight(a["L0_ffn_exp_W2"].reshape(EXPERTS, HB, P, D).transpose(2, 0, 1, 3)),
        "moe_b2": a["L0_ffn_exp_b2"],
        "stable_wq": padded_heads(tight(qkv[:D].T), 1), "stable_wk": padded_heads(tight(qkv[D:2 * D].T), 1),
        "stable_wv": tight(qkv[2 * D:].T), "stable_bq": on_slots(padded_heads(zero, 0)),
        "stable_bk": on_slots(c["ones_row"]), "stable_bv": zero.reshape(1, D),
        "stable_wout": tight(a["L1_attn_w_out"].T), "stable_bout": a["L1_attn_b_out"].reshape(1, D),
        "norm_w": column(a["L1_ffn_norm_w"]),
        "peer_w_q": tight(a["L1_ffn_w_q"].reshape(2 * PH, P, D).transpose(1, 0, 2)),
        "peer_keys": tight(a["L1_ffn_keys"].transpose(3, 0, 2, 1).reshape(P, 2 * PH, NKEYS)),
        "peer_down": tight(down.transpose(4, 3, 1, 2, 0).reshape(P, DC, JB, P)),
        "peer_up": tight(up.transpose(2, 0, 1, 3).reshape(P, JB, D)),
        "ident": c["ident"], "decay": c["decay"], "own": c["own"], "own17": c["own17"], "sel": c["sel"], "avg": c["avg"],
        "aug": c["aug"], "mask": c["mask"],
    }


def tower(nc, i, out):
    rows = out.rearrange("b t d -> (b t) d")

    def scratch(name, shape):
        return nc.dram_tensor(name, shape, F32, kind="Internal").ap()

    h0 = scratch("h0", (B, T, D))
    xT, aT = scratch("xT", (D, NTOK)), scratch("aT", (D, NTOK))
    x2, hx, h2 = scratch("x2", (NTOK, D)), scratch("hx", (NTOK, D)), scratch("h2", (NTOK, D))
    h0_rows = h0.rearrange("b t d -> (b t) d")
    token_mixer(nc, i["log_dt"], i["inv_A_real"], i["A_imag"], i["B_ri"], i["C_ri"], i["cls_tok"], h0)
    enter_retention(nc, h0_rows, i["ident"], xT)
    retention(nc, xT, i["ret_wq"], i["ret_wk"], i["ret_wv"], i["ret_gnw"], i["ret_gnb"], i["decay"], i["own"], i["sel"],
              i["avg"], aT)
    enter_attention(nc, aT, h0_rows, i["ret_wout"], i["ln1_g"], i["ln1_b"], i["ident"], hx, x2, xT)
    attention(nc, True, xT, i["soft_wq"], i["soft_wk"], i["soft_wv"], i["soft_bq"], i["soft_bk"], i["soft_bv"],
              i["own17"], i["sel"], i["aug"], i["ident"], i["mask"], aT)
    experts(nc, aT, x2, hx, i["soft_wp"], i["soft_bp"], i["ln2_g"], i["ln2_b"], i["gate_w"], i["gate_b"],
            i["moe_w1"], i["moe_b1"], i["moe_w2"], i["moe_b2"], i["ident"], h2, xT)
    attention(nc, False, xT, i["stable_wq"], i["stable_wk"], i["stable_wv"], i["stable_bq"], i["stable_bk"],
              i["stable_bv"], i["own17"], i["sel"], i["aug"], i["ident"], i["mask"], aT)
    product_keys(nc, aT, h2, i["stable_wout"], i["stable_bout"], i["norm_w"], i["peer_w_q"], i["peer_keys"],
                 i["peer_down"], i["peer_up"], i["ident"], rows)


def kernel(**inputs):
    import concourse.bacc as bacc
    from concourse.bass_utils import run_bass_kernel_spmd

    arrays = laid_out(inputs)
    nc = bacc.Bacc("TRN2", target_bir_lowering=False, num_devices=1)
    aps = {name: nc.dram_tensor(f"in_{name}", a.shape, mybir.dt.from_np(a.dtype), kind="ExternalInput").ap()
           for name, a in arrays.items()}
    out = nc.dram_tensor("out", (B, T, D), F32, kind="ExternalOutput").ap()
    tower(nc, aps, out)
    result = run_bass_kernel_spmd(nc, [{f"in_{name}": a for name, a in arrays.items()}], core_ids=[0])
    return result.results[0]["out"]
```

```python
import math
from contextlib import ExitStack

import numpy as np

import concourse.bass as bass
from concourse import mybir

F32 = mybir.dt.float32
U32 = mybir.dt.uint32
ALU = mybir.AluOpType
ACT = mybir.ActivationFunctionType
AX = mybir.AxisListType

P = 128
B = 16
D = 256
DC = D // P
T = D + 1
NTOK = B * T
HEADS, HD = 16, 16
SLOT = 32
SLOTS = P // SLOT
HG = HEADS // SLOTS
GROUP = 512
NGROUPS = NTOK // GROUP
TAIL = NTOK - NGROUPS * GROUP
LN_EPS = 1e-5
RMS_EPS = 1e-6


class Chain:

    def __init__(self, engine, sem, per=0, turn=0, base=0):
        self.engine, self.sem, self.per, self.turn, self.base, self.count = engine, sem, per, turn, base, 0

    def link(self, instruction):
        instruction.then_inc(self.sem, 1)
        self.count += 1
        self.engine.wait_ge(self.sem, self.turn * self.per + self.base + self.count)

    def link_apart(self, instruction):
        self.link(instruction)
        self.engine.sem_inc(self.sem, 1)
        self.count += 1

    def done(self):
        assert self.count == self.per, (self.count, self.per)


class Room:

    def __init__(self, nc, ctx, name):
        self.nc, self.ctx, self.name, self.sems = nc, ctx, name, []
        ctx.callback(self.close)

    def close(self):
        self.nc.clear_and_free_semaphores(self.sems)
        self.nc.all_engine_barrier()

    def sb(self, name, shape, dt=F32):
        return self.ctx.enter_context(self.nc.sbuf_tensor(f"{self.name}_{name}", shape, dt))

    def ps(self, name, shape, dt=F32):
        return self.ctx.enter_context(self.nc.psum_tensor(f"{self.name}_{name}", shape, dt))

    def sem(self, name):
        self.sems.append(self.nc.alloc_semaphore(f"{self.name}_{name}"))
        return self.sems[-1]


L1 = 64
LA = D // L1
PAIRS = D // 2
PC = 16
LN2 = math.log(2.0)
LN2_HI = math.floor(LN2 * 2 ** 15) / 2 ** 15
LN2_LO = LN2 - LN2_HI
ROUND = 1.5 * 2 ** 23
EXP_TERMS = 8
TOK_LINKS = 75


def token_mixer(nc, log_dt, inv_A_real, A_imag, B_ri, C_ri, cls_tok, h_out):
    ctx = ExitStack()
    with ctx:
        r = Room(nc, ctx, "tok")
        par = r.sb("par", [P, 5, PC])
        c_ri = r.sb("c_ri", [P, 2, PC, B])
        ex = r.sb("ex", [P, 2, PC])
        two_k = r.sb("two_k", [P, PC], mybir.dt.int32)
        tmp = r.sb("tmp", [P, 6, PC])
        E = r.sb("E", [P, 2, 8, PC])
        V = r.sb("V", [P, 2, PC, L1])
        W = r.sb("W", [P, 2, PC, LA, B])
        prod = r.sb("prod", [P, 4, PC * 32])
        res = r.sb("res", [P, PC, L1])
        cls = r.sb("cls", [B, D])
        acc = r.ps("acc", [P, PC, L1])
        loaded, inputs_free = r.sem("loaded"), r.sem("inputs_free")
        exps, chained, powers_ready, products_done = r.sem("exps"), r.sem("chained"), r.sem("powers"), r.sem("products")
        res_ready, stored, cls_in, cls_out = r.sem("res_ready"), r.sem("stored"), r.sem("cls_in"), r.sem("cls_out")
        waits_passed = r.sem("waits_passed")
        turns = PAIRS // PC
        block = ctx.enter_context(nc.Block())

        @block.sync
        def _(sp):
            sp.dma_start(cls[:, :], cls_tok[0:1, :].broadcast_to([B, D])).then_inc(cls_in, 16)
            sp.wait_ge(cls_in, 16)
            sp.dma_start(h_out[:, 0, :], cls[:, :]).then_inc(cls_out, 16)
            sp.sem_inc(stored, 16)
            with sp.Fori(0, turns) as t:
                sp.wait_ge(inputs_free, t + 1)
                at = bass.ds(t * PC, PC)
                for h2 in range(2):
                    half = slice(64 * h2, 64 * h2 + 64)
                    sp.dma_start(par[half, 0, :], log_dt[h2:h2 + 1, at].broadcast_to([64, PC])).then_inc(loaded, 16)
                sp.dma_start(par[:, 1, :], inv_A_real[:, at]).then_inc(loaded, 16)
                sp.dma_start(par[:, 2, :], A_imag[:, at]).then_inc(loaded, 16)
                sp.dma_start(par[:, 3:5, :], B_ri[:, :, at]).then_inc(loaded, 16)
                sp.dma_start(c_ri[:, :, :, :], C_ri[:, :, at, :]).then_inc(loaded, 16)
                sp.wait_ge(res_ready, t + 2)
                for h2 in range(2):
                    for a in range(LA):
                        p0 = 64 * h2 + B * a
                        dst = h_out[:, bass.ds(1 + h2 + t * (2 * PC), PC, 2), L1 * a:L1 * a + L1]
                        sp.dma_start(dst, res[p0:p0 + B, :, :]).then_inc(stored, 16)
            sp.wait_ge(stored, 16 * 8 * turns + 16)
            sp.wait_ge(cls_out, 16)

        @block.scalar
        def _(act):
            act.sem_inc(res_ready, 1)
            with act.Fori(0, turns) as t:
                act.wait_ge(loaded, (t + 1) * 96)
                nc.scalar.activation(ex[:, 1, :], par[:, 1, :], ACT.Exp).then_inc(exps, 1)
                act.wait_ge(stored, t * 128 + 16)
                act.wait_ge(products_done, t + 2)
                nc.scalar.activation(res[:, :, :], acc[:, :, :], ACT.Copy, scale=2.0).then_inc(res_ready, 1)

        @block.vector
        def _(dve):
            nc.vector.memset(prod[:, :, 0:1], 0.0).then_inc(inputs_free, 1)
            v = nc.vector

            def products(chain, x, er, ei, n):
                shape = x[0].shape
                q = [prod[:, k, 0:n].rearrange("p (a b) -> p a b", a=shape[1]) if len(shape) == 3 else
                     prod[:, k, 0:n].rearrange("p (a b c) -> p a b c", a=shape[1], b=shape[2]) for k in range(4)]
                v.tensor_tensor(q[0], x[0], er, ALU.mult)
                v.tensor_tensor(q[1], x[1], ei, ALU.mult)
                v.tensor_tensor(q[2], x[0], ei, ALU.mult)
                chain.link(v.tensor_tensor(q[3], x[1], er, ALU.mult))
                return q

            with dve.Fori(0, turns) as t:
                chain = Chain(dve, chained, TOK_LINKS, t)
                link = chain.link
                a, b, den, x2, y2, na = (tmp[:, k, :] for k in range(6))
                dve.wait_ge(loaded, (t + 1) * 96)
                x, k_, rem, p, dt = par[:, 0, :], tmp[:, 0, :], tmp[:, 1, :], tmp[:, 2, :], ex[:, 0, :]
                link(v.tensor_scalar(k_, x, 1.0 / LN2, None, ALU.mult))
                link(v.tensor_scalar(k_, k_, ROUND, None, ALU.add))
                link(v.tensor_scalar(k_, k_, ROUND, None, ALU.subtract))
                link(v.tensor_scalar(k_, k_, -126.0, 127.0, ALU.max, ALU.min))
                link(v.scalar_tensor_tensor(rem, k_, -LN2_HI, x, ALU.mult, ALU.add))
                link(v.scalar_tensor_tensor(rem, k_, -LN2_LO, rem, ALU.mult, ALU.add))
                link(v.tensor_scalar(p, rem, 1.0 / math.factorial(EXP_TERMS), None, ALU.mult))
                for n in range(EXP_TERMS - 1, 0, -1):
                    link(v.scalar_tensor_tensor(p, p, 1.0 / math.factorial(n), rem, ALU.add, ALU.mult))
                link(v.tensor_scalar(two_k[:, :], k_, 127.0, float(1 << 23), ALU.add, ALU.mult))
                link(v.scalar_tensor_tensor(dt, p, 1.0, two_k[:, :].bitcast(F32), ALU.add, ALU.mult))
                dve.wait_ge(exps, t + 1)
                link(v.scalar_tensor_tensor(a, ex[:, 1, :], -0.5, dt, ALU.mult, ALU.mult))
                link(v.scalar_tensor_tensor(b, par[:, 2, :], 0.5, dt, ALU.mult, ALU.mult))
                link(v.tensor_scalar(na, a, -1.0, 1.0, ALU.mult, ALU.add))
                link(v.tensor_tensor(den, na, na, ALU.mult))
                link(v.tensor_tensor(y2, b, b, ALU.mult))
                link(v.tensor_tensor(den, den, y2, ALU.add))
                link(v.reciprocal(den, den))
                link(v.scalar_tensor_tensor(x2, a, -1.0, a, ALU.mult, ALU.mult))
                link(v.scalar_tensor_tensor(x2, x2, 1.0, y2, ALU.add, ALU.subtract))
                dve.wait_ge(products_done, t + 1)
                link(v.tensor_tensor(E[:, 0, 0, :], x2, den, ALU.mult))
                link(v.scalar_tensor_tensor(E[:, 1, 0, :], b, -2.0, den, ALU.mult, ALU.mult))
                for k in range(7):
                    link(v.tensor_tensor(x2, E[:, 0, k, :], E[:, 0, k, :], ALU.mult))
                    link(v.tensor_tensor(y2, E[:, 1, k, :], E[:, 1, k, :], ALU.mult))
                    link(v.scalar_tensor_tensor(E[:, 1, k + 1, :], E[:, 0, k, :], 2.0, E[:, 1, k, :], ALU.mult, ALU.mult))
                    link(v.tensor_tensor(E[:, 0, k + 1, :], x2, y2, ALU.subtract))
                link(v.memset(V[:, 0, :, 0:1], 1.0))
                link(v.memset(V[:, 1, :, 0:1], 0.0))
                for k in range(6):
                    n = 1 << k
                    e = [E[:, c, k, :].rearrange("p (a b) -> p a b", b=1).broadcast_to([P, PC, n]) for c in range(2)]
                    q = products(chain, [V[:, c, :, 0:n] for c in range(2)], e[0], e[1], PC * n)
                    v.tensor_tensor(V[:, 0, :, n:2 * n], q[0], q[1], ALU.subtract)
                    link(v.tensor_tensor(V[:, 1, :, n:2 * n], q[2], q[3], ALU.add))
                bb = [par[:, 3 + c, :].rearrange("p (a b) -> p a b", b=1).broadcast_to([P, PC, B]) for c in range(2)]
                q = products(chain, [c_ri[:, c, :, :] for c in range(2)], bb[0], bb[1], PC * B)
                v.tensor_tensor(W[:, 0, :, 0, :], q[0], q[1], ALU.subtract)
                last = v.tensor_tensor(W[:, 1, :, 0, :], q[2], q[3], ALU.add)
                link(last)
                v.memset(prod[:, :, 0:1], 0.0).then_inc(inputs_free, 1)
                dve.wait_ge(inputs_free, t + 2)
                for k, s in ((6, 1), (7, 2)):
                    e = [E[:, c, k, :].rearrange("p (a b) -> p a b", b=1).broadcast_to([P, PC, s * B]) for c in range(2)]
                    w = [W[:, c, :, :, :].rearrange("p a s c -> p a (s c)") for c in range(2)]
                    q = products(chain, [w[c][:, :, 0:s * B] for c in range(2)], e[0], e[1], PC * s * B)
                    v.tensor_tensor(w[0][:, :, s * B:2 * s * B], q[0], q[1], ALU.add)
                    link(v.tensor_tensor(w[1][:, :, s * B:2 * s * B], q[3], q[2], ALU.subtract))
                v.memset(prod[:, :, 0:1], 0.0).then_inc(powers_ready, 1)
                dve.wait_ge(powers_ready, t + 1)
                chain.done()

        @block.tensor
        def _(pe):
            pe.sem_inc(products_done, 1)
            with pe.Fori(0, turns) as t:
                pe.wait_ge(powers_ready, t + 1)
                pe.wait_ge(res_ready, t + 1)
                pe.sem_inc(waits_passed, 1)
                for i in range(PC):
                    for h2 in range(2):
                        half = slice(64 * h2, 64 * h2 + 64)
                        for c in range(2):
                            last = nc.tensor.matmul(acc[half, i, :], W[half, c, i, :, :].rearrange("p a c -> p (a c)"),
                                                    V[half, c, i, :], start=c == 0, stop=c == 1)
                last.then_inc(products_done, 1)


def groups(engine, step):
    with engine.Fori(0, NGROUPS) as g:
        step(g * GROUP, g, GROUP // P, P)
    step(NGROUPS * GROUP, NGROUPS, 1, TAIL)


def tokens(ap, t0, tiles, rows):
    return ap[bass.ds(t0, tiles * rows), :].rearrange("(j p) d -> p j d", p=rows)


def statistics(v, chain, x, stats, mv, ve, tiles, rows, eps):
    for j in range(tiles):
        last = v.bn_stats(stats[:rows, j, :], x[:rows, j, :])
    chain.link_apart(last)
    for j in range(tiles):
        last = v.bn_aggr(mv[:rows, j, :], stats[:rows, j, :])
    chain.link(last)
    return v.tensor_scalar(ve[:rows, 0:tiles], mv[:rows, 0:tiles, 1], eps, None, ALU.add)


def normalise(v, x, out, mv, rstd, tiles, rows):
    for j in range(tiles):
        last = v.tensor_scalar(out[:rows, j, :], x[:rows, j, :], mv[:rows, j, 0:1], rstd[:rows, j:j + 1],
                               ALU.subtract, ALU.mult)
    return last


def transposed(nc, out, x, ident, tiles, rows):
    for c in range(DC):
        for j in range(tiles):
            last = nc.tensor.transpose(out[:, c, j * P:j * P + rows], x[:rows, j, c * P:c * P + P],
                                       ident[:rows, :rows])
    return last


def enter_retention(nc, h, ident_in, xT_out):
    ctx = ExitStack()
    with ctx:
        r = Room(nc, ctx, "ent")
        ident = r.sb("ident", [P, P])
        hs = r.sb("hs", [P, 2, 4, D])
        xn = r.sb("xn", [P, 4, D])
        xt = r.sb("xt", [P, DC, GROUP])
        stats, mv = r.sb("stats", [P, 4, 6]), r.sb("mv", [P, 4, 2])
        ve, rstd, minus_half = r.sb("ve", [P, 4]), r.sb("rstd", [P, 4]), r.sb("mh", [P, 4])
        tp = r.ps("tp", [P, DC, GROUP])
        const_in, loaded, h_free = r.sem("const_in"), r.sem("loaded"), r.sem("h_free")
        const_made, chained, var_ready, rstd_ready = r.sem("const_made"), r.sem("chained"), r.sem("var"), r.sem("rstds")
        xn_ready, tp_ready, xt_ready, stored = r.sem("xn_ready"), r.sem("tp_ready"), r.sem("xt_ready"), r.sem("stored")
        block = ctx.enter_context(nc.Block())

        @block.sync
        def _(sp):
            sp.dma_start(ident[:, :], ident_in).then_inc(const_in, 16)

            def step(t0, g, tiles, rows):
                sp.wait_ge(h_free, g + 1)
                sp.dma_start(hs[:rows, 0, 0:tiles, :], tokens(h, t0, tiles, rows)).then_inc(loaded, 16)
            groups(sp, step)

        @block.vector
        def _(dve):
            v = nc.vector
            dve.sem_inc(h_free, 1)

            def step(t0, g, tiles, rows):
                chain = Chain(dve, chained, 3, g)
                dve.wait_ge(loaded, g * 16 + 16)
                statistics(v, chain, hs[:, 0], stats, mv, ve, tiles, rows, LN_EPS).then_inc(var_ready, 1)
                dve.wait_ge(rstd_ready, g + 1)
                dve.wait_ge(tp_ready, g + 1)
                normalise(v, hs[:, 0], xn, mv, rstd, tiles, rows).then_inc(xn_ready, 1)
                dve.wait_ge(xn_ready, g + 1)
                dve.sem_inc(h_free, 1)
                chain.done()
            groups(dve, step)

        @block.gpsimd
        def _(pool):
            nc.gpsimd.memset(minus_half[:, :], -0.5).then_inc(const_made, 1)
            pool.wait_ge(const_made, 1)

            def step(t0, g, tiles, rows):
                pool.wait_ge(var_ready, g + 1)
                nc.gpsimd.tensor_tensor(rstd[:rows, 0:tiles], ve[:rows, 0:tiles], minus_half[:rows, 0:tiles],
                                        ALU.pow).then_inc(rstd_ready, 1)
            groups(pool, step)

        @block.tensor
        def _(pe):
            pe.sem_inc(tp_ready, 1)
            pe.wait_ge(const_in, 16)

            def step(t0, g, tiles, rows):
                pe.wait_ge(xt_ready, g + 1)
                pe.wait_ge(xn_ready, g + 1)
                transposed(nc, tp, xn, ident, tiles, rows).then_inc(tp_ready, 1)
            groups(pe, step)

        @block.scalar
        def _(act):
            act.sem_inc(xt_ready, 1)
            act.sem_inc(stored, 16)

            def step(t0, g, tiles, rows):
                act.wait_ge(stored, g * 16 + 16)
                act.wait_ge(tp_ready, g + 2)
                n = tiles * rows
                nc.scalar.activation(xt[:, :, 0:n], tp[:, :, 0:n], ACT.Copy).then_inc(xt_ready, 1)
                act.wait_ge(xt_ready, g + 2)
                act.dma_start(xT_out[:, bass.ds(t0, n)].rearrange("(c p) t -> p c t", p=P),
                              xt[:, :, 0:n]).then_inc(stored, 16)
            groups(act, step)
            act.wait_ge(stored, 16 * (NGROUPS + 2))


ODD = T - 1
SPAN = T + (T - P)
PAIRS_OF_HEADS = HEADS // 2
PROJ = 2 * HG + DC + 1
SCALE = HD ** -0.5


def slot(head):
    return head // SLOTS, slice(SLOT * (head % SLOTS), SLOT * (head % SLOTS) + HD)


def retention(nc, xT_in, wq, wk, wv, gnw_in, gnb_in, decay_in, own_in, sel_in, avg_in, cT_out):
    ctx = ExitStack()
    with ctx:
        r = Room(nc, ctx, "ret")
        wq_s, wk_s, wv_s = (r.sb(n, [P, DC, 512]) for n in ("wq", "wk", "wv"))
        decay = r.sb("decay", [P, HEADS, SPAN])
        own = r.sb("own", [HEADS, 512])
        sel = r.sb("sel", [P, HG, HEADS])
        avg = r.sb("avg", [P, P])
        gnw, gnb = r.sb("gnw", [P, HG]), r.sb("gnb", [P, HG])
        xT = r.sb("xT", [P, DC, T])
        odd_x = r.sb("odd_x", [P, DC, HEADS])
        QT, KT = r.sb("QT", [P, HG, T]), r.sb("KT", [P, HG, T])
        V = r.sb("V", [P, DC, 512])
        v_odd, V_odd = r.sb("v_odd", [HEADS, 512]), r.sb("V_odd", [HEADS, 512])
        K_odd = r.sb("K_odd", [P, HG, HEADS])
        p_odd = r.sb("p_odd", [HEADS, 1])
        PT = r.sb("PT", [P, 2, 2, SPAN])
        cT, cN = r.sb("cT", [P, HG, T]), r.sb("cN", [P, HG, T])
        stats, mv = r.sb("stats", [P, HG, 6]), r.sb("mv", [P, HG, 2])
        d, q, ve, rstd, mh = (r.sb(n, [P, HG]) for n in ("d", "q", "ve", "rstd", "mh"))
        gmean, gscale, gbias = (r.sb(n, [P, HG]) for n in ("gmean", "gscale", "gbias"))
        S = r.ps("S", [P, 2, 2, 512])
        O = r.ps("O", [P, 2, 512])
        proj = r.ps("proj", [P, 2, 512])
        const_in, loaded, x_free = r.sem("const_in"), r.sem("loaded"), r.sem("x_free")
        proj_ready, proj_taken, odd_ready, odd_copied = (r.sem(n) for n in ("proj_ready", "proj_taken", "odd_ready", "odd_x"))
        s_ready, p_ready, av_done = r.sem("s_ready"), r.sem("p_ready"), r.sem("av_done")
        o_ready, o_taken, so_ready, so_taken = (r.sem(n) for n in ("o_ready", "o_taken", "so_ready", "so_taken"))
        chained, means_ready, gm_ready, gv_ready, q_ready = (r.sem(n) for n in ("chained", "means", "gm", "gv", "q"))
        ve_ready, rstd_ready, affine_ready, normed, stored = (r.sem(n) for n in ("ve", "rstd", "affine", "normed", "stored"))
        const_made = r.sem("const_made")
        block = ctx.enter_context(nc.Block())

        @block.sync
        def _(sp):
            for dst, src in ((wq_s, wq), (wk_s, wk), (wv_s, wv)):
                sp.dma_start(dst[:, :, :], src.rearrange("(c p) n -> p c n", p=P)).then_inc(const_in, 16)
            for dst, src in ((own, own_in), (avg, avg_in), (gnw, gnw_in), (gnb, gnb_in)):
                sp.dma_start(dst[:, :], src).then_inc(const_in, 16)
            sp.dma_start(sel[:, :, :], sel_in).then_inc(const_in, 16)
            sp.dma_start(decay[:, :, :], decay_in).then_inc(const_in, 16)
            with sp.Fori(0, B) as b:
                sp.wait_ge(x_free, b + 1)
                sp.dma_start(xT[:, :, :], xT_in[:, bass.ds(b * T, T)].rearrange("(c p) t -> p c t", p=P))\
                  .then_inc(loaded, 16)
                sp.wait_ge(normed, b + 1)
                for s in range(SLOTS):
                    dst = cT_out[:, bass.ds(b * T, T)].rearrange("(g s e) t -> s e g t", g=HG, s=SLOTS)
                    sp.dma_start(dst[s], cN[SLOT * s:SLOT * s + HD, :, :]).then_inc(stored, 16)
            sp.wait_ge(stored, 16 * (SLOTS * B + 1))

        @block.tensor
        def _(pe):
            pe.wait_ge(const_in, 144)
            for s in (s_ready, av_done, x_free):
                pe.sem_inc(s, 1)
            with pe.Fori(0, B) as b:
                pe.wait_ge(loaded, b * 16 + 16)

                def take_bank(n):
                    if n != 1:
                        pe.wait_ge(proj_taken, b * PROJ + 1 + (n - 1 if n else 0))
                    else:
                        pe.wait_ge(affine_ready, b + 1)

                for n in range(2 * HG):
                    take_bank(n)
                    w, g = (wq_s, wk_s)[n // HG], n % HG
                    for c in range(DC):
                        last = nc.tensor.matmul(proj[:, n % 2, 0:T], w[:, c, g * P:g * P + P], xT[:, c, :],
                                                start=c == 0, stop=c == DC - 1)
                    last.then_inc(proj_ready, 1)
                for k in range(DC):
                    n = 2 * HG + k
                    take_bank(n)
                    for c in range(DC):
                        last = nc.tensor.matmul(proj[:, n % 2, :], xT[:, c, k * P:k * P + P], wv_s[:, c, :],
                                                start=c == 0, stop=c == DC - 1)
                    last.then_inc(proj_ready, 1)
                n = PROJ - 1
                take_bank(n)
                pe.wait_ge(odd_copied, b + 1)
                for c in range(DC):
                    last = nc.tensor.matmul(proj[:HEADS, n % 2, :], odd_x[:, c, :], wv_s[:, c, :],
                                            start=c == 0, stop=c == DC - 1)
                last.then_inc(proj_ready, 1)
                pe.wait_ge(proj_taken, b * PROJ + 1 + PROJ)
                pe.sem_inc(x_free, 1)

                def scores(u):
                    pe.wait_ge(p_ready, b * PAIRS_OF_HEADS + u if u else b * PAIRS_OF_HEADS + 1)
                    for i in range(2):
                        g, rows = slot(2 * u + i)
                        nc.tensor.matmul(S[:, u % 2, i, 0:T], KT[rows, g, 0:P], QT[rows, g, :], start=True, stop=True)
                        last = nc.tensor.matmul(S[:, u % 2, i, T:SPAN], KT[rows, g, P:2 * P], QT[rows, g, P:T],
                                                start=True, stop=True)
                    last.then_inc(s_ready, 1)

                pe.wait_ge(odd_ready, 2 * b + 2)
                pe.wait_ge(so_taken, b + 1)
                for g in range(HG):
                    last = nc.tensor.matmul(O[:HEADS, 1, 511:512], K_odd[:, g, :], QT[:, g, ODD:T],
                                            start=g == 0, stop=g == HG - 1)
                last.then_inc(so_ready, 1)
                scores(0)
                for u in range(PAIRS_OF_HEADS):
                    if u + 1 < PAIRS_OF_HEADS:
                        scores(u + 1)
                    g = u // 2
                    pe.wait_ge(p_ready, b * PAIRS_OF_HEADS + u + 2)
                    if u == 1:
                        pe.wait_ge(so_taken, b + 2)
                    if u % 2 == 0:
                        pe.wait_ge(o_taken, b * HG + max(g, 1))
                        pe.wait_ge(o_taken, 1)
                    for i in range(2):
                        rows = slice(SLOT * (2 * (u % 2) + i), SLOT * (2 * (u % 2) + i) + SLOT)
                        at = slice(SLOT * (2 * u + i), SLOT * (2 * u + i) + SLOT)
                        nc.tensor.matmul(O[rows, g % 2, 0:T], V[:, 0, at], PT[:, u % 2, i, 0:T],
                                         start=True, stop=False, skip_group_check=True)
                        last = nc.tensor.matmul(O[rows, g % 2, P:T], V[:, 1, at], PT[:, u % 2, i, T:SPAN],
                                                start=False, stop=False, skip_group_check=True)
                    last.then_inc(av_done, 1)
                    if u % 2:
                        nc.tensor.matmul(O[:, g % 2, ODD:T], V_odd[:, g * P:g * P + P], p_odd[:, :],
                                         start=False, stop=True, skip_group_check=True).then_inc(o_ready, 1)
                pe.wait_ge(means_ready, b + 1)
                nc.tensor.matmul(proj[:, 1, 0:HG], avg[:, :], mv[:, :, 0], start=True, stop=True).then_inc(gm_ready, 1)
                pe.wait_ge(q_ready, b + 1)
                nc.tensor.matmul(proj[:, 1, 0:HG], avg[:, :], q[:, :], start=True, stop=True).then_inc(gv_ready, 1)

        @block.scalar
        def _(act):
            act.sem_inc(proj_taken, 1)
            act.sem_inc(o_taken, 1)
            act.sem_inc(so_taken, 1)
            act.sem_inc(stored, 16)
            with act.Fori(0, B) as b:
                for n in range(PROJ):
                    act.wait_ge(proj_ready, b * PROJ + n + 1)
                    if n < 2 * HG:
                        dst, src = (QT, KT)[n // HG][:, n % HG, :], proj[:, n % 2, 0:T]
                    elif n < PROJ - 1:
                        dst, src = V[:, n - 2 * HG, :], proj[:, n % 2, :]
                    else:
                        dst, src = v_odd[:, :], proj[:HEADS, n % 2, :]
                    nc.scalar.activation(dst, src, ACT.Copy).then_inc(proj_taken, 1)
                act.wait_ge(so_ready, b + 1)
                nc.scalar.activation(p_odd[:, :], O[:HEADS, 1, 511:512], ACT.Copy, scale=SCALE).then_inc(so_taken, 1)
                for g in range(HG):
                    act.wait_ge(o_ready, b * HG + g + 1)
                    nc.scalar.activation(cT[:, g, :], O[:, g % 2, 0:T], ACT.Copy).then_inc(o_taken, 1)
                act.wait_ge(affine_ready, b + 2)
                act.wait_ge(stored, b * 16 * SLOTS + 16)
                for g in range(HG):
                    last = nc.scalar.activation(cN[:, g, :], cT[:, g, :], ACT.Identity, bias=gbias[:, g:g + 1],
                                                scale=gscale[:, g:g + 1])
                last.then_inc(normed, 1)

        @block.vector
        def _(dve):
            v = nc.vector
            dve.wait_ge(const_in, 144)
            dve.sem_inc(p_ready, 1)
            dve.sem_inc(affine_ready, 1)
            with dve.Fori(0, B) as b:
                chain = Chain(dve, chained, 8, b)
                for u in range(PAIRS_OF_HEADS):
                    dve.wait_ge(s_ready, b * PAIRS_OF_HEADS + u + 2)
                    dve.wait_ge(av_done, b * PAIRS_OF_HEADS + max(u, 1))
                    v.tensor_tensor(PT[:, u % 2, :, :], S[:, u % 2, :, 0:SPAN], decay[:, 2 * u:2 * u + 2, :],
                                    ALU.mult).then_inc(p_ready, 1)
                for g in range(HG):
                    dve.wait_ge(o_taken, b * HG + g + 2)
                    last = v.bn_stats(stats[:, g, :], cT[:, g, :])
                chain.link_apart(last)
                for g in range(HG):
                    last = v.bn_aggr(mv[:, g, :], stats[:, g, :])
                last.then_inc(means_ready, 1)
                dve.wait_ge(gm_ready, b + 1)
                dve.wait_ge(means_ready, b + 1)
                v.tensor_copy(gmean[:, :], proj[:, 1, 0:HG])
                chain.link(v.tensor_tensor(d[:, :], mv[:, :, 0], proj[:, 1, 0:HG], ALU.subtract))
                chain.link(v.tensor_tensor(d[:, :], d[:, :], d[:, :], ALU.mult))
                v.tensor_tensor(q[:, :], d[:, :], mv[:, :, 1], ALU.add).then_inc(q_ready, 1)
                dve.wait_ge(gv_ready, b + 1)
                v.tensor_scalar(ve[:, :], proj[:, 1, 0:HG], LN_EPS, None, ALU.add).then_inc(ve_ready, 1)
                dve.wait_ge(rstd_ready, b + 1)
                chain.link(v.tensor_tensor(gscale[:, :], rstd[:, :], gnw[:, :], ALU.mult))
                chain.link(v.tensor_tensor(d[:, :], gmean[:, :], gscale[:, :], ALU.mult))
                chain.link(v.tensor_tensor(gbias[:, :], gnb[:, :], d[:, :], ALU.subtract))
                chain.link(v.tensor_copy(q[:, :], d[:, :]))
                dve.sem_inc(affine_ready, 1)
                chain.done()

        @block.gpsimd
        def _(pool):
            pool.wait_ge(const_in, 144)
            nc.gpsimd.memset(mh[:, :], -0.5).then_inc(const_made, 1)
            pool.wait_ge(const_made, 1)
            with pool.Fori(0, B) as b:
                pool.wait_ge(loaded, b * 16 + 16)
                pool.sem_inc(const_made, 1)
                nc.gpsimd.tensor_copy(odd_x[:, :, :], xT[:, :, ODD:T].broadcast_to([P, DC, HEADS])).then_inc(odd_copied, 1)
                pool.wait_ge(proj_taken, b * PROJ + 1 + 2 * HG)
                nc.gpsimd.tensor_tensor(K_odd[:, :, :], KT[:, :, ODD:T].broadcast_to([P, HG, HEADS]), sel[:, :, :],
                                        ALU.mult).then_inc(odd_ready, 1)
                pool.wait_ge(proj_taken, b * PROJ + 1 + PROJ)
                nc.gpsimd.tensor_tensor(V_odd[:, :], v_odd[:, :], own[:, :], ALU.mult).then_inc(odd_ready, 1)
                pool.wait_ge(ve_ready, b + 1)
                nc.gpsimd.tensor_tensor(rstd[:, :], ve[:, :], mh[:, :], ALU.pow).then_inc(rstd_ready, 1)


N_ODD = 4
NW = 8
ODD_LN = 5
LN_HEADS = {5: (0, 1, 2, 3, 4), 10: (5, 6, 8, 9), HEADS: (11, 13, 14, 15)}
PRODUCTS = {True: {h + 2: (h,) for h in range(HEADS)},
            False: {8: (0, 1), 9: (2, 3), 10: (4,), 11: (7,), 13: (5, 6), 14: (8, 9), 15: (10,), 16: (12,),
                    18: (11, 13), 19: (14, 15)}}
N_ONES = 11
ROOT = -0.5960716379833213
REST = 3 + 0.75 * ROOT ** 2
LINKS_A, LINKS_B = {True: 0, False: 1}, {True: 2, False: 2}
BF16 = mybir.dt.bfloat16
VC = HD + 1
BIG = -1e30


def attention(nc, causal, xT_in, wq, wk, wv, bq_in, bk_in, bv_in, own_in, sel_in, sums_in, share_in, ident_in,
              mask_in, aT_out):
    ctx = ExitStack()
    with ctx:
        r = Room(nc, ctx, "soft" if causal else "stable")
        wq_s, wk_s, wv_s = r.sb("wq", [P, DC, 512]), r.sb("wk", [P, DC, 512]), r.sb("wv", [P, DC, D])
        bq, bk = r.sb("bq", [P, HG]), r.sb("bk", [P, HG])
        bv = r.sb("bv", [P, HEADS, HD])
        own = r.sb("own", [HEADS, 512])
        sel = r.sb("sel", [P, HG, HEADS])
        ident, ident_b = r.sb("ident", [P, P]), r.sb("ident_b", [P, P], BF16)
        mask = r.sb("mask", [P, 2, P], BF16)
        sums_of = r.sb("sums_of", [P, HG, HEADS])
        share = r.sb("share", [HEADS, HG, P])
        sel_one = r.sb("sel_one", [P, HG, HEADS + 1])
        one_less, one_more = r.sb("one_less", [P, 1]), r.sb("one_more", [P, 1])
        xT = r.sb("xT", [P, DC, T])
        odd_x = r.sb("odd_x", [P, DC, HEADS])
        ones = r.sb("ones", [HEADS, P])
        QTs, KTs = r.sb("QT", [P, 2, HG, T]), r.sb("KT", [P, 2, HG, T])
        QHs = r.sb("QH", [P, 2, HG, SLOTS, T])
        Vs = r.sb("V", [P, 2, 2, HEADS, SLOT])
        v_odd, V_odds = r.sb("v_odd", [HEADS, HEADS, SLOT]), r.sb("V_odd", [HEADS, 2, 512])
        K_odds, Q_odds = r.sb("K_odd", [P, 2, HG, HEADS]), r.sb("Q_odd", [P, 2, HG, HEADS])
        negmax, negmax_T = r.sb("negmax", [P, 2, HEADS]), r.sb("negmax_T", [HEADS, 2, T])
        diag_odd = r.sb("diag_odd", [HEADS, 2, HEADS])
        U, Y, W = (r.sb(n, [P, NW, 512]) for n in ("U", "Y", "W"))
        w_oq, u_oq, y_oq = (r.sb(n, [P, 2 * HEADS]) for n in ("w_oq", "u_oq", "y_oq"))
        w_ok, u_ok, y_ok = (r.sb(n, [HEADS, T]) for n in ("w_ok", "u_ok", "y_ok"))
        oq, oq_sum = r.sb("oq", [P, HG, HEADS + 1]), r.sb("oq_sum", [P, HG])
        OT, inv = r.sb("OT", [P, HG, T]), r.sb("inv", [HEADS, T])
        aT = r.sb("aT", [P, HG, T])
        S = r.ps("S", [P, 2, 512])
        O = r.ps("O", [P, HG, 256])
        misc_a, misc_b, misc_c = r.ps("misc_a", [P, 2, 512]), r.ps("misc_b", [P, 1, 512]), r.ps("misc_c", [P, 1, 512])
        const_in, loaded, x_free, stored = r.sem("const_in"), r.sem("loaded"), r.sem("x_free"), r.sem("stored")
        ones_made, x_odd_ready, odd_ready, passed = r.sem("ones_made"), r.sem("x_odd"), r.sem("odd"), r.sem("passed")
        max_done, row_in, sp_passed = r.sem("max_done"), r.sem("row_in"), r.sem("sp_passed")
        s_ready, s_taken = r.sem("s_ready"), r.sem("s_taken")
        y_ready, t_ready, av_done = r.sem("y"), r.sem("t"), r.sem("av")
        maker = {h: "act" if causal or h in sum(LN_HEADS.values(), ()) else "dve" for h in range(HEADS)}
        made = {who: [h for h in range(HEADS) if maker[h] == who] for who in sorted(set(maker.values()))}
        w_ready = {who: r.sem(f"w_{who}") for who in made}
        ln_ready, ot_ready, ow_ready = r.sem("ln"), r.sem("ot"), r.sem("ow")
        o_taken, ot_copied = r.sem("o_taken"), r.sem("ot_copied")
        chain_a, chain_b, chain_c = r.sem("chain_a"), r.sem("chain_b"), r.sem("chain_c")

        def wait_weights(engine, g, h):
            who = maker[h % HEADS]
            engine.wait_ge(w_ready[who], (g + h // HEADS) * len(made[who]) + made[who].index(h % HEADS) + 1 + len(made[who]))

        order = [h for s in sorted(PRODUCTS[causal]) for h in PRODUCTS[causal][s]]

        def wait_multiplied(engine, g, h):
            engine.wait_ge(av_done, (g + h // HEADS) * HEADS + order.index(h % HEADS) + 1 + HEADS)

        nq = 1 if causal else T
        n_const = 12
        width = 3 * P if causal else 512

        class Track:

            def __init__(self, name, psum, banks, units):
                self.psum, self.banks, self.units = psum, banks, units
                self.at = {unit: n for n, (unit, _) in enumerate(units)}
                self.ready = r.sem(f"{name}_ready")
                self.taken = {who: r.sem(f"{name}_taken_{who}") for who in sorted({w for _, w in units})}
                self.per = {who: sum(w == who for _, w in units) for who in self.taken}

            def open(self, engines):
                for who, engine in engines.items():
                    if who in self.taken:
                        engine.sem_inc(self.taken[who], 1)

            def wait_taken(self, engine, b, unit):
                n = self.at[unit]
                who = self.units[n][1]
                engine.wait_ge(self.taken[who], b * self.per[who] + sum(w == who for _, w in self.units[:n + 1]) + 1)

            def bank(self, pe, b, unit):
                n = self.at[unit]
                if n >= self.banks:
                    self.wait_taken(pe, b, self.units[n - self.banks][0])
                else:
                    for who, sem in self.taken.items():
                        pe.wait_ge(sem, b * self.per[who] + 1)
                pe.sem_inc(passed, 1)
                return self.psum[:, n % self.banks, :]

            def full(self, engine, b, unit):
                engine.wait_ge(self.ready, b * len(self.units) + self.at[unit] + 1)
                return self.psum[:, self.at[unit] % self.banks, :]

        taker = "act" if causal else "dve"
        units = [(f"{what}{g}", "dve" if what == "q" else taker) for g in range(HG) for what in "qk"]
        units += [("max0", "dve"), ("max1", "dve")] + [(v, taker) for v in ("v0", "v1", "v_odd")]
        units += [(f"max{h}", "dve") for h in range(2, HEADS)]
        units += [] if causal else [("odd_key_max", "dve")]
        units += [("odd_query_max", "dve"), ("negmax_T", "dve")]
        ta = Track("ta", misc_a, 2, units)
        tb = Track("tb", misc_b, 1, [("odd_query", "act"), ("odd_key", "act"), ("odd_out", "dve")])
        tc = Track("tc", misc_c, 1, [("sums", "dve")] + [(f"share{hg}", "dve") for hg in range(HG)])
        shares = [["q0", "k0", "q1"], ["k1", "q2", "k2"], ["q3", "k3"], ["max0", "max1"], ["v0", "v1", "v_odd"]]
        shares += [[f"max{2 * u}", f"max{2 * u + 1}"] for u in range(1, HEADS // 2)]
        shares += [["odd_query_max"] if causal else ["odd_key_max", "odd_query_max"], ["negmax_T"], [], []]
        assert len(shares) == HEADS and [u for s in shares for u in s] == [u for u, _ in units]
        X_FREE, ODD_Q, ODD_K, ODD_W, ODD_OUT, COPY_OUT = 6, 1, 2, 3, 9, 3 if causal else 4
        PASS_OUT = {5: "sums"} | {7 + hg: f"share{hg}" for hg in range(HG)}

        def take_projected(engine, unit, b, p):
            src = ta.full(engine, b, unit)
            n = int(unit[-1]) if unit[-1].isdigit() else 0
            if unit[0] in "qk":
                dst, bias = (QTs, bq) if unit[0] == "q" else (KTs, bk)
                dst, src, bias = dst[:, p, n, :], src[:, 0:T], bias[:, n:n + 1]
                if unit[0] == "q":
                    nc.vector.scalar_tensor_tensor(
                        QHs[:, p, n, :, :], src.rearrange("p (o t) -> p o t", o=1).broadcast_to([P, SLOTS, T]), bias,
                        sel[:, n, n * SLOTS:(n + 1) * SLOTS].rearrange("p (j o) -> p j o", o=1).broadcast_to([P, SLOTS, T]),
                        ALU.add, ALU.mult)
                if causal and unit[0] == "k":
                    last = nc.scalar.activation(dst, src, ACT.Identity, bias=bias)
                else:
                    last = nc.vector.tensor_scalar(dst, src, bias, None, ALU.add)
            else:
                dst = v_odd[:, :, 0:HD] if unit == "v_odd" else Vs[:, p, n, :, 0:HD]
                src = src[:dst.shape[0], 0:D].rearrange("p (h e) -> p h e", e=HD)
                last = nc.scalar.activation(dst, src, ACT.Copy) if causal else nc.vector.tensor_copy(dst, src)
            last.then_inc(ta.taken[ta.units[ta.at[unit]][1]], 1)
        block = ctx.enter_context(nc.Block())

        def turns(engine, turn):
            turn(-1, "A", 1)
            turn(0, "AB", 0)
            with engine.Fori(0, B // 2 - 1) as n:
                turn(2 * n + 1, "ABC", 1)
                turn(2 * n + 2, "ABC", 0)
            turn(B - 1, "BC", 1)
            turn(B, "C", 0)

        @block.sync
        def _(sp):
            for dst, src in ((wq_s, wq), (wk_s, wk), (wv_s, wv)):
                sp.dma_start(dst[:, :, :], src.rearrange("(c p) n -> p c n", p=P)).then_inc(const_in, 16)
            for dst, src in ((bq, bq_in), (bk, bk_in), (ident, ident_in), (own, own_in)):
                sp.dma_start(dst[:, :], src).then_inc(const_in, 16)
            sp.dma_start(bv[:, :, :].rearrange("p h e -> p (h e)"), bv_in.broadcast_to([P, D])).then_inc(const_in, 16)
            for dst, src in ((sel, sel_in), (mask, mask_in), (sums_of, sums_in), (share, share_in)):
                sp.dma_start(dst[:, :, :], src).then_inc(const_in, 16)

            def turn(g, stages, q):
                if "A" in stages:
                    sp.wait_ge(x_free, g + 2)
                    sp.dma_start(xT[:, :, :], xT_in[:, bass.ds((g + 1) * T, T)].rearrange("(c p) t -> p c t", p=P))\
                      .then_inc(loaded, 16)
                if "C" in stages:
                    tc.wait_taken(sp, g - 1, f"share{HG - 1}")
                    dst = aT_out[:, bass.ds((g - 1) * T, T)].rearrange("(g s e) t -> s e g t", g=HG, s=SLOTS)
                    for s in range(SLOTS):
                        sp.dma_start(dst[s], aT[SLOT * s:SLOT * s + HD, :, :]).then_inc(stored, 16)
                if "A" in stages:
                    ta.wait_taken(sp, g + 1, "negmax_T")
                    for j in range(SLOTS):
                        row = SLOT * j + HD
                        sp.dma_start(QHs[row:row + 1, 1 - q, :, j, :], negmax_T[j:HEADS:SLOTS, 1 - q, :]).then_inc(row_in, 16)
            turns(sp, turn)
            sp.wait_ge(stored, 16 * (SLOTS * B + 1))

        @block.tensor
        def _(pe):
            mm = nc.tensor.matmul
            pe.wait_ge(const_in, 16 * n_const)
            pe.wait_ge(ones_made, N_ONES)
            pe.sem_inc(x_free, 1)
            pe.sem_inc(av_done, HEADS)

            def stand():
                pe.sem_inc(passed, 1)

            def turn(g, stages, q):
                p, b = 1 - q, g + 1

                def masked(out, side):
                    for at in (0, 2 * P):
                        last = mm(out[:, at:at + P], ident_b[:, :], mask[:, side, :], start=False, stop=True,
                                  skip_group_check=True)
                    return last

                def form(unit):
                    QT, KT = QTs[:, p], KTs[:, p]
                    if unit == "v_odd":
                        pe.wait_ge(x_odd_ready, b + 1)
                    elif unit in ("odd_key_max", "odd_query_max"):
                        pe.wait_ge(odd_ready, b * N_ODD + 3)
                    elif unit == "negmax_T":
                        pe.wait_ge(max_done, b + 1)
                    elif unit.startswith("max"):
                        ta.wait_taken(pe, b, "k3")
                    out = ta.bank(pe, b, unit)
                    n = int(unit[-1]) if unit[-1].isdigit() else 0
                    if unit[0] in "qk":
                        w = wq_s if unit[0] == "q" else wk_s
                        for c in range(DC):
                            last = mm(out[:, 0:T], w[:, c, n * P:n * P + P], xT[:, c, :], start=c == 0, stop=c == DC - 1)
                    elif unit == "v_odd":
                        for c in range(DC):
                            last = mm(out[:HEADS, 0:D], odd_x[:, c, :], wv_s[:, c, :], start=c == 0, stop=c == DC - 1)
                    elif unit[0] == "v":
                        for c in range(DC):
                            last = mm(out[:, 0:D], xT[:, c, n * P:n * P + P], wv_s[:, c, :], start=c == 0, stop=c == DC - 1)
                    elif unit.startswith("max"):
                        hg, j = divmod(int(unit[3:]), SLOTS)
                        QH = QHs[:, p, hg, j, :]
                        if causal:
                            mm(out[:, 0:P], QH[:, 0:P], KT[:, hg, 0:P], start=True, stop=True,
                               skip_group_check=True)
                            mm(out[:, P:3 * P], QH[:, P:2 * P], KT[:, hg, 0:2 * P], start=False, stop=True,
                               skip_group_check=True)
                            last = masked(out, 0)
                        else:
                            for k in range(2):
                                last = mm(out[:, k * D:k * D + D], QH[:, k * P:k * P + P], KT[:, hg, 0:D],
                                          start=True, stop=True)
                    elif unit == "odd_key_max":
                        for k in range(2):
                            for hg in range(HG):
                                last = mm(out[:, k * HEADS:k * HEADS + HEADS], QT[:, hg, k * P:k * P + P],
                                          K_odds[:, p, hg, :], start=hg == 0, stop=hg == HG - 1)
                    elif unit == "odd_query_max":
                        for hg in range(HG):
                            last = mm(out[:HEADS, 0:T], Q_odds[:, p, hg, :], KT[:, hg, :], start=hg == 0, stop=hg == HG - 1)
                    else:
                        for k in range(2):
                            last = nc.tensor.transpose(out[:HEADS, k * P:k * P + P], negmax[:, k, :], ident[:, :])
                    last.then_inc(ta.ready, 1)

                def scores(h):
                    KT = KTs[:, q]
                    if h == 0:
                        pe.wait_ge(row_in, (g + 1) * 16 * SLOTS)
                    pe.wait_ge(s_taken, g * HEADS + h + 1)
                    stand()
                    hg, j = divmod(h, SLOTS)
                    QH = QHs[:, q, hg, j, :]
                    out = S[:, h % 2, :]
                    if causal:
                        mm(out[:, 0:2 * P], KT[:, hg, 0:P], QH[:, 0:2 * P], start=True, stop=True,
                           skip_group_check=True)
                        mm(out[:, 2 * P:3 * P], KT[:, hg, P:2 * P], QH[:, P:2 * P], start=False, stop=True,
                           skip_group_check=True)
                        last = masked(out, 1)
                    else:
                        for k in range(2):
                            last = mm(out[:, k * D:k * D + D], KT[:, hg, k * P:k * P + P], QH[:, 0:D], start=True,
                                      stop=True)
                    last.then_inc(s_ready, 1)

                def products(g, h, q):
                    wait_weights(pe, g, h)
                    if h == order[0]:
                        pe.wait_ge(o_taken, g + 1)
                        pe.wait_ge(odd_ready, g * N_ODD + 3)
                        if not causal:
                            pe.wait_ge(ow_ready, g + 1)
                            stand()
                            for hg in range(HG):
                                mm(O[:, hg, :], V_odds[:, q, hg * P:hg * P + P], w_ok[:, 0:2 * P], start=hg % 2 == 0,
                                   stop=False, skip_group_check=True)
                    stand()
                    hg, rows = h // SLOTS, slice(SLOT * (h % SLOTS), SLOT * (h % SLOTS) + SLOT)
                    if causal:
                        mm(O[rows, hg, :], Vs[:, q, 0, h, :], W[:, h % NW, 0:2 * P], start=True, stop=False,
                           skip_group_check=True)
                        last = mm(O[rows, hg, P:2 * P], Vs[:, q, 1, h, :], W[:, h % NW, 2 * P:3 * P], start=False,
                                  stop=True, skip_group_check=True)
                    else:
                        for k in range(2):
                            last = mm(O[rows, hg, :], Vs[:, q, k, h, :], W[:, h % NW, k * D:k * D + D], start=False,
                                      stop=k == 1, skip_group_check=True)
                    last.then_inc(av_done, 1)

                for s in range(HEADS):
                    if "A" in stages:
                        if s == 0:
                            pe.wait_ge(loaded, b * 16 + 16)
                        for unit in shares[s]:
                            form(unit)
                        if s == X_FREE:
                            pe.wait_ge(ta.ready, b * len(ta.units) + ta.at["v_odd"] + 1)
                            pe.sem_inc(x_free, 1)
                    if "B" in stages:
                        scores(s)
                        if s == ODD_Q:
                            out = tb.bank(pe, g, "odd_query")
                            pe.wait_ge(odd_ready, g * N_ODD + 4)
                            stand()
                            for k in range(2):
                                for hg in range(HG):
                                    mm(out[:, k * HEADS:k * HEADS + HEADS], KTs[:, q, hg, k * P:k * P + P],
                                       Q_odds[:, q, hg, :], start=hg == 0, stop=False)
                                last = mm(out[:, k * HEADS:k * HEADS + HEADS], ones[:, :], diag_odd[:, q, :],
                                          start=False, stop=True)
                            last.then_inc(tb.ready, 1)
                        if s == ODD_K:
                            out = tb.bank(pe, g, "odd_key")
                            for hg in range(HG):
                                mm(out[:HEADS, 0:nq], K_odds[:, q, hg, :], QTs[:, q, hg, T - nq:T], start=hg == 0,
                                   stop=False)
                            last = mm(out[:HEADS, 0:nq], ident[:HEADS, :HEADS], negmax_T[:, q, T - nq:T], start=False,
                                      stop=True)
                            last.then_inc(tb.ready, 1)
                        if s == ODD_OUT:
                            out = tb.bank(pe, g, "odd_out")
                            pe.wait_ge(ow_ready, g + 1)
                            pe.wait_ge(odd_ready, g * N_ODD + 3)
                            stand()
                            for hg in range(HG):
                                at = hg * (HEADS + 1)
                                for k in range(2):
                                    mm(out[:, at:at + HEADS],
                                       Vs[:, q, k, hg * SLOTS:hg * SLOTS + SLOTS, :].rearrange("p h e -> p (h e)"),
                                       w_oq[:, k * HEADS:k * HEADS + HEADS], start=k == 0, stop=k == 1)
                                last = mm(out[:, at + HEADS:at + HEADS + 1], V_odds[:, q, hg * P:hg * P + P],
                                          w_ok[:, nq - 1:nq], start=True, stop=True)
                            last.then_inc(tb.ready, 1)
                        for h in PRODUCTS[causal].get(s, ()):
                            products(g, h, q)
                    if "C" in stages:
                        for h in PRODUCTS[causal].get(s + HEADS, ()):
                            products(g - 1, h, 1 - q)
                    if "C" in stages and s in PASS_OUT:
                        unit = PASS_OUT[s]
                        if unit == "sums":
                            out = tc.bank(pe, g - 1, unit)
                            pe.wait_ge(ot_copied, g)
                            stand()
                            for hg in range(HG):
                                last = mm(out[:HEADS, 0:T], sums_of[:, hg, :], OT[:, hg, :], start=hg == 0,
                                          stop=hg == HG - 1)
                        else:
                            out = tc.bank(pe, g - 1, unit)
                            last = mm(out[:, 0:T], share[:, int(unit[-1]), :], inv[:, :], start=True, stop=True)
                        last.then_inc(tc.ready, 1)
            turns(pe, turn)

        @block.scalar
        def _(act):
            A = nc.scalar.activation
            act.wait_ge(const_in, 16 * n_const)
            for track in (ta, tb, tc):
                track.open({"act": act})
            act.sem_inc(stored, 16)
            act.sem_inc(s_taken, 2)
            act.wait_ge(ones_made, N_ONES)
            for who, heads in made.items():
                act.sem_inc(w_ready[who], len(heads))
            act.sem_inc(ln_ready, len(LN_HEADS))

            def wait_logs(g, h):
                row = [h % HEADS in LN_HEADS[s] for s in sorted(LN_HEADS)].index(True)
                act.wait_ge(ln_ready, (g + h // HEADS) * len(LN_HEADS) + row + 1 + len(LN_HEADS))

            def turn(g, stages, q):
                p, b = 1 - q, g + 1

                def factors(u, y, x, rows):
                    A(u, x, ACT.Identity, scale=-SCALE, bias=one_less[:rows, :])
                    return A(y, x, ACT.Square, scale=-SCALE, bias=one_more[:rows, :])

                def logs(g, s):
                    for h in LN_HEADS.get(s, ()):
                        act.wait_ge(t_ready, g * HEADS + h + 1)
                        wait_multiplied(act, g, h - NW)
                        last = A(W[:, h % NW, :], U[:, h % NW, :], ACT.Ln)
                    if s == ODD_LN:
                        act.wait_ge(ot_ready, g + 1)
                        act.wait_ge(o_taken, g + 1)
                        A(w_oq[:, :], u_oq[:, :], ACT.Ln)
                        last = A(w_ok[:, :], u_ok[:, :], ACT.Ln)
                    if s in LN_HEADS:
                        last.then_inc(ln_ready, 1)

                def exponentials(g, s):
                    if s in LN_HEADS:
                        wait_logs(g, LN_HEADS[s][0])
                        for h in LN_HEADS[s]:
                            A(W[:, h % NW, :], W[:, h % NW, :], ACT.Exp, scale=-1.0).then_inc(w_ready["act"], 1)
                    if s == ODD_LN:
                        A(w_oq[:, :], w_oq[:, :], ACT.Exp, scale=-1.0)
                        A(w_ok[:, :], w_ok[:, :], ACT.Exp, scale=-1.0).then_inc(ow_ready, 1)

                for s in range(HEADS):
                    if "A" in stages:
                        for unit in shares[s]:
                            if ta.units[ta.at[unit]][1] == "act":
                                take_projected(act, unit, b, p)
                    if "B" in stages:
                        if s < HEADS:
                            n = g * HEADS + s
                            act.wait_ge(s_ready, n + 1)
                            at = s % NW
                            if causal:
                                wait_multiplied(act, g, s - NW)
                                A(W[:, at, 0:width], S[:, s % 2, 0:width], ACT.Exp, scale=SCALE).then_inc(w_ready["act"], 1)
                                wait_weights(act, g, s)
                                act.sem_inc(s_taken, 1)
                            else:
                                if maker[(s - NW) % HEADS] == "dve":
                                    wait_weights(act, g, s - NW)
                                else:
                                    wait_logs(g, s - NW)
                                factors(U[:, at, :], Y[:, at, :], S[:, s % 2, :], P).then_inc(y_ready, 1)
                                act.wait_ge(y_ready, n + 1)
                                act.sem_inc(s_taken, 1)
                        if not causal:
                            logs(g, s)
                            exponentials(g, s - 1)
                        if s == ODD_Q:
                            src = tb.full(act, g, "odd_query")[:, 0:2 * HEADS]
                            act.wait_ge(tb.taken["dve"], g + 1)
                            if causal:
                                A(w_oq[:, :], src, ACT.Exp, scale=SCALE).then_inc(tb.taken["act"], 1)
                            else:
                                factors(u_oq[:, :], y_oq[:, :], src, P).then_inc(tb.taken["act"], 1)
                        if s == ODD_K:
                            src = tb.full(act, g, "odd_key")[:HEADS, 0:nq]
                            if causal:
                                A(w_ok[:, 0:nq], src, ACT.Exp, scale=SCALE).then_inc(tb.taken["act"], 1)
                                tb.wait_taken(act, g, "odd_key")
                                act.sem_inc(ow_ready, 1)
                            else:
                                factors(u_ok[:, :], y_ok[:, :], src, HEADS).then_inc(tb.taken["act"], 1)
                    if "C" in stages and not causal:
                        logs(g - 1, s + HEADS)
                        exponentials(g - 1, s + HEADS - 1)
            turns(act, turn)

        @block.vector
        def _(dve):
            v = nc.vector
            dve.wait_ge(const_in, 16 * n_const)
            for track in (ta, tb, tc):
                track.open({"dve": dve})
            dve.sem_inc(o_taken, 1)

            def turn(g, stages, q):
                p, b = 1 - q, g + 1
                links_a, links_b = Chain(dve, chain_a, LINKS_A[causal], b), Chain(dve, chain_b, LINKS_B[causal], g)
                links_c = Chain(dve, chain_c, 1, g - 1)

                def take(unit):
                    if unit[0] in "qkv":
                        return take_projected(dve, unit, b, p)
                    taken = ta.taken["dve"]
                    src = ta.full(dve, b, unit)
                    if unit.startswith("max"):
                        h = int(unit[3:])
                        if causal:
                            v.tensor_reduce(negmax[:, 0, h:h + 1], src[:, 0:P], AX.X, ALU.max, negate=True)
                            last = v.tensor_reduce(negmax[:, 1, h:h + 1], src[:, P:3 * P], AX.X, ALU.max, negate=True)
                        else:
                            last = v.tensor_reduce(negmax[:, :, h], src[:, :].rearrange("p (k n) -> p k n", k=2), AX.X,
                                                   ALU.max, negate=True)
                        last.then_inc(taken, 1)
                        if causal and h == HEADS - 1:
                            ta.wait_taken(dve, b, unit)
                            dve.sem_inc(max_done, 1)
                    elif unit == "odd_key_max":
                        ta.wait_taken(dve, b, f"max{HEADS - 1}")
                        both = negmax[:, :, :].rearrange("p k h -> p (k h)")
                        links_a.link(v.scalar_tensor_tensor(both, src[:, 0:2 * HEADS], -1.0, both, ALU.mult, ALU.min))
                        dve.sem_inc(taken, 1)
                        dve.sem_inc(max_done, 1)
                    elif unit == "odd_query_max":
                        v.tensor_reduce(negmax_T[:, p, ODD:T], src[:HEADS, 0:T], AX.X, ALU.max, negate=True).then_inc(taken, 1)
                    else:
                        v.tensor_copy(negmax_T[:, p, 0:2 * P], src[:HEADS, 0:2 * P]).then_inc(taken, 1)

                def cubic(u, y):
                    return v.scalar_tensor_tensor(u, y, REST, u, ALU.add, ALU.mult)

                for s in range(HEADS):
                    if "C" in stages and s == COPY_OUT:
                        dve.wait_ge(tc.taken["dve"], (g - 1) * (HG + 1) + 1)
                        dve.wait_ge(av_done, (g - 1) * HEADS + 2 * HEADS)
                        v.tensor_copy(OT[:, :, 0:2 * P], O[:, :, :])
                        links_c.link(v.tensor_copy(OT[:, :, ODD:T], oq_sum[:, :].rearrange("p (g o) -> p g o", o=1)))
                        dve.sem_inc(o_taken, 1)
                        dve.sem_inc(ot_copied, 1)
                    if "A" in stages:
                        for unit in shares[s]:
                            if ta.units[ta.at[unit]][1] == "dve":
                                take(unit)
                    if "C" in stages and s in PASS_OUT:
                        unit = PASS_OUT[s]
                        src = tc.full(dve, g - 1, unit)
                        if unit == "sums":
                            v.reciprocal(inv[:, :], src[:HEADS, 0:T]).then_inc(tc.taken["dve"], 1)
                        else:
                            if unit == "share0":
                                dve.wait_ge(stored, (g - 1) * 16 * SLOTS + 16)
                            hg = int(unit[-1])
                            v.tensor_tensor(aT[:, hg, :], OT[:, hg, :], src[:, 0:T], ALU.mult).then_inc(tc.taken["dve"], 1)
                    if "B" not in stages:
                        continue
                    n = g * HEADS + s
                    if not causal:
                        if s < HEADS:
                            dve.wait_ge(y_ready, n + 1)
                            cubic(U[:, s % NW, :], Y[:, s % NW, :]).then_inc(t_ready, 1)
                        if 1 <= s <= HEADS:
                            if maker[s - 1] == "dve":
                                dve.wait_ge(t_ready, n)
                                wait_multiplied(dve, g, s - 1 - NW)
                                v.reciprocal(W[:, (s - 1) % NW, :], U[:, (s - 1) % NW, :]).then_inc(w_ready["dve"], 1)
                        if s == ODD_W:
                            tb.wait_taken(dve, g, "odd_key")
                            cubic(u_oq[:, :], y_oq[:, :])
                            cubic(u_ok[:, :], y_ok[:, :]).then_inc(ot_ready, 1)
                    if s == ODD_OUT:
                        src = tb.full(dve, g, "odd_out")[:, 0:HG * (HEADS + 1)]
                        links_b.link(v.tensor_tensor(oq[:, :, :], src.rearrange("p (g h) -> p g h", g=HG), sel_one[:, :, :],
                                                     ALU.mult))
                        dve.sem_inc(tb.taken["dve"], 1)
                        links_b.link(v.tensor_reduce(oq_sum[:, :], oq[:, :, :], AX.X, ALU.add))
                for stage, links in (("A", links_a), ("B", links_b), ("C", links_c)):
                    if stage in stages:
                        links.done()
            turns(dve, turn)

        @block.gpsimd
        def _(pool):
            g_ = nc.gpsimd
            g_.memset(Vs[:, :, :, :, :], 0.0).then_inc(ones_made, 1)
            g_.memset(v_odd[:, :, :], 0.0).then_inc(ones_made, 1)
            g_.memset(sel_one[:, :, :], 1.0).then_inc(ones_made, 1)
            pool.wait_ge(ones_made, 3)
            for q in range(2):
                g_.memset(Vs[:, q, :, :, HD:VC], 1.0).then_inc(ones_made, 1)
            g_.memset(v_odd[:, :, HD:VC], 1.0).then_inc(ones_made, 1)
            g_.memset(ones[:, :], 1.0).then_inc(ones_made, 1)
            g_.memset(one_less[:, :], 1.0 - ROOT).then_inc(ones_made, 1)
            g_.memset(one_more[:, :], 1.0 + ROOT / 2).then_inc(ones_made, 1)
            pool.wait_ge(const_in, 16 * n_const)
            g_.tensor_copy(ident_b[:, :], ident[:, :]).then_inc(ones_made, 1)
            g_.tensor_copy(sel_one[:, :, 0:HEADS], sel[:, :, :]).then_inc(ones_made, 1)
            pool.wait_ge(ones_made, N_ONES)

            def turn(g, stages, q):
                if "A" not in stages:
                    return
                p, b = 1 - q, g + 1

                def of_heads(dst, src):
                    return g_.tensor_tensor(dst[:, p, :, :], src[:, p, :, ODD:T].broadcast_to([P, HG, HEADS]), sel[:, :, :],
                                            ALU.mult)
                pool.wait_ge(loaded, b * 16 + 16)
                pool.sem_inc(ones_made, 1)
                g_.tensor_copy(odd_x[:, :, :], xT[:, :, ODD:T].broadcast_to([P, DC, HEADS])).then_inc(x_odd_ready, 1)
                ta.wait_taken(pool, b, "v_odd")
                of_heads(K_odds, KTs)
                of_heads(Q_odds, QTs).then_inc(odd_ready, 1)
                if causal:
                    for k in range(2):
                        g_.tensor_tensor(Vs[:, p, k, :, 0:HD], Vs[:, p, k, :, 0:HD], bv[:, :, :], ALU.add)
                    g_.tensor_tensor(v_odd[:, :, 0:HD], v_odd[:, :, 0:HD], bv[:HEADS, :, :], ALU.add)\
                        .then_inc(odd_ready, 1)
                else:
                    pool.sem_inc(odd_ready, 1)
                pool.wait_ge(odd_ready, b * N_ODD + 2)
                g_.tensor_tensor(V_odds[:, p, :], v_odd[:, :, :].rearrange("k h e -> k (h e)"), own[:, :], ALU.mult).then_inc(odd_ready, 1)
                ta.wait_taken(pool, b, "odd_query_max")
                g_.tensor_tensor(diag_odd[:, p, :], ident[:HEADS, :HEADS],
                                 negmax_T[:, p, ODD:T].broadcast_to([HEADS, HEADS]), ALU.mult).then_inc(odd_ready, 1)
            turns(pool, turn)


def enter_attention(nc, cT_in, h_in, wout_in, gamma_in, beta_in, ident_in, hx_out, x_out, xT_out):
    ctx = ExitStack()
    with ctx:
        r = Room(nc, ctx, "mid")
        ident, wout = r.sb("ident", [P, P]), r.sb("wout", [P, DC, D])
        gamma, beta = r.sb("gamma", [P, DC]), r.sb("beta", [P, DC])
        cT, h = r.sb("cT", [P, DC, GROUP]), r.sb("h", [P, 4, D])
        h1, x, hx, xn = (r.sb(n, [P, 4, D]) for n in ("h1", "x", "hx", "xn"))
        xt = r.sb("xt", [P, DC, GROUP])
        stats, mv = r.sb("stats", [P, 4, 6]), r.sb("mv", [P, 4, 2])
        ve, rstd, minus_half = r.sb("ve", [P, 4]), r.sb("rstd", [P, 4]), r.sb("mh", [P, 4])
        out_ps = r.ps("out", [P, 4, D])
        tp = r.ps("tp", [P, DC, GROUP])
        const_in, loaded, inputs_free = r.sem("const_in"), r.sem("loaded"), r.sem("inputs_free")
        const_made, chained, var_ready, rstd_ready = r.sem("const_made"), r.sem("chained"), r.sem("var"), r.sem("rstds")
        out_ready, out_taken = r.sem("out_ready"), r.sem("out_taken")
        xn_ready, tp_ready, xt_ready = r.sem("xn_ready"), r.sem("tp_ready"), r.sem("xt_ready")
        rows_ready, rows_stored, stored = r.sem("rows_ready"), r.sem("rows_stored"), r.sem("stored")
        block = ctx.enter_context(nc.Block())

        @block.sync
        def _(sp):
            sp.dma_start(ident[:, :], ident_in).then_inc(const_in, 16)
            sp.dma_start(wout[:, :, :], wout_in.rearrange("(c p) n -> p c n", p=P)).then_inc(const_in, 16)
            sp.dma_start(gamma[:, :], gamma_in).then_inc(const_in, 16)
            sp.dma_start(beta[:, :], beta_in).then_inc(const_in, 16)

            def step(t0, g, tiles, rows):
                sp.wait_ge(inputs_free, g + 1)
                sp.wait_ge(out_ready, g + 1)
                sp.dma_start(cT[:, :, 0:tiles * rows], cT_in[:, bass.ds(t0, tiles * rows)]
                             .rearrange("(c p) t -> p c t", p=P)).then_inc(loaded, 16)
                sp.dma_start(h[:rows, 0:tiles, :], tokens(h_in, t0, tiles, rows)).then_inc(loaded, 16)
            groups(sp, step)

        @block.tensor
        def _(pe):
            pe.sem_inc(tp_ready, 1)
            pe.sem_inc(out_ready, 1)
            pe.wait_ge(const_in, 64)

            def step(t0, g, tiles, rows):
                pe.wait_ge(loaded, g * 32 + 32)
                pe.wait_ge(out_taken, g + 1)
                for j in range(tiles):
                    for c in range(DC):
                        last = nc.tensor.matmul(out_ps[:rows, j, :], cT[:, c, j * P:j * P + rows], wout[:, c, :],
                                                start=c == 0, stop=c == DC - 1)
                last.then_inc(out_ready, 1)
                pe.wait_ge(xt_ready, g + 1)
                pe.wait_ge(xn_ready, g + 1)
                transposed(nc, tp, xn, ident, tiles, rows).then_inc(tp_ready, 1)
            groups(pe, step)

        @block.vector
        def _(dve):
            v = nc.vector
            dve.sem_inc(inputs_free, 1)
            dve.sem_inc(out_taken, 1)

            def step(t0, g, tiles, rows):
                chain = Chain(dve, chained, 8, g)
                dve.wait_ge(out_ready, g + 2)
                dve.wait_ge(rows_stored, g * 32 + 32)
                v.tensor_tensor(h1[:rows, 0:tiles, :], h[:rows, 0:tiles, :], out_ps[:rows, 0:tiles, :], ALU.add)\
                    .then_inc(out_taken, 1)
                dve.wait_ge(out_taken, g + 2)
                dve.sem_inc(inputs_free, 1)
                statistics(v, chain, h1, stats, mv, ve, tiles, rows, LN_EPS).then_inc(var_ready, 1)
                dve.wait_ge(rstd_ready, 2 * g + 1)
                dve.wait_ge(var_ready, 2 * g + 1)
                chain.link_apart(normalise(v, h1, x, mv, rstd, tiles, rows))
                statistics(v, chain, x, stats, mv, ve, tiles, rows, LN_EPS).then_inc(var_ready, 1)
                v.tensor_tensor(hx[:rows, 0:tiles, :], h1[:rows, 0:tiles, :], x[:rows, 0:tiles, :], ALU.add)\
                    .then_inc(rows_ready, 1)
                dve.wait_ge(rstd_ready, 2 * g + 2)
                dve.wait_ge(var_ready, 2 * g + 2)
                dve.wait_ge(tp_ready, g + 1)
                normalise(v, x, xn, mv, rstd, tiles, rows).then_inc(xn_ready, 1)
                chain.done()
            groups(dve, step)

        @block.gpsimd
        def _(pool):
            nc.gpsimd.memset(minus_half[:, :], -0.5).then_inc(const_made, 1)
            pool.wait_ge(const_made, 1)

            def step(t0, g, tiles, rows):
                for n in range(2):
                    pool.wait_ge(var_ready, 2 * g + n + 1)
                    nc.gpsimd.tensor_tensor(rstd[:rows, 0:tiles], ve[:rows, 0:tiles], minus_half[:rows, 0:tiles],
                                            ALU.pow).then_inc(rstd_ready, 1)
            groups(pool, step)

        @block.scalar
        def _(act):
            act.sem_inc(xt_ready, 1)
            act.sem_inc(stored, 16)
            act.sem_inc(rows_stored, 32)
            act.wait_ge(const_in, 64)

            def step(t0, g, tiles, rows):
                act.wait_ge(stored, g * 16 + 16)
                act.wait_ge(tp_ready, g + 2)
                n = tiles * rows
                for c in range(DC):
                    last = nc.scalar.activation(xt[:, c, 0:n], tp[:, c, 0:n], ACT.Identity, bias=beta[:, c:c + 1],
                                                scale=gamma[:, c:c + 1])
                last.then_inc(xt_ready, 1)
                act.wait_ge(xt_ready, g + 2)
                act.dma_start(xT_out[:, bass.ds(t0, n)].rearrange("(c p) t -> p c t", p=P),
                              xt[:, :, 0:n]).then_inc(stored, 16)
                act.wait_ge(rows_ready, g + 1)
                act.dma_start(tokens(hx_out, t0, tiles, rows), hx[:rows, 0:tiles, :]).then_inc(rows_stored, 16)
                act.dma_start(tokens(x_out, t0, tiles, rows), x[:rows, 0:tiles, :]).then_inc(rows_stored, 16)
            groups(act, step)
            act.wait_ge(rows_stored, 32 * (NGROUPS + 2))
            act.wait_ge(stored, 16 * (NGROUPS + 2))


EXPERTS, HIDDEN = 8, 4 * D
MOE_LINKS = 20
HB = HIDDEN // P


def experts(nc, aT_in, x_in, hx_in, wp_in, bp_in, gamma_in, beta_in, gate_w_in, gate_b_in, w1_in, b1_in, w2_in, b2_in,
            ident_in, h_out, xT_out):
    ctx = ExitStack()
    with ctx:
        r = Room(nc, ctx, "moe")
        ident, wp, bp = r.sb("ident", [P, P]), r.sb("wp", [P, DC, D]), r.sb("bp", [P, D])
        gamma, beta = r.sb("gamma", [P, DC]), r.sb("beta", [P, DC])
        gate_w, gate_b = r.sb("gate_w", [P, DC, EXPERTS]), r.sb("gate_b", [P, EXPERTS])
        w1, w2 = r.sb("w1", [P, EXPERTS, DC, HIDDEN]), r.sb("w2", [P, EXPERTS, HB, D])
        b1, b2 = r.sb("b1", [P, EXPERTS, HB]), r.sb("b2", [EXPERTS, D])
        aT = r.sb("aT", [P, DC, GROUP])
        x, acc = r.sb("x", [P, 4, D]), r.sb("acc", [P, 4, D])
        xn = r.sb("xn", [P, 4, D])
        mT = r.sb("mT", [P, DC, GROUP])
        mid = r.sb("mid", [P, 2, HB, GROUP])
        xt = aT
        stats, mv = r.sb("stats", [P, 4, 6]), r.sb("mv", [P, 4, 2])
        ve, rstd, minus_half = r.sb("ve", [P, 4]), r.sb("rstd", [P, 4]), r.sb("mh", [P, 4])
        logits, top, index = r.sb("logits", [P, 4, EXPERTS]), r.sb("top", [P, 4, 8]), r.sb("index", [P, 4, 8], U32)
        index_f, iota = r.sb("index_f", [P, 4, 8]), r.sb("iota", [P, EXPERTS])
        gap, second, total = r.sb("gap", [P, 4]), r.sb("second", [P, 4]), r.sb("total", [P, 4])
        wa, wb, one_hot, w_full = r.sb("wa", [P, 4]), r.sb("wb", [P, 4]), r.sb("one_hot", [P, 4, EXPERTS]), r.sb("w_full", [P, 4, EXPERTS])
        wT = r.sb("wT", [EXPERTS, GROUP])
        hid = r.ps("hid", [P, 2, GROUP])
        y = r.ps("y", [P, 2, 2, 2, D])
        tp = r.ps("tp", [P, DC, GROUP])
        const_in, const_made, loaded, loaded_hx = r.sem("const_in"), r.sem("const_made"), r.sem("loaded"), r.sem("loaded_hx")
        x_free, acc_free, proj_ready, proj_taken = r.sem("x_free"), r.sem("acc_free"), r.sem("proj_ready"), r.sem("proj_taken")
        chained, var_ready, rstd_ready, xn_ready = r.sem("chained"), r.sem("var"), r.sem("rstds"), r.sem("xn")
        tp_ready, tp_taken, gate_ready, gap_ready, exp_ready = (r.sem(n) for n in ("tp_ready", "tp_taken", "gate", "gap", "exp"))
        w_ready, wT_ready, wT_taken = r.sem("w_ready"), r.sem("wT_ready"), r.sem("wT_taken")
        hid_ready, mid_ready, y_ready, y_taken = r.sem("hid_ready"), r.sem("mid_ready"), r.sem("y_ready"), r.sem("y_taken")
        h_stored, stored, passed = r.sem("h_stored"), r.sem("stored"), r.sem("passed")
        h_ready, sp_passed = r.sem("h_ready"), r.sem("sp_passed")
        YU = 2 * (EXPERTS + 1)
        block = ctx.enter_context(nc.Block())

        @block.sync
        def _(sp):
            for dst, src in ((wp, wp_in), (gate_w, gate_w_in)):
                sp.dma_start(dst[:, :, :], src.rearrange("(c p) n -> p c n", p=P)).then_inc(const_in, 16)
            for dst, src in ((ident, ident_in), (gamma, gamma_in), (beta, beta_in), (b2, b2_in)):
                sp.dma_start(dst[:, :], src).then_inc(const_in, 16)
            sp.dma_start(bp[:, :], bp_in.broadcast_to([P, D])).then_inc(const_in, 16)
            sp.dma_start(gate_b[:, :], gate_b_in.broadcast_to([P, EXPERTS])).then_inc(const_in, 16)
            sp.dma_start(b1[:, :, :], b1_in).then_inc(const_in, 16)
            for e in range(EXPERTS):
                sp.dma_start(w1[:, e, :, :], w1_in[:, e, :, :]).then_inc(const_in, 16)
                sp.dma_start(w2[:, e, :, :], w2_in[:, e, :, :]).then_inc(const_in, 16)

            def step(t0, g, tiles, rows):
                n = tiles * rows
                sp.wait_ge(stored, g * 16 + 16)
                sp.sem_inc(sp_passed, 1)
                sp.wait_ge(x_free, g + 1)
                sp.sem_inc(sp_passed, 1)
                sp.dma_start(aT[:, :, 0:n], aT_in[:, bass.ds(t0, n)].rearrange("(c p) t -> p c t", p=P)).then_inc(loaded, 16)
                sp.dma_start(x[:rows, 0:tiles, :], tokens(x_in, t0, tiles, rows)).then_inc(loaded, 16)
                sp.wait_ge(h_stored, g * 16 + 16)
                sp.sem_inc(sp_passed, 1)
                sp.dma_start(acc[:rows, 0:tiles, :], tokens(hx_in, t0, tiles, rows)).then_inc(loaded_hx, 16)
            groups(sp, step)

        @block.tensor
        def _(pe):
            mm = nc.tensor.matmul
            pe.sem_inc(y_ready, 2)
            pe.wait_ge(const_in, 16 * (9 + 2 * EXPERTS))

            def step(t0, g, tiles, rows):
                n = tiles * rows
                pairs = (tiles + 1) // 2

                def stand():
                    pe.sem_inc(passed, 1)

                pe.wait_ge(loaded, g * 32 + 32)
                pe.wait_ge(tp_taken, 3 * g + 1)
                for j in range(tiles):
                    for c in range(DC):
                        last = mm(tp[:rows, j // 2, (j % 2) * D:(j % 2) * D + D], aT[:, c, j * P:j * P + rows], wp[:, c, :],
                                  start=c == 0, stop=c == DC - 1)
                last.then_inc(proj_ready, 1)
                pe.wait_ge(proj_taken, g + 1)
                pe.wait_ge(xn_ready, 2 * g + 1)
                transposed(nc, tp, xn, ident, tiles, rows).then_inc(tp_ready, 1)
                pe.wait_ge(tp_taken, 3 * g + 2)
                stand()
                for j in range(tiles):
                    for c in range(DC):
                        last = mm(tp[:rows, 0, j * EXPERTS:(j + 1) * EXPERTS], mT[:, c, j * P:j * P + rows],
                                  gate_w[:, c, :], start=c == 0, stop=c == DC - 1)
                last.then_inc(gate_ready, 1)

                def hidden(e, hb):
                    u = e * HB + hb
                    pe.wait_ge(mid_ready, g * EXPERTS * HB + u + 1)
                    for c in range(DC):
                        last = mm(hid[:, u % 2, 0:n], w1[:, e, c, hb * P:hb * P + P], mT[:, c, 0:n], start=c == 0,
                                  stop=c == DC - 1)
                    last.then_inc(hid_ready, 1)

                def out(e):
                    pe.wait_ge(mid_ready, g * EXPERTS * HB + (e + 1) * HB + 2)
                    for k in range(pairs):
                        pe.wait_ge(y_taken, g * YU + 4 + max(0, pairs * (e - 1) + k + 1))
                        for j in range(2 * k, min(2 * k + 2, tiles)):
                            for hb in range(HB):
                                last = mm(y[:rows, (e + 1) % 2, k, j % 2, :], mid[:, e % 2, hb, j * P:j * P + rows],
                                          w2[:, e, hb, :], start=hb == 0, stop=hb == HB - 1)
                        last.then_inc(y_ready, 1)

                for hb in range(HB):
                    hidden(0, hb)
                pe.wait_ge(w_ready, g + 1)
                stand()
                for j in range(tiles):
                    last = nc.tensor.transpose(tp[:EXPERTS, 1, j * P:j * P + rows], w_full[:rows, j, :], ident[:rows, :rows])
                last.then_inc(wT_ready, 1)
                pe.wait_ge(wT_taken, g + 1)
                pe.wait_ge(y_taken, g * YU + 4)
                for k in range(pairs):
                    stand()
                    for j in range(2 * k, min(2 * k + 2, tiles)):
                        last = mm(y[:rows, 0, k, j % 2, :], wT[:, j * P:j * P + rows], b2[:, :], start=True, stop=True)
                    last.then_inc(y_ready, 1)
                for e in range(EXPERTS):
                    if e + 1 < EXPERTS:
                        for hb in range(HB):
                            hidden(e + 1, hb)
                    out(e)
                pe.wait_ge(xn_ready, 2 * g + 2)
                transposed(nc, tp, xn, ident, tiles, rows).then_inc(tp_ready, 1)
            groups(pe, step)

        @block.scalar
        def _(act):
            A = nc.scalar.activation
            act.sem_inc(tp_taken, 1)
            act.sem_inc(mid_ready, 2)
            act.sem_inc(stored, 16)
            act.wait_ge(const_in, 16 * (9 + 2 * EXPERTS))

            def step(t0, g, tiles, rows):
                n = tiles * rows
                pairs = (tiles + 1) // 2
                act.wait_ge(tp_ready, 2 * g + 1)
                for c in range(DC):
                    last = A(mT[:, c, 0:n], tp[:, c, 0:n], ACT.Identity, bias=beta[:, c:c + 1], scale=gamma[:, c:c + 1])
                last.then_inc(tp_taken, 1)
                act.wait_ge(gap_ready, g + 1)
                A(second[:rows, 0:tiles], gap[:rows, 0:tiles], ACT.Exp).then_inc(exp_ready, 1)
                for e in range(EXPERTS):
                    act.wait_ge(y_ready, g * YU + 2 + (pairs * e if e >= 2 else 0))
                    for hb in range(HB):
                        u = e * HB + hb
                        act.wait_ge(hid_ready, g * EXPERTS * HB + u + 1)
                        A(mid[:, e % 2, hb, 0:n], hid[:, u % 2, 0:n], ACT.Gelu, bias=b1[:, e, hb:hb + 1])\
                            .then_inc(mid_ready, 1)
                    if e == 0:
                        act.wait_ge(wT_ready, g + 1)
                        A(wT[:, 0:n], tp[:EXPERTS, 1, 0:n], ACT.Copy).then_inc(wT_taken, 1)
                act.wait_ge(tp_ready, 2 * g + 2)
                A(xt[:, :, 0:n], tp[:, :, 0:n], ACT.Copy).then_inc(tp_taken, 1)
                act.sem_inc(tp_taken, 1)
                act.wait_ge(tp_taken, 3 * g + 4)
                act.dma_start(xT_out[:, bass.ds(t0, n)].rearrange("(c p) t -> p c t", p=P),
                              xt[:, :, 0:n]).then_inc(stored, 16)
                act.wait_ge(h_ready, g + 1)
                act.dma_start(tokens(h_out, t0, tiles, rows), acc[:rows, 0:tiles, :]).then_inc(h_stored, 16)
            groups(act, step)
            act.wait_ge(stored, 16 * (NGROUPS + 2))
            act.wait_ge(h_stored, 16 * (NGROUPS + 2))

        @block.vector
        def _(dve):
            v = nc.vector
            dve.sem_inc(x_free, 1)
            dve.sem_inc(y_taken, 4)
            dve.wait_ge(const_made, 3)
            dve.wait_ge(const_in, 16 * (9 + 2 * EXPERTS))

            def step(t0, g, tiles, rows):
                chain = Chain(dve, chained, MOE_LINKS, g)
                link = chain.link
                t_ = slice(0, tiles)
                pairs = (tiles + 1) // 2
                dve.wait_ge(loaded_hx, g * 16 + 16)
                dve.wait_ge(proj_ready, g + 1)
                proj = tp[:rows, :, :].rearrange("p c (k d) -> p (c k) d", k=2)[:, t_, :]
                bias = bp[:rows, :].rearrange("p (a d) -> p a d", a=1).broadcast_to([rows, tiles, D])
                link(v.tensor_tensor(xn[:rows, t_, :], proj, bias, ALU.add))
                dve.sem_inc(proj_taken, 1)
                v.tensor_tensor(acc[:rows, t_, :], acc[:rows, t_, :], xn[:rows, t_, :], ALU.add)
                chain.link_apart(v.tensor_tensor(x[:rows, t_, :], x[:rows, t_, :], xn[:rows, t_, :], ALU.add))
                statistics(v, chain, x, stats, mv, ve, tiles, rows, LN_EPS).then_inc(var_ready, 1)
                dve.wait_ge(rstd_ready, 2 * g + 1)
                normalise(v, x, xn, mv, rstd, tiles, rows).then_inc(xn_ready, 1)
                dve.wait_ge(xn_ready, 2 * g + 1)
                dve.sem_inc(x_free, 1)
                dve.wait_ge(gate_ready, g + 1)
                bias = gate_b[:rows, :].rearrange("p (a d) -> p a d", a=1).broadcast_to([rows, tiles, EXPERTS])
                chain.link_apart(v.tensor_tensor(logits[:rows, t_, :], tp[:rows, 0, 0:tiles * EXPERTS]
                                                 .rearrange("p (j e) -> p j e", e=EXPERTS), bias, ALU.add))
                for j in range(tiles):
                    last = v.max(top[:rows, j, :], logits[:rows, j, :])
                chain.link_apart(last)
                for j in range(tiles):
                    last = v.max_index(index[:rows, j, :], top[:rows, j, :], logits[:rows, j, :])
                v.tensor_tensor(gap[:rows, t_], top[:rows, t_, 1], top[:rows, t_, 0], ALU.subtract).then_inc(gap_ready, 1)
                link(last)
                link(v.tensor_copy(index_f[:rows, t_, :], index[:rows, t_, :]))
                dve.wait_ge(exp_ready, g + 1)
                link(v.tensor_scalar(total[:rows, t_], second[:rows, t_], 1.0, None, ALU.add))
                link(v.reciprocal(wa[:rows, t_], total[:rows, t_]))
                link(v.tensor_tensor(wb[:rows, t_], wa[:rows, t_], second[:rows, t_], ALU.mult))
                for j in range(tiles):
                    last = v.tensor_scalar(one_hot[:rows, j, :], iota[:rows, :], index_f[:rows, j, 1:2], wb[:rows, j:j + 1],
                                           ALU.is_equal, ALU.mult)
                    v.tensor_scalar(w_full[:rows, j, :], iota[:rows, :], index_f[:rows, j, 0:1], wa[:rows, j:j + 1],
                                    ALU.is_equal, ALU.mult)
                link(v.tensor_copy(total[:rows, t_], wb[:rows, t_]))
                link(v.tensor_tensor(w_full[:rows, t_, :], w_full[:rows, t_, :], one_hot[:rows, t_, :], ALU.add))
                dve.sem_inc(w_ready, 1)
                for e in range(-1, EXPERTS):
                    for k in range(pairs):
                        dve.wait_ge(y_ready, g * YU + 2 + pairs * (e + 1) + k + 1)
                        for j in range(2 * k, min(2 * k + 2, tiles)):
                            src = y[:rows, (e + 1) % 2, k, j % 2, :]
                            if e < 0:
                                last = v.tensor_tensor(acc[:rows, j, :], acc[:rows, j, :], src, ALU.add)
                            else:
                                last = v.scalar_tensor_tensor(acc[:rows, j, :], src, w_full[:rows, j, e:e + 1],
                                                              acc[:rows, j, :], ALU.mult, ALU.add)
                        last.then_inc(y_taken, 1)
                        dve.wait_ge(y_taken, g * YU + 4 + pairs * (e + 1) + k + 1)
                dve.sem_inc(h_ready, 1)
                statistics(v, chain, acc, stats, mv, ve, tiles, rows, LN_EPS).then_inc(var_ready, 1)
                dve.wait_ge(rstd_ready, 2 * g + 2)
                normalise(v, acc, xn, mv, rstd, tiles, rows).then_inc(xn_ready, 1)
                chain.done()
            groups(dve, step)

        @block.gpsimd
        def _(pool):
            nc.gpsimd.memset(minus_half[:, :], -0.5).then_inc(const_made, 1)
            nc.gpsimd.iota(iota[:, :], [[1, EXPERTS]], base=0, channel_multiplier=0, allow_small_or_imprecise_dtypes=True)\
                .then_inc(const_made, 1)
            pool.wait_ge(const_made, 2)
            pool.sem_inc(const_made, 1)
            pool.sem_inc(h_stored, 16)

            def step(t0, g, tiles, rows):
                for n in range(2):
                    pool.wait_ge(var_ready, 2 * g + n + 1)
                    nc.gpsimd.tensor_tensor(rstd[:rows, 0:tiles], ve[:rows, 0:tiles], minus_half[:rows, 0:tiles],
                                            ALU.pow).then_inc(rstd_ready, 1)
            groups(pool, step)

PH, PK = 8, 8
NKEYS = 64
JB = NKEYS // 2
SUB = 16
EG = 2 * P
EGROUPS = NTOK // EG
LAG = 5
NHID = 8
ROUTE_LINKS = 61
PE_AT = {"proj": 0, "tp": 6, "sims": (7, 13), "fields": (17, 25), "scatter": ((21, 24, 26, 27), (29, 30, 31, 33))}
DVE_AT = {"h": 1, "x": 3, "xn": 4, "pick": ((8, 9, 10, 11, 12, 13, 14), (15, 16, 17, 19, 20, 22, 22)),
          "one_hot": ((18, 21, 23, 24), (26, 27, 28, 30))}


def product_keys(nc, aT_in, h_in, wout_in, bout_in, norm_w_in, w_q_in, keys_in, down_in, up_in, ident_in, h_out):
    ctx = ExitStack()
    with ctx:
        r = Room(nc, ctx, "peer")
        ident, wout, bout = r.sb("ident", [P, P]), r.sb("wout", [P, DC, D]), r.sb("bout", [P, D])
        norm_w = r.sb("norm_w", [P, DC])
        down, up = r.sb("down", [P, DC, JB, P]), r.sb("up", [P, JB, D])
        simw = r.sb("simw", [P, DC, 2 * PH * NKEYS])
        G = r.sb("G", [P, 2, JB, EG])
        G_flat = G[:, :, :, :].rearrange("p g a b -> p (g a b)")
        w_q = G_flat[:, 0:16 * D].rearrange("p (a b) -> p a b", a=16)
        keys = G_flat[:, 16 * D:16 * D + 16 * NKEYS].rearrange("p (a b) -> p a b", a=16)
        hin = r.sb("hin", [P, 2, D])
        aT, xnT = r.sb("aT", [P, DC, EG]), r.sb("xnT", [P, 2, DC, EG])
        h, x = r.sb("h", [P, 2, 2, D]), r.sb("x", [P, 2, D])
        stats, mv = r.sb("stats", [P, 2, 6]), r.sb("mv", [P, 2, 2])
        ve, rstd, minus_half, m2 = (r.sb(n, [P, 2]) for n in ("ve", "rstd", "mh", "m2"))
        best, best_i = r.sb("best", [P, 2 * PH, 8]), r.sb("best_i", [P, 2 * PH, 8], U32)
        best_if = r.sb("best_if", [P, 2 * PH, 8])
        sums = r.sb("sums", [P, PH, 8, 8])
        fs, pk = r.sb("fs", [P, PH, PK]), r.sb("pk", [P, PH * PK], U32)
        pk_u, pk_f = r.sb("pk_u", [P, 2, PH * PK], U32), r.sb("pk_f", [P, 2, PH * PK])
        picked = r.sb("picked", [P, PH, PK, 8])
        j_f, j_u, j_parts, par = r.sb("j_f", [P, 64]), r.sb("j_u", [P, 64], U32), r.sb("j_parts", [P, 2, 64], U32), r.sb("par", [P, 64])
        fields = r.sb("fields", [P, 4, 64])
        FT = r.sb("FT", [P, 2, 4, 64])
        iota = r.sb("iota", [P, NKEYS])
        eq = r.sb("eq", [P, 2, SUB, NKEYS])
        iota_j = r.sb("iota_j", [P, 2 * JB])
        one_i, one_j = r.sb("one_i", [P, 2, SUB, 2, NKEYS]), r.sb("one_j", [P, 2, SUB, 2 * JB])
        hid = r.sb("hid", [P, NHID, EG])
        route = r.ps("route", [P, 2, 512])
        turned = r.ps("turned", [P, 512])
        work = r.ps("work", [P, 2, 512])
        total = r.ps("total", [P, 2, D])
        scat = r.ps("scat", [P, 2, SUB // 2, 2 * JB])
        const_in, const_made, loaded, a_free, h_stored = (r.sem(n) for n in ("const_in", "const_made", "loaded", "a_free", "h_stored"))
        simw_ready, simw_taken = r.sem("simw_ready"), r.sem("simw_taken")
        proj_ready, proj_taken, chained, var_ready, rstd_ready = (r.sem(n) for n in ("proj", "proj_taken", "chained", "var", "rstds"))
        xn_ready, tp_ready, tp_taken = r.sem("xn"), r.sem("tp"), r.sem("tp_taken")
        sims_ready, sims_taken, fields_ready, f_ready, f_taken = (r.sem(n) for n in ("sims", "sims_taken", "fields_r", "f", "f_taken"))
        one_ready, eq_ready, odd_ready, scat_ready, scat_taken = r.sem("one"), r.sem("eq_r"), r.sem("odd"), r.sem("scat_r"), r.sem("scat_taken")
        hid_ready, gelu_ready, gated, up_done = r.sem("hid_r"), r.sem("gelu"), r.sem("gated"), r.sem("up_done")
        out_taken, passed, sp_passed = r.sem("out_taken"), r.sem("passed"), r.sem("sp_passed")
        h_free = r.sem("h_free")
        dve_passed, pool_passed = r.sem("dve_passed"), r.sem("pool_passed")
        N_CONST = 9
        block = ctx.enter_context(nc.Block())

        def shape_of(is_tail):
            return (1, TAIL, 1, TAIL) if is_tail else (2, P, 2, P // 2)

        def turns(engine, turn):
            turn(-1, None, "full", 1)
            with engine.Fori(0, EGROUPS - 2, 2) as g:
                turn(g, "full", "full", 0)
                turn(g + 1, "full", "full", 1)
            turn(EGROUPS - 2, "full", "full", 0)
            turn(EGROUPS - 1, "full", "tail", 1)
            turn(EGROUPS, "tail", None, 0)

        @block.sync
        def _(sp):
            sp.dma_start(w_q, w_q_in).then_inc(const_in, 16)
            sp.dma_start(keys, keys_in).then_inc(const_in, 16)
            sp.dma_start(wout[:, :, :], wout_in.rearrange("(c p) n -> p c n", p=P)).then_inc(const_in, 16)
            sp.dma_start(ident[:, :], ident_in).then_inc(const_in, 16)
            sp.dma_start(bout[:, :], bout_in.broadcast_to([P, D])).then_inc(const_in, 16)
            sp.dma_start(norm_w[:, :], norm_w_in).then_inc(const_in, 16)
            for c in range(DC):
                sp.dma_start(down[:, c, :, :], down_in[:, c, :, :]).then_inc(const_in, 16)
            sp.dma_start(up[:, :, :], up_in).then_inc(const_in, 16)

            def turn(g, blocks, routing, q):
                if routing is None:
                    return
                tiles, rows, _, _ = shape_of(routing == "tail")
                ga, n = g + 1, tiles * rows
                sp.wait_ge(a_free, ga + 1)
                sp.sem_inc(sp_passed, 1)
                sp.wait_ge(h_free, ga + 1)
                sp.sem_inc(sp_passed, 1)
                sp.dma_start(aT[:, :, 0:n], aT_in[:, bass.ds(ga * EG, n)].rearrange("(c p) t -> p c t", p=P))\
                  .then_inc(loaded, 16)
                sp.dma_start(hin[:rows, 0:tiles, :], tokens(h_in, ga * EG, tiles, rows)).then_inc(loaded, 16)
            turns(sp, turn)

        @block.tensor
        def _(pe):
            mm = nc.tensor.matmul
            pe.sem_inc(a_free, 1)
            pe.sem_inc(scat_ready, 4)
            pe.sem_inc(up_done, NHID)
            pe.wait_ge(const_in, 16 * N_CONST)
            for c in range(DC):
                for half in range(2):
                    for n in range(PH):
                        s = half * PH + n
                        last = mm(route[:, half, n * NKEYS:(n + 1) * NKEYS], w_q[:, s, c * P:c * P + P], keys[:, s, :],
                                  start=True, stop=True)
                last.then_inc(simw_ready, 1)
                pe.wait_ge(simw_taken, c + 1)

            def stand():
                pe.sem_inc(passed, 1)

            def turn(g, blocks, routing, q):
                tiles, rows, halves, tt = shape_of(routing == "tail")
                b_tiles, b_rows, _, _ = shape_of(blocks == "tail")
                nb = b_tiles * b_rows
                ga, b = g + 1, 1 - q
                for jj in range(JB + LAG):
                    if blocks and jj < JB:
                        pe.wait_ge(gelu_ready, g * JB + jj + 1)
                        if jj == 0:
                            pe.wait_ge(tp_taken, g + 1)
                            stand()
                        for c in range(DC):
                            last = mm(work[:, jj % 2, 0:nb], down[:, c, jj, :], xnT[:, q, c, 0:nb], start=c == 0,
                                      stop=c == DC - 1)
                        last.then_inc(hid_ready, 1)
                    if routing and jj == PE_AT["proj"]:
                        pe.wait_ge(loaded, ga * 32 + 32)
                        pe.wait_ge(sims_taken, ga * 2 + 1)
                        stand()
                        for j in range(tiles):
                            for c in range(DC):
                                last = mm(route[:rows, 0, j * D:j * D + D], aT[:, c, j * P:j * P + rows],
                                          wout[:, c, :], start=c == 0, stop=c == DC - 1)
                        last.then_inc(proj_ready, 1)
                        pe.wait_ge(proj_ready, ga + 1)
                        pe.sem_inc(a_free, 1)
                    if routing and jj == PE_AT["tp"]:
                        pe.wait_ge(proj_taken, ga + 1)
                        pe.wait_ge(xn_ready, ga + 1)
                        for c in range(DC):
                            for j in range(tiles):
                                last = nc.tensor.transpose(route[:, 0, c * EG + j * P:c * EG + j * P + rows],
                                                           x[:rows, j, c * P:c * P + P], ident[:rows, :rows])
                        last.then_inc(tp_ready, 1)
                    for j in range(tiles if routing else 0):
                        t = ga * 2 + j
                        if jj == PE_AT["sims"][j]:
                            pe.wait_ge(tp_taken, ga + 1)
                            pe.wait_ge(sims_taken, t + 1)
                            stand()
                            for half in range(2):
                                for c in range(DC):
                                    last = mm(route[:rows, half, :], xnT[:, b, c, j * P:j * P + rows],
                                              simw[:, c, half * 512:half * 512 + 512], start=c == 0, stop=c == DC - 1)
                            last.then_inc(sims_ready, 1)
                        if jj == PE_AT["fields"][j]:
                            pe.wait_ge(fields_ready, t + 1)
                            pe.wait_ge(f_taken, t + 1)
                            stand()
                            for half in range(halves):
                                part = slice(64 * half, 64 * half + tt)
                                for f in range(4):
                                    last = mm(turned[64 * half:64 * half + 64, f * 64:f * 64 + tt], fields[part, f, :],
                                              ident[part, part], start=True, stop=True)
                            last.then_inc(f_ready, 1)
                        if jj in PE_AT["scatter"][j][:tt // SUB]:
                            s = PE_AT["scatter"][j].index(jj)
                            u = t * 4 + s
                            q_ = 64 * halves
                            pe.wait_ge(one_ready, u + 1)
                            pe.wait_ge(odd_ready, u + 1)
                            for k in range(SUB):
                                bank, at = divmod(k, SUB // 2)
                                if at == 0:
                                    pe.wait_ge(scat_taken, u * 2 + bank + 1)
                                    stand()
                                last = mm(scat[:, bank, at, :], one_i[:q_, s % 2, k, :, :].rearrange("p a i -> p (a i)"),
                                          one_j[:q_, s % 2, k, :], start=True, stop=True)
                                if at == SUB // 2 - 1:
                                    last.then_inc(scat_ready, 1)
                    if blocks and jj >= LAG:
                        e = jj - LAG
                        pe.wait_ge(gated, g * JB + e + 1)
                        if e == 0:
                            pe.wait_ge(out_taken, g + 1)
                            stand()
                        for j in range(b_tiles):
                            last = mm(total[:b_rows, j, :], hid[:, e % NHID, j * P:j * P + b_rows], up[:, e, :],
                                      start=e == 0 and j == 0, stop=e == JB - 1, skip_group_check=True)
                        last.then_inc(up_done, 1)
            turns(pe, turn)

        @block.scalar
        def _(act):
            A = nc.scalar.activation
            act.sem_inc(gelu_ready, 2)
            act.sem_inc(f_taken, 1)
            act.sem_inc(scat_taken, 2)
            act.sem_inc(h_stored, 32)
            act.wait_ge(const_in, 16 * N_CONST)
            for c in range(DC):
                act.wait_ge(simw_ready, c + 1)
                A(simw[:, c, :].rearrange("p (a b) -> p a b", a=2), route[:, :, :], ACT.Copy).then_inc(simw_taken, 1)

            def turn(g, blocks, routing, q):
                tiles, rows, halves, tt = shape_of(routing == "tail")
                b_tiles, b_rows, _, _ = shape_of(blocks == "tail")
                nb, n = b_tiles * b_rows, tiles * rows
                ga, b = g + 1, 1 - q
                for jj in range(JB + LAG):
                    if blocks and jj < JB:
                        act.wait_ge(hid_ready, g * JB + jj + 1)
                        act.wait_ge(up_done, g * JB + jj + 1)
                        A(hid[:, jj % NHID, 0:nb], work[:, jj % 2, 0:nb], ACT.Gelu).then_inc(gelu_ready, 1)
                    if routing and jj == PE_AT["tp"]:
                        act.wait_ge(tp_ready, ga + 1)
                        for c in range(DC):
                            last = A(xnT[:, b, c, 0:n], route[:, 0, c * EG:c * EG + n], ACT.Copy, scale=norm_w[:, c:c + 1])
                        last.then_inc(tp_taken, 1)
                    for j in range(tiles if routing else 0):
                        t = ga * 2 + j
                        if jj == PE_AT["fields"][j]:
                            act.wait_ge(f_ready, t + 1)
                            src = turned[:64 * halves, 0:256].rearrange("p (f t) -> p f t", f=4)[:, :, 0:tt]
                            A(FT[:64 * halves, j, :, 0:tt], src, ACT.Copy).then_inc(f_taken, 1)
                        if jj in PE_AT["scatter"][j][:tt // SUB]:
                            s = PE_AT["scatter"][j].index(jj)
                            for bank in range(2):
                                act.wait_ge(scat_ready, (t * 4 + s) * 2 + bank + 5)
                                at = j * P + s * SUB + bank * (SUB // 2)
                                to = G[:, b, :, at:at + SUB // 2] if halves == 1 else \
                                    G[:, b, :, j * P:j * P + P].rearrange("p j (h t) -> p j h t", h=2)[:, :, :, at - j * P:at - j * P + SUB // 2]
                                if halves == 1:
                                    A(to.rearrange("p j t -> p t j"), scat[:, bank, :, 0:JB], ACT.Copy).then_inc(scat_taken, 1)
                                else:
                                    A(to.rearrange("p j h t -> p t h j"), scat[:, bank, :, :].rearrange("p t (h j) -> p t h j", h=2),
                                      ACT.Copy).then_inc(scat_taken, 1)
                if blocks:
                    act.wait_ge(out_taken, g + 2)
                    act.dma_start(tokens(h_out, g * EG, b_tiles, b_rows), h[:b_rows, q, 0:b_tiles, :]).then_inc(h_stored, 16)
            turns(act, turn)
            act.wait_ge(h_stored, 16 * (EGROUPS + 3))

        @block.vector
        def _(dve):
            v = nc.vector
            dve.sem_inc(sims_taken, 1)
            dve.sem_inc(out_taken, 1)
            dve.sem_inc(h_free, 1)
            dve.wait_ge(const_made, 5)
            dve.wait_ge(const_in, 16 * N_CONST)

            def pick(step, t, link, link_apart, rows):
                R = slice(0, rows)
                flat = sums[R].rearrange("p h a b -> p h (a b)")
                sims = route[R, :, :].rearrange("p a (h s k) -> p (a h s) k", s=2, k=NKEYS)
                eight = iota[R, 0:8].rearrange("p (o a) -> p o a", o=1).broadcast_to([rows, 64, 8])
                num = best_if[R, :, :].rearrange("p (h s) k -> p h s k", s=2)

                def number(side, dst):
                    where = pk_f[R, side, :].rearrange("p (k o) -> p k o", o=1).broadcast_to([rows, 64, 8])
                    link(v.tensor_tensor(picked[R].rearrange("p h k a -> p (h k) a"), where, eight, ALU.is_equal))
                    link(v.tensor_tensor(picked[R], picked[R], num[:, :, side, :].rearrange("p h (o a) -> p h o a", o=1)
                                         .broadcast_to([rows, PH, PK, 8]), ALU.mult))
                    link(v.tensor_reduce(dst, picked[R].rearrange("p h k a -> p (h k) a"), AX.X, ALU.add))

                if step == 0:
                    dve.wait_ge(sims_ready, t + 1)
                    dve.sem_inc(dve_passed, 1)
                    for s in range(2 * PH):
                        last = v.max(best[R, s, :], sims[:, s, :])
                    link_apart(last)
                elif step == 1:
                    for s in range(2 * PH):
                        last = v.max_index(best_i[R, s, :], best[R, s, :], sims[:, s, :])
                    link(last)
                    dve.sem_inc(sims_taken, 1)
                    v.tensor_copy(best_if[R], best_i[R])
                elif step == 2:
                    s1 = best[R, :, :].rearrange("p (h s) k -> p h s k", s=2)
                    b1 = s1[:, :, 0, :].rearrange("p h (k o) -> p h k o", o=1).broadcast_to([rows, PH, 8, 8])
                    b2 = s1[:, :, 1, :].rearrange("p h (o k) -> p h o k", o=1).broadcast_to([rows, PH, 8, 8])
                    link_apart(v.tensor_tensor(sums[R], b1, b2, ALU.add))
                    for h_ in range(PH):
                        last = v.max(fs[R, h_, :], flat[:, h_, :])
                    link_apart(last)
                elif step == 3:
                    for h_ in range(PH):
                        last = v.max_index(pk[R, h_ * PK:(h_ + 1) * PK], fs[R, h_, :], flat[:, h_, :])
                    link(last)
                    v.tensor_scalar(pk_u[R, 0, :], pk[R, :], 3, None, ALU.logical_shift_right)
                    link(v.tensor_scalar(pk_u[R, 1, :], pk[R, :], 7, None, ALU.bitwise_and))
                    link(v.tensor_copy(pk_f[R], pk_u[R]))
                elif step == 4:
                    number(0, fields[R, 0, :])
                elif step == 5:
                    number(1, j_f[R, :])
                else:
                    link(v.tensor_copy(j_u[R, :], j_f[R, :]))
                    v.tensor_scalar(j_parts[R, 0, :], j_u[R, :], 1, None, ALU.logical_shift_right)
                    link(v.tensor_scalar(j_parts[R, 1, :], j_u[R, :], 1, None, ALU.bitwise_and))
                    v.tensor_copy(fields[R, 1, :], j_parts[R, 0, :])
                    link(v.tensor_copy(par[R, :], j_parts[R, 1, :]))
                    weight = fs[R].rearrange("p h k -> p (h k)")
                    link(v.scalar_tensor_tensor(fields[R, 3, :], weight, 0.0, par[R, :], ALU.max, ALU.mult))
                    v.scalar_tensor_tensor(fields[R, 2, :], weight, 0.0, fields[R, 3, :], ALU.max, ALU.subtract)\
                        .then_inc(fields_ready, 1)

            def one_hot(s, t, j, link, halves):
                q = 64 * halves
                at = slice(s * SUB, (s + 1) * SUB)

                def wide(f, n):
                    return FT[:q, j, f, at].rearrange("p (t o) -> p t o", o=1).broadcast_to([q, SUB, n])

                def numbers(row, n):
                    return row[:q, 0:n].rearrange("p (o i) -> p o i", o=1).broadcast_to([q, SUB, n])
                if s == 0:
                    dve.wait_ge(f_taken, t + 2)
                dve.wait_ge(scat_ready, (t * 4 + s) * 2 + 2)
                link(v.tensor_tensor(eq[:q, s % 2], wide(0, NKEYS), numbers(iota, NKEYS), ALU.is_equal))
                dve.sem_inc(eq_ready, 1)
                v.tensor_tensor(one_j[:q, s % 2], wide(1, 2 * JB), numbers(iota_j, 2 * JB), ALU.is_equal)
                v.tensor_tensor(one_i[:q, s % 2, :, 0, :], eq[:q, s % 2], wide(2, NKEYS), ALU.mult).then_inc(one_ready, 1)

            def turn(g, blocks, routing, q):
                tiles, rows, halves, tt = shape_of(routing == "tail")
                b_tiles, b_rows, _, _ = shape_of(blocks == "tail")
                nb = b_tiles * b_rows
                ga, b = g + 1, 1 - q
                chain = Chain(dve, chained, ROUTE_LINKS, ga)
                link = chain.link
                R, t_ = slice(0, rows), slice(0, tiles)
                for jj in range(JB):
                    if blocks:
                        dve.wait_ge(gelu_ready, g * JB + jj + 3)
                        if jj == 0:
                            dve.wait_ge(scat_taken, g * 16 + (18 if blocks == "full" else 4))
                        v.tensor_tensor(hid[:, jj % NHID, 0:nb], hid[:, jj % NHID, 0:nb], G[:, q, jj, 0:nb], ALU.mult)\
                            .then_inc(gated, 1)
                    if not routing:
                        continue
                    if jj == DVE_AT["h"]:
                        dve.wait_ge(loaded, ga * 32 + 32)
                        bias = bout[R, :].rearrange("p (a d) -> p a d", a=1).broadcast_to([rows, tiles, D])
                        hb = h[:, b]
                        dve.wait_ge(h_stored, ga * 16 + 16)
                        link(v.tensor_tensor(hb[R, t_, :], hin[R, t_, :], bias, ALU.add))
                        dve.sem_inc(h_free, 1)
                        dve.wait_ge(proj_ready, ga + 1)
                        proj = route[R, 0, :].rearrange("p (k d) -> p k d", k=2)[:, t_, :]
                        chain.link_apart(v.tensor_tensor(hb[R, t_, :], hb[R, t_, :], proj, ALU.add))
                        dve.sem_inc(proj_taken, 1)
                        statistics(v, chain, hb, stats, mv, ve, tiles, rows, LN_EPS).then_inc(var_ready, 1)
                    if jj == DVE_AT["x"]:
                        dve.wait_ge(rstd_ready, 2 * ga + 1)
                        chain.link_apart(normalise(v, h[:, b], x, mv, rstd, tiles, rows))
                        link(statistics(v, chain, x, stats, mv, ve, tiles, rows, RMS_EPS))
                        link(v.tensor_tensor(m2[R, t_], mv[R, t_, 0], mv[R, t_, 0], ALU.mult))
                        v.tensor_tensor(ve[R, t_], ve[R, t_], m2[R, t_], ALU.add).then_inc(var_ready, 1)
                    if jj == DVE_AT["xn"]:
                        dve.wait_ge(rstd_ready, 2 * ga + 2)
                        for j in range(tiles):
                            last = v.tensor_scalar(x[R, j, :], x[R, j, :], rstd[R, j:j + 1], None, ALU.mult)
                        last.then_inc(xn_ready, 1)
                    for j in range(tiles):
                        t = ga * 2 + j
                        for step, at in enumerate(DVE_AT["pick"][j]):
                            if at == jj:
                                pick(step, t, link, chain.link_apart, rows)
                        if jj in DVE_AT["one_hot"][j][:tt // SUB]:
                            one_hot(DVE_AT["one_hot"][j].index(jj), t, j, link, halves)
                if blocks:
                    dve.wait_ge(up_done, g * JB + JB + NHID)
                    v.tensor_tensor(h[:b_rows, q, 0:b_tiles, :], h[:b_rows, q, 0:b_tiles, :], total[:b_rows, 0:b_tiles, :],
                                    ALU.add).then_inc(out_taken, 1)
                assert routing != "full" or chain.count == ROUTE_LINKS, chain.count
            turns(dve, turn)

        @block.gpsimd
        def _(pool):
            nc.gpsimd.memset(minus_half[:, :], -0.5).then_inc(const_made, 1)
            nc.gpsimd.iota(iota[:, :], [[1, NKEYS]], base=0, channel_multiplier=0, allow_small_or_imprecise_dtypes=True)\
                .then_inc(const_made, 1)
            pool.wait_ge(const_made, 2)
            for half in range(2):
                nc.gpsimd.iota(iota_j[64 * half:64 * half + 64, :], [[1, 2 * JB]], base=-JB * half, channel_multiplier=0,
                               allow_small_or_imprecise_dtypes=True).then_inc(const_made, 1)
            pool.wait_ge(const_made, 4)
            pool.sem_inc(const_made, 1)

            def turn(g, blocks, routing, q):
                if routing is None:
                    return
                tiles, rows, halves, tt = shape_of(routing == "tail")
                for n in range(2):
                    pool.wait_ge(var_ready, 2 * (g + 1) + n + 1)
                    nc.gpsimd.tensor_tensor(rstd[:rows, 0:tiles], ve[:rows, 0:tiles], minus_half[:rows, 0:tiles],
                                            ALU.pow).then_inc(rstd_ready, 1)
                n = 64 * halves
                for j in range(tiles):
                    for s in range(tt // SUB):
                        t = (g + 1) * 2 + j
                        pool.wait_ge(eq_ready, t * 4 + s + 1)
                        pool.sem_inc(pool_passed, 1)
                        nc.gpsimd.tensor_tensor(
                            one_i[:n, s % 2, :, 1, :], eq[:n, s % 2],
                            FT[:n, j, 3, s * SUB:(s + 1) * SUB].rearrange("p (t o) -> p t o", o=1).broadcast_to([n, SUB, NKEYS]),
                            ALU.mult).then_inc(odd_ready, 1)
            turns(pool, turn)


def padded_heads(w, axis):
    w = np.moveaxis(np.asarray(w), axis, 0)
    out = np.zeros((HEADS, SLOT) + w.shape[1:], w.dtype)
    out[:, :HD] = w.reshape((HEADS, HD) + w.shape[1:])
    return np.ascontiguousarray(np.moveaxis(out.reshape((HEADS * SLOT,) + w.shape[1:]), 0, axis))


def on_slots(vec):
    return np.ascontiguousarray(vec.reshape(HG, P).T)


def constants():
    p = np.arange(P)
    head = np.arange(HEADS)
    gamma = np.array([1.0 - 2.0 ** (-5 - 8 * i // HEADS) for i in range(HEADS)], np.float32)
    query = np.concatenate([np.arange(T), np.arange(P, T)])
    key = np.concatenate([np.zeros(T, np.int64), np.full(T - P, P)])[None, :] + p[:, None]
    diff = query[None, :] - key
    power = gamma[None, :, None] ** np.maximum(diff, 0).astype(np.float32)[:, None, :]
    decay = np.where(diff[:, None, :] >= 0, power * np.float32(SCALE), np.float32(0)).astype(np.float32)
    col = np.arange(HEADS * SLOT)
    own = (col[None, :] // SLOT == head[:, None]).astype(np.float32)
    sel = (head[None, None, :] == SLOTS * np.arange(HG)[None, :, None] + (p // SLOT)[:, None, None]).astype(np.float32)
    avg = ((p[:, None] // SLOT == p[None, :] // SLOT) & (p[:, None] % SLOT < HD)).astype(np.float32) / HD
    valid = p[None, :] <= p[:, None]
    mask = np.where(np.stack([valid, valid.T], 1), 0.0, BIG).astype(mybir.dt.np(BF16))
    aug = np.zeros((HEADS, HG, P), np.float32)
    aug[head, head // SLOTS, SLOT * (head % SLOTS) + HD] = 1
    ones_row = np.zeros((HEADS, SLOT), np.float32)
    ones_row[:, HD] = 1
    return {"mask": mask, "sums_of": np.ascontiguousarray(aug.T), "share": np.ascontiguousarray(sel.T), "ones_row": ones_row.reshape(-1), "ident": np.eye(P, dtype=np.float32), "decay": decay, "own": own, "sel": sel, "avg": avg.astype(np.float32)}


def laid_out(inputs):
    a = {k: np.asarray(v) for k, v in inputs.items()}
    c = constants()
    tight = np.ascontiguousarray

    def by_state(m):
        return m.reshape(PAIRS, 2, 64).transpose(1, 2, 0).reshape(P, PAIRS)

    def column(vec):
        return tight(vec.reshape(DC, P).T)

    def head_weight(w):
        return padded_heads(w.transpose(1, 0, 2).reshape(D, D), 1)

    def slots(vec):
        return on_slots(padded_heads(vec, 0))

    b_ri, qkv, zero = a["L0_tok_B_ri"], a["L1_attn_w_qkv"], np.zeros(D, np.float32)
    down = a["L1_ffn_expert_down"].reshape(NKEYS, JB, 2, DC, P)
    up = a["L1_ffn_expert_up"].reshape(NKEYS, JB, 2, D)
    return {
        "cls_tok": a["cls_tok"].reshape(1, D),
        "log_dt": tight(a["L0_tok_log_dt"].reshape(PAIRS, 2).T),
        "inv_A_real": tight(by_state(a["L0_tok_inv_A_real"])),
        "A_imag": tight(by_state(a["L0_tok_A_imag"])),
        "B_ri": tight(np.stack([by_state(b_ri[..., 0]), by_state(b_ri[..., 1])], 1)),
        "C_ri": tight(a["x"].reshape(B, PAIRS, 2, 64, 2).transpose(2, 3, 4, 1, 0).reshape(P, 2, PAIRS, B)),
        "ret_wq": head_weight(a["L0_attn_Wq"]), "ret_wk": head_weight(a["L0_attn_Wk"]),
        "ret_wv": head_weight(a["L0_attn_Wv"]),
        "ret_gnw": slots(a["L0_attn_gn_weight"]), "ret_gnb": slots(a["L0_attn_gn_bias"]),
        "ret_wout": a["L0_attn_Wout"],
        "ln1_g": column(a["L0_ffn_ln1_g"]), "ln1_b": column(a["L0_ffn_ln1_b"]),
        "ln2_g": column(a["L0_ffn_ln2_g"]), "ln2_b": column(a["L0_ffn_ln2_b"]),
        "soft_wq": padded_heads(a["L0_ffn_Wq"], 1), "soft_wk": padded_heads(a["L0_ffn_Wk"], 1),
        "soft_wv": a["L0_ffn_Wv"], "soft_bq": slots(a["L0_ffn_bq"]),
        "soft_bk": on_slots(np.where(c["ones_row"] > 0, c["ones_row"], padded_heads(a["L0_ffn_bk"], 0))),
        "soft_bv": a["L0_ffn_bv"].reshape(1, D), "soft_wp": a["L0_ffn_Wp"], "soft_bp": a["L0_ffn_bp"].reshape(1, D),
        "gate_w": a["L0_ffn_gate_W"], "gate_b": a["L0_ffn_gate_b"].reshape(1, EXPERTS),
        "moe_w1": tight(a["L0_ffn_exp_W1"].reshape(EXPERTS, DC, P, HIDDEN).transpose(2, 0, 1, 3)),
        "moe_b1": tight(a["L0_ffn_exp_b1"].reshape(EXPERTS, HB, P).transpose(2, 0, 1)),
        "moe_w2": tight(a["L0_ffn_exp_W2"].reshape(EXPERTS, HB, P, D).transpose(2, 0, 1, 3)),
        "moe_b2": a["L0_ffn_exp_b2"],
        "stable_wq": padded_heads(tight(qkv[:D].T), 1), "stable_wk": padded_heads(tight(qkv[D:2 * D].T), 1),
        "stable_wv": tight(qkv[2 * D:].T), "stable_bq": on_slots(padded_heads(zero, 0)),
        "stable_bk": on_slots(c["ones_row"]), "stable_bv": zero.reshape(1, D),
        "stable_wout": tight(a["L1_attn_w_out"].T), "stable_bout": a["L1_attn_b_out"].reshape(1, D),
        "norm_w": column(a["L1_ffn_norm_w"]),
        "peer_w_q": tight(a["L1_ffn_w_q"].reshape(2 * PH, P, D).transpose(1, 0, 2)),
        "peer_keys": tight(a["L1_ffn_keys"].transpose(3, 0, 2, 1).reshape(P, 2 * PH, NKEYS)),
        "peer_down": tight(down.transpose(4, 3, 1, 2, 0).reshape(P, DC, JB, P)),
        "peer_up": tight(up.transpose(2, 0, 1, 3).reshape(P, JB, D)),
        "ident": c["ident"], "decay": c["decay"], "own": c["own"], "sel": c["sel"], "avg": c["avg"],
        "sums_of": c["sums_of"], "share": c["share"], "mask": c["mask"],
    }


def tower(nc, i, out):
    rows = out.rearrange("b t d -> (b t) d")

    def scratch(name, shape):
        return nc.dram_tensor(name, shape, F32, kind="Internal").ap()

    h0 = scratch("h0", (B, T, D))
    xT, aT = scratch("xT", (D, NTOK)), scratch("aT", (D, NTOK))
    x2, hx, h2 = scratch("x2", (NTOK, D)), scratch("hx", (NTOK, D)), scratch("h2", (NTOK, D))
    h0_rows = h0.rearrange("b t d -> (b t) d")
    token_mixer(nc, i["log_dt"], i["inv_A_real"], i["A_imag"], i["B_ri"], i["C_ri"], i["cls_tok"], h0)
    enter_retention(nc, h0_rows, i["ident"], xT)
    retention(nc, xT, i["ret_wq"], i["ret_wk"], i["ret_wv"], i["ret_gnw"], i["ret_gnb"], i["decay"], i["own"], i["sel"],
              i["avg"], aT)
    enter_attention(nc, aT, h0_rows, i["ret_wout"], i["ln1_g"], i["ln1_b"], i["ident"], hx, x2, xT)
    attention(nc, True, xT, i["soft_wq"], i["soft_wk"], i["soft_wv"], i["soft_bq"], i["soft_bk"], i["soft_bv"],
              i["own"], i["sel"], i["sums_of"], i["share"], i["ident"], i["mask"], aT)
    experts(nc, aT, x2, hx, i["soft_wp"], i["soft_bp"], i["ln2_g"], i["ln2_b"], i["gate_w"], i["gate_b"],
            i["moe_w1"], i["moe_b1"], i["moe_w2"], i["moe_b2"], i["ident"], h2, xT)
    attention(nc, False, xT, i["stable_wq"], i["stable_wk"], i["stable_wv"], i["stable_bq"], i["stable_bk"],
              i["stable_bv"], i["own"], i["sel"], i["sums_of"], i["share"], i["ident"], i["mask"], aT)
    product_keys(nc, aT, h2, i["stable_wout"], i["stable_bout"], i["norm_w"], i["peer_w_q"], i["peer_keys"],
                 i["peer_down"], i["peer_up"], i["ident"], rows)


def kernel(**inputs):
    import concourse.bacc as bacc
    from concourse.bass_utils import run_bass_kernel_spmd

    arrays = laid_out(inputs)
    nc = bacc.Bacc("TRN2", target_bir_lowering=False, num_devices=1)
    aps = {name: nc.dram_tensor(f"in_{name}", a.shape, mybir.dt.from_np(a.dtype), kind="ExternalInput").ap()
           for name, a in arrays.items()}
    out = nc.dram_tensor("out", (B, T, D), F32, kind="ExternalOutput").ap()
    tower(nc, aps, out)
    result = run_bass_kernel_spmd(nc, [{f"in_{name}": a for name, a in arrays.items()}], core_ids=[0])
    return result.results[0]["out"]
```

```python
import math
from contextlib import ExitStack

import numpy as np

import concourse.bass as bass
from concourse import mybir

F32 = mybir.dt.float32
U32 = mybir.dt.uint32
ALU = mybir.AluOpType
ACT = mybir.ActivationFunctionType
AX = mybir.AxisListType

P = 128
B = 16
D = 256
DC = D // P
T = D + 1
NTOK = B * T
HEADS, HD = 16, 16
SLOT = 32
SLOTS = P // SLOT
HG = HEADS // SLOTS
GROUP = 512
NGROUPS = NTOK // GROUP
TAIL = NTOK - NGROUPS * GROUP
EG = 2 * P
EGROUPS = NTOK // EG
LN_EPS = 1e-5
RMS_EPS = 1e-6


class Chain:

    def __init__(self, engine, sem, per=0, turn=0, base=0):
        self.engine, self.sem, self.per, self.turn, self.base, self.count = engine, sem, per, turn, base, 0

    def link(self, instruction):
        instruction.then_inc(self.sem, 1)
        self.count += 1
        self.engine.wait_ge(self.sem, self.turn * self.per + self.base + self.count)

    def link_apart(self, instruction):
        self.link(instruction)
        self.engine.sem_inc(self.sem, 1)
        self.count += 1

    def done(self):
        assert self.count == self.per, (self.count, self.per)


class Room:

    def __init__(self, nc, ctx, name):
        self.nc, self.ctx, self.name, self.sems = nc, ctx, name, []
        ctx.callback(self.close)

    def close(self):
        self.nc.clear_and_free_semaphores(self.sems)
        self.nc.all_engine_barrier()

    def sb(self, name, shape, dt=F32):
        return self.ctx.enter_context(self.nc.sbuf_tensor(f"{self.name}_{name}", shape, dt))

    def ps(self, name, shape, dt=F32):
        return self.ctx.enter_context(self.nc.psum_tensor(f"{self.name}_{name}", shape, dt))

    def sem(self, name):
        self.sems.append(self.nc.alloc_semaphore(f"{self.name}_{name}"))
        return self.sems[-1]


class Track:

    def __init__(self, r, passed, name, psum, banks, units):
        self.passed = passed
        self.psum, self.banks, self.units = psum, banks, units
        self.at = {unit: n for n, (unit, _) in enumerate(units)}
        self.ready = r.sem(f"{name}_ready")
        self.taken = {who: r.sem(f"{name}_taken_{who}") for who in sorted({w for _, w in units})}
        self.per = {who: sum(w == who for _, w in units) for who in self.taken}

    def open(self, engines):
        for who, engine in engines.items():
            if who in self.taken:
                engine.sem_inc(self.taken[who], 1)

    def wait_taken(self, engine, b, unit):
        n = self.at[unit]
        who = self.units[n][1]
        engine.wait_ge(self.taken[who], b * self.per[who] + sum(w == who for _, w in self.units[:n + 1]) + 1)

    def bank(self, pe, b, unit):
        n = self.at[unit]
        if n >= self.banks:
            self.wait_taken(pe, b, self.units[n - self.banks][0])
        else:
            for who, sem in self.taken.items():
                pe.wait_ge(sem, b * self.per[who] + 1)
        pe.sem_inc(self.passed, 1)
        return self.psum[:, n % self.banks, :]

    def full(self, engine, b, unit):
        engine.wait_ge(self.ready, b * len(self.units) + self.at[unit] + 1)
        return self.psum[:, self.at[unit] % self.banks, :]



def turns(engine, turn):
    turn(-1, "A", 1)
    turn(0, "AB", 0)
    with engine.Fori(0, B // 2 - 1) as n:
        turn(2 * n + 1, "ABC", 1)
        turn(2 * n + 2, "ABC", 0)
    turn(B - 1, "BC", 1)
    turn(B, "C", 0)


L1 = 64
LA = D // L1
PAIRS = D // 2
PC = 32
LN2 = math.log(2.0)
LN2_HI = math.floor(LN2 * 2 ** 15) / 2 ** 15
LN2_LO = LN2 - LN2_HI
ROUND = 1.5 * 2 ** 23
EXP_TERMS = 8
TOK_LINKS = 75


def token_mixer(nc, log_dt, inv_A_real, A_imag, B_ri, C_ri, cls_tok, h_out):
    ctx = ExitStack()
    with ctx:
        r = Room(nc, ctx, "tok")
        par = r.sb("par", [P, 5, PC])
        c_ri = r.sb("c_ri", [P, 2, PC, B])
        ex = r.sb("ex", [P, 2, PC])
        two_k = r.sb("two_k", [P, PC], mybir.dt.int32)
        tmp = r.sb("tmp", [P, 6, PC])
        E = r.sb("E", [P, 2, 8, PC])
        Vs = r.sb("V", [P, 2, 2, PC, L1])
        Ws = r.sb("W", [P, 2, 2, PC, LA, B])
        prod = r.sb("prod", [P, 4, PC * 32])
        res = r.sb("res", [P, PC, L1])
        cls = r.sb("cls", [B, D])
        acc = r.ps("acc", [P, PC, L1])
        loaded, inputs_free = r.sem("loaded"), r.sem("inputs_free")
        exps, chained, powers_ready, products_done = r.sem("exps"), r.sem("chained"), r.sem("powers"), r.sem("products")
        res_ready, stored, cls_in, cls_out = r.sem("res_ready"), r.sem("stored"), r.sem("cls_in"), r.sem("cls_out")
        waits_passed = r.sem("waits_passed")
        turns = PAIRS // PC
        block = ctx.enter_context(nc.Block())

        @block.sync
        def _(sp):
            sp.dma_start(cls[:, :], cls_tok[0:1, :].broadcast_to([B, D])).then_inc(cls_in, 16)
            sp.wait_ge(cls_in, 16)
            sp.dma_start(h_out[:, 0, :], cls[:, :]).then_inc(cls_out, 16)
            sp.sem_inc(stored, 16)

            def load(t):
                sp.wait_ge(inputs_free, t + 1)
                at = bass.ds(t * PC, PC)
                for h2 in range(2):
                    half = slice(64 * h2, 64 * h2 + 64)
                    sp.dma_start(par[half, 0, :], log_dt[h2:h2 + 1, at].broadcast_to([64, PC])).then_inc(loaded, 16)
                sp.dma_start(par[:, 1, :], inv_A_real[:, at]).then_inc(loaded, 16)
                sp.dma_start(par[:, 2, :], A_imag[:, at]).then_inc(loaded, 16)
                sp.dma_start(par[:, 3:5, :], B_ri[:, :, at]).then_inc(loaded, 16)
                sp.dma_start(c_ri[:, :, :, :], C_ri[:, :, at, :]).then_inc(loaded, 16)

            def store(t):
                sp.wait_ge(res_ready, t + 2)
                for h2 in range(2):
                    for a in range(LA):
                        p0 = 64 * h2 + B * a
                        dst = h_out[:, bass.ds(1 + h2 + t * (2 * PC), PC, 2), L1 * a:L1 * a + L1]
                        sp.dma_start(dst, res[p0:p0 + B, :, :]).then_inc(stored, 16)

            load(0)
            with sp.Fori(0, turns - 1) as t:
                load(t + 1)
                store(t)
            store(turns - 1)
            sp.wait_ge(stored, 16 * 8 * turns + 16)
            sp.wait_ge(cls_out, 16)

        @block.scalar
        def _(act):
            act.sem_inc(res_ready, 1)

            def exponential(t):
                act.wait_ge(loaded, (t + 1) * 96)
                nc.scalar.activation(ex[:, 1, :], par[:, 1, :], ACT.Exp).then_inc(exps, 1)

            def copy_out(t):
                act.wait_ge(stored, t * 128 + 16)
                act.wait_ge(products_done, t + 3)
                nc.scalar.activation(res[:, :, :], acc[:, :, :], ACT.Copy, scale=2.0).then_inc(res_ready, 1)

            exponential(0)
            with act.Fori(0, turns - 1) as t:
                exponential(t + 1)
                copy_out(t)
            copy_out(turns - 1)

        @block.vector
        def _(dve):
            nc.vector.memset(prod[:, :, 0:1], 0.0).then_inc(inputs_free, 1)
            v = nc.vector

            def products(chain, x, er, ei, n):
                shape = x[0].shape
                q = [prod[:, k, 0:n].rearrange("p (a b) -> p a b", a=shape[1]) if len(shape) == 3 else
                     prod[:, k, 0:n].rearrange("p (a b c) -> p a b c", a=shape[1], b=shape[2]) for k in range(4)]
                v.tensor_tensor(q[0], x[0], er, ALU.mult)
                v.tensor_tensor(q[1], x[1], ei, ALU.mult)
                v.tensor_tensor(q[2], x[0], ei, ALU.mult)
                chain.link(v.tensor_tensor(q[3], x[1], er, ALU.mult))
                return q

            def turn(t, parity):
                V, W = Vs[:, parity], Ws[:, parity]
                chain = Chain(dve, chained, TOK_LINKS, t)
                link = chain.link
                a, b, den, x2, y2, na = (tmp[:, k, :] for k in range(6))
                dve.wait_ge(loaded, (t + 1) * 96)
                x, k_, rem, p, dt = par[:, 0, :], tmp[:, 0, :], tmp[:, 1, :], tmp[:, 2, :], ex[:, 0, :]
                link(v.tensor_scalar(k_, x, 1.0 / LN2, None, ALU.mult))
                link(v.tensor_scalar(k_, k_, ROUND, None, ALU.add))
                link(v.tensor_scalar(k_, k_, ROUND, None, ALU.subtract))
                link(v.tensor_scalar(k_, k_, -126.0, 127.0, ALU.max, ALU.min))
                link(v.scalar_tensor_tensor(rem, k_, -LN2_HI, x, ALU.mult, ALU.add))
                link(v.scalar_tensor_tensor(rem, k_, -LN2_LO, rem, ALU.mult, ALU.add))
                link(v.tensor_scalar(p, rem, 1.0 / math.factorial(EXP_TERMS), None, ALU.mult))
                for n in range(EXP_TERMS - 1, 0, -1):
                    link(v.scalar_tensor_tensor(p, p, 1.0 / math.factorial(n), rem, ALU.add, ALU.mult))
                link(v.tensor_scalar(two_k[:, :], k_, 127.0, float(1 << 23), ALU.add, ALU.mult))
                link(v.scalar_tensor_tensor(dt, p, 1.0, two_k[:, :].bitcast(F32), ALU.add, ALU.mult))
                dve.wait_ge(exps, t + 1)
                link(v.scalar_tensor_tensor(a, ex[:, 1, :], -0.5, dt, ALU.mult, ALU.mult))
                link(v.scalar_tensor_tensor(b, par[:, 2, :], 0.5, dt, ALU.mult, ALU.mult))
                link(v.tensor_scalar(na, a, -1.0, 1.0, ALU.mult, ALU.add))
                link(v.tensor_tensor(den, na, na, ALU.mult))
                link(v.tensor_tensor(y2, b, b, ALU.mult))
                link(v.tensor_tensor(den, den, y2, ALU.add))
                link(v.reciprocal(den, den))
                link(v.scalar_tensor_tensor(x2, a, -1.0, a, ALU.mult, ALU.mult))
                link(v.scalar_tensor_tensor(x2, x2, 1.0, y2, ALU.add, ALU.subtract))
                dve.wait_ge(products_done, t + 1)
                link(v.tensor_tensor(E[:, 0, 0, :], x2, den, ALU.mult))
                link(v.scalar_tensor_tensor(E[:, 1, 0, :], b, -2.0, den, ALU.mult, ALU.mult))
                for k in range(7):
                    link(v.tensor_tensor(x2, E[:, 0, k, :], E[:, 0, k, :], ALU.mult))
                    link(v.tensor_tensor(y2, E[:, 1, k, :], E[:, 1, k, :], ALU.mult))
                    link(v.scalar_tensor_tensor(E[:, 1, k + 1, :], E[:, 0, k, :], 2.0, E[:, 1, k, :], ALU.mult, ALU.mult))
                    link(v.tensor_tensor(E[:, 0, k + 1, :], x2, y2, ALU.subtract))
                link(v.memset(V[:, 0, :, 0:1], 1.0))
                link(v.memset(V[:, 1, :, 0:1], 0.0))
                for k in range(6):
                    n = 1 << k
                    e = [E[:, c, k, :].rearrange("p (a b) -> p a b", b=1).broadcast_to([P, PC, n]) for c in range(2)]
                    q = products(chain, [V[:, c, :, 0:n] for c in range(2)], e[0], e[1], PC * n)
                    v.tensor_tensor(V[:, 0, :, n:2 * n], q[0], q[1], ALU.subtract)
                    link(v.tensor_tensor(V[:, 1, :, n:2 * n], q[2], q[3], ALU.add))
                bb = [par[:, 3 + c, :].rearrange("p (a b) -> p a b", b=1).broadcast_to([P, PC, B]) for c in range(2)]
                q = products(chain, [c_ri[:, c, :, :] for c in range(2)], bb[0], bb[1], PC * B)
                v.tensor_tensor(W[:, 0, :, 0, :], q[0], q[1], ALU.subtract)
                last = v.tensor_tensor(W[:, 1, :, 0, :], q[2], q[3], ALU.add)
                link(last)
                v.memset(prod[:, :, 0:1], 0.0).then_inc(inputs_free, 1)
                dve.wait_ge(inputs_free, t + 2)
                for k, s in ((6, 1), (7, 2)):
                    e = [E[:, c, k, :].rearrange("p (a b) -> p a b", b=1).broadcast_to([P, PC, s * B]) for c in range(2)]
                    w = [W[:, c, :, :, :].rearrange("p a s c -> p a (s c)") for c in range(2)]
                    q = products(chain, [w[c][:, :, 0:s * B] for c in range(2)], e[0], e[1], PC * s * B)
                    v.tensor_tensor(w[0][:, :, s * B:2 * s * B], q[0], q[1], ALU.add)
                    link(v.tensor_tensor(w[1][:, :, s * B:2 * s * B], q[3], q[2], ALU.subtract))
                v.memset(prod[:, :, 0:1], 0.0).then_inc(powers_ready, 1)
                dve.wait_ge(powers_ready, t + 1)
                chain.done()

            with dve.Fori(0, turns // 2) as n:
                turn(2 * n, 0)
                turn(2 * n + 1, 1)

        @block.tensor
        def _(pe):
            pe.sem_inc(products_done, 2)

            def turn(t, parity):
                V, W = Vs[:, parity], Ws[:, parity]
                pe.wait_ge(powers_ready, t + 1)
                pe.wait_ge(res_ready, t + 1)
                pe.sem_inc(waits_passed, 1)
                for i in range(PC):
                    for h2 in range(2):
                        half = slice(64 * h2, 64 * h2 + 64)
                        for c in range(2):
                            last = nc.tensor.matmul(acc[half, i, :], W[half, c, i, :, :].rearrange("p a c -> p (a c)"),
                                                    V[half, c, i, :], start=c == 0, stop=c == 1)
                last.then_inc(products_done, 1)

            with pe.Fori(0, turns // 2) as n:
                turn(2 * n, 0)
                turn(2 * n + 1, 1)


def groups(engine, step):
    with engine.Fori(0, NGROUPS // 2) as n:
        for q in range(2):
            g = 2 * n + q
            step(g * GROUP, g, GROUP // P, P, q)
    step(NGROUPS * GROUP, NGROUPS, 1, TAIL, 0)


def tokens(ap, t0, tiles, rows):
    return ap[bass.ds(t0, tiles * rows), :].rearrange("(j p) d -> p j d", p=rows)


def statistics(v, chain, x, stats, mv, ve, tiles, rows, eps):
    for j in range(tiles):
        last = v.bn_stats(stats[:rows, j, :], x[:rows, j, :])
    chain.link_apart(last)
    for j in range(tiles):
        last = v.bn_aggr(mv[:rows, j, :], stats[:rows, j, :])
    chain.link(last)
    return v.tensor_scalar(ve[:rows, 0:tiles], mv[:rows, 0:tiles, 1], eps, None, ALU.add)


def normalise(v, x, out, mv, rstd, tiles, rows):
    for j in range(tiles):
        last = v.tensor_scalar(out[:rows, j, :], x[:rows, j, :], mv[:rows, j, 0:1], rstd[:rows, j:j + 1],
                               ALU.subtract, ALU.mult)
    return last


def transposed(nc, out, x, ident, tiles, rows):
    for c in range(DC):
        for j in range(tiles):
            last = nc.tensor.transpose(out[:, c, j * P:j * P + rows], x[:rows, j, c * P:c * P + P],
                                       ident[:rows, :rows])
    return last


def enter_retention(nc, h, ident_in, xT_out):
    ctx = ExitStack()
    with ctx:
        r = Room(nc, ctx, "ent")
        ident = r.sb("ident", [P, P])
        hs = r.sb("hs", [P, 2, 4, D])
        xn = r.sb("xn", [P, 2, 4, D])
        xt = r.sb("xt", [P, 2, DC, GROUP])
        stats, mv = r.sb("stats", [P, 4, 6]), r.sb("mv", [P, 4, 2])
        ve, rstd, minus_half = r.sb("ve", [P, 4]), r.sb("rstd", [P, 4]), r.sb("mh", [P, 4])
        tp = r.ps("tp", [P, 2, DC, GROUP])
        const_in, h_free = r.sem("const_in"), r.sem("h_free")
        loaded, stored = ([r.sem(f"{n}{q}") for q in range(2)] for n in ("loaded", "stored"))
        const_made, chained, var_ready, rstd_ready = r.sem("const_made"), r.sem("chained"), r.sem("var"), r.sem("rstds")
        xn_ready, tp_ready, xt_ready = r.sem("xn_ready"), r.sem("tp_ready"), r.sem("xt_ready")
        block = ctx.enter_context(nc.Block())

        @block.sync
        def _(sp):
            sp.dma_start(ident[:, :], ident_in).then_inc(const_in, 16)

            def step(t0, g, tiles, rows, q):
                sp.wait_ge(h_free, g + 1)
                sp.dma_start(hs[:rows, q, 0:tiles, :], tokens(h, t0, tiles, rows)).then_inc(loaded[q], 16)
            groups(sp, step)

        @block.vector
        def _(dve):
            v = nc.vector
            dve.sem_inc(h_free, 2)

            def step(t0, g, tiles, rows, q):
                chain = Chain(dve, chained, 3, g)
                dve.wait_ge(loaded[q], (g - q) * 8 + 16)
                statistics(v, chain, hs[:, q], stats, mv, ve, tiles, rows, LN_EPS).then_inc(var_ready, 1)
                dve.wait_ge(rstd_ready, g + 1)
                dve.wait_ge(tp_ready, g + 1)
                normalise(v, hs[:, q], xn[:, q], mv, rstd, tiles, rows).then_inc(xn_ready, 1)
                dve.wait_ge(xn_ready, g + 1)
                dve.sem_inc(h_free, 1)
                chain.done()
            groups(dve, step)

        @block.gpsimd
        def _(pool):
            nc.gpsimd.memset(minus_half[:, :], -0.5).then_inc(const_made, 1)
            pool.wait_ge(const_made, 1)

            def step(t0, g, tiles, rows, q):
                pool.wait_ge(var_ready, g + 1)
                nc.gpsimd.tensor_tensor(rstd[:rows, 0:tiles], ve[:rows, 0:tiles], minus_half[:rows, 0:tiles],
                                        ALU.pow).then_inc(rstd_ready, 1)
            groups(pool, step)

        @block.tensor
        def _(pe):
            pe.sem_inc(tp_ready, 2)
            pe.wait_ge(const_in, 16)

            def step(t0, g, tiles, rows, q):
                pe.wait_ge(xt_ready, g + 1)
                pe.wait_ge(xn_ready, g + 1)
                transposed(nc, tp[:, q], xn[:, q], ident, tiles, rows).then_inc(tp_ready, 1)
            groups(pe, step)

        @block.scalar
        def _(act):
            act.sem_inc(xt_ready, 2)
            for q in range(2):
                act.sem_inc(stored[q], 16)

            def step(t0, g, tiles, rows, q):
                act.wait_ge(stored[q], (g - q) * 8 + 16)
                act.wait_ge(tp_ready, g + 3)
                n = tiles * rows
                nc.scalar.activation(xt[:, q, :, 0:n], tp[:, q, :, 0:n], ACT.Copy).then_inc(xt_ready, 1)
                act.wait_ge(xt_ready, g + 3)
                act.dma_start(xT_out[:, bass.ds(t0, n)].rearrange("(c p) t -> p c t", p=P),
                              xt[:, q, :, 0:n]).then_inc(stored[q], 16)
            groups(act, step)
            for q in range(2):
                act.wait_ge(stored[q], 16 * (NGROUPS // 2 + 2 - q))


ODD = T - 1
SPAN = T + (T - P)
SCALE = HD ** -0.5


NP = 4


def retention(nc, xT_in, wq, wk, wv, gnw_in, gnb_in, decay_in, own_in, sel_in, avg_in, cT_out):
    ctx = ExitStack()
    with ctx:
        r = Room(nc, ctx, "ret")
        wq_s, wk_s, wv_s = (r.sb(n, [P, DC, 512]) for n in ("wq", "wk", "wv"))
        decay = r.sb("decay", [P, HEADS, SPAN])
        own = r.sb("own", [HEADS, 512])
        sel = r.sb("sel", [P, HG, HEADS])
        avg = r.sb("avg", [P, P])
        gnw, gnb = r.sb("gnw", [P, HG]), r.sb("gnb", [P, HG])
        xT = r.sb("xT", [P, DC, T])
        odd_x = r.sb("odd_x", [P, DC, HEADS])
        QHs, KTs = r.sb("QH", [P, 2, HG, SLOTS, T]), r.sb("KT", [P, 2, HG, T])
        Vs = r.sb("V", [P, 2, DC, 512])
        v_odd, V_odds = r.sb("v_odd", [HEADS, 512]), r.sb("V_odd", [HEADS, 2, 512])
        K_odds, q_odds = r.sb("K_odd", [P, 2, HG, HEADS]), r.sb("q_odd", [P, 2, HG])
        cTs = r.sb("cT", [P, 2, HG, T])
        p_odd = r.sb("p_odd", [HEADS, 1])
        PT = r.sb("PT", [P, NP, SPAN])
        cN = r.sb("cN", [P, HG, T])
        stats, mv = r.sb("stats", [P, HG, 6]), r.sb("mv", [P, HG, 2])
        d, q_, ve, rstd, mh = (r.sb(n, [P, HG]) for n in ("d", "q", "ve", "rstd", "mh"))
        gmean, gscale, gbias = (r.sb(n, [P, HG]) for n in ("gmean", "gscale", "gbias"))
        S = r.ps("S", [P, 2, 512])
        O = r.ps("O", [P, 2, 512])
        misc_a, misc_b, norm = r.ps("misc_a", [P, 2, 512]), r.ps("misc_b", [P, 1, 512]), r.ps("norm", [P, 512])
        const_in, loaded, x_free, passed = r.sem("const_in"), r.sem("loaded"), r.sem("x_free"), r.sem("passed")
        odd_ready, odd_copied, q_odd_ready = r.sem("odd_ready"), r.sem("odd_x"), r.sem("q_odd_ready")
        s_ready, p_ready, av_done = r.sem("s_ready"), r.sem("p_ready"), r.sem("av_done")
        o_ready, o_taken = r.sem("o_ready"), r.sem("o_taken")
        chained, means_ready, gm_ready, gv_ready, q_ready = (r.sem(n) for n in ("chained", "means", "gm", "gv", "q"))
        ve_ready, rstd_ready, affine_ready, normed, stored = (r.sem(n) for n in ("ve", "rstd", "affine", "normed", "stored"))
        const_made, sp_passed = r.sem("const_made"), r.sem("sp_passed")
        ta = Track(r, passed, "ta", misc_a, 2, [(f"{what}{g}", "dve" if what == "q" else "act") for g in range(HG) for what in "qk"]
                   + [(v, "act") for v in ("v0", "v1", "v_odd")])
        tb = Track(r, passed, "tb", misc_b, 1, [("odd_score", "act")])
        shares = [[f"q{g}", f"k{g}"] for g in range(HG)] + [["v0"], ["v1"], ["v_odd"]] + [[]] * (HEADS - HG - 3)
        X_FREE, ODD_SCORE = 8, 2
        LAST = HEADS // HG + 1
        GN = {"stats": 2, "mean": 4, "square": 5, "var": 6, "eps": 7, "affine": 9, "norm": 10}
        block = ctx.enter_context(nc.Block())

        @block.sync
        def _(sp):
            for dst, src in ((wq_s, wq), (wk_s, wk), (wv_s, wv)):
                sp.dma_start(dst[:, :, :], src.rearrange("(c p) n -> p c n", p=P)).then_inc(const_in, 16)
            for dst, src in ((own, own_in), (avg, avg_in), (gnw, gnw_in), (gnb, gnb_in)):
                sp.dma_start(dst[:, :], src).then_inc(const_in, 16)
            sp.dma_start(sel[:, :, :], sel_in).then_inc(const_in, 16)
            sp.dma_start(decay[:, :, :], decay_in).then_inc(const_in, 16)

            def turn(g, stages, q):
                if "A" in stages:
                    sp.wait_ge(x_free, g + 2)
                    sp.dma_start(xT[:, :, :], xT_in[:, bass.ds((g + 1) * T, T)].rearrange("(c p) t -> p c t", p=P))\
                      .then_inc(loaded, 16)
                if "C" in stages:
                    sp.wait_ge(normed, g)
                    dst = cT_out[:, bass.ds((g - 1) * T, T)].rearrange("(g s e) t -> s e g t", g=HG, s=SLOTS)
                    for s in range(SLOTS):
                        sp.dma_start(dst[s], cN[SLOT * s:SLOT * s + HD, :, :]).then_inc(stored, 16)
            turns(sp, turn)
            sp.wait_ge(stored, 16 * (SLOTS * B + 1))

        @block.tensor
        def _(pe):
            mm = nc.tensor.matmul
            pe.wait_ge(const_in, 144)
            pe.sem_inc(x_free, 1)
            pe.sem_inc(av_done, NP)

            def stand():
                pe.sem_inc(passed, 1)

            def turn(g, stages, q):
                p, b = 1 - q, g + 1

                def form(unit):
                    if unit == "v_odd":
                        pe.wait_ge(odd_copied, b + 1)
                    out = ta.bank(pe, b, unit)
                    n = int(unit[-1]) if unit[-1].isdigit() else 0
                    for c in range(DC):
                        if unit[0] in "qk":
                            w = wq_s if unit[0] == "q" else wk_s
                            last = mm(out[:, 0:T], w[:, c, n * P:n * P + P], xT[:, c, :], start=c == 0, stop=c == DC - 1)
                        elif unit == "v_odd":
                            last = mm(out[:HEADS, :], odd_x[:, c, :], wv_s[:, c, :], start=c == 0, stop=c == DC - 1)
                        else:
                            last = mm(out[:, :], xT[:, c, n * P:n * P + P], wv_s[:, c, :], start=c == 0, stop=c == DC - 1)
                    last.then_inc(ta.ready, 1)

                def scores(h):
                    if h == 0:
                        ta.wait_taken(pe, g, "q3")
                        ta.wait_taken(pe, g, "k3")
                    pe.wait_ge(p_ready, g * HEADS + h + 1)
                    stand()
                    hg, j = divmod(h, SLOTS)
                    mm(S[:, h % 2, 0:T], KTs[:, q, hg, 0:P], QHs[:, q, hg, j, :], start=True, stop=True)
                    mm(S[:, h % 2, T:SPAN], KTs[:, q, hg, P:2 * P], QHs[:, q, hg, j, P:T], start=True, stop=True)\
                        .then_inc(s_ready, 1)

                def products(g, h, q):
                    hg, j = divmod(h, SLOTS)
                    pe.wait_ge(p_ready, g * HEADS + h + 3)
                    if h == 0:
                        ta.wait_taken(pe, g, "v1")
                    if j == 0:
                        pe.wait_ge(o_taken, g * HG + hg + 1)
                    stand()
                    rows, at = slice(SLOT * j, SLOT * j + SLOT), slice(SLOT * h, SLOT * h + SLOT)
                    mm(O[rows, hg % 2, 0:T], Vs[:, q, 0, at], PT[:, h % NP, 0:T], start=True, stop=False,
                       skip_group_check=True)
                    mm(O[rows, hg % 2, P:T], Vs[:, q, 1, at], PT[:, h % NP, T:SPAN], start=False, stop=False,
                       skip_group_check=True).then_inc(av_done, 1)
                    if j == SLOTS - 1:
                        if hg == 0:
                            tb.wait_taken(pe, g, "odd_score")
                            pe.wait_ge(odd_ready, 2 * g + 2)
                            stand()
                        mm(O[:, hg % 2, ODD:T], V_odds[:, q, hg * P:hg * P + P], p_odd[:, :], start=False, stop=True,
                           skip_group_check=True).then_inc(o_ready, 1)

                for s in range(HEADS):
                    if "A" in stages:
                        if s == 0:
                            pe.wait_ge(loaded, b * 16 + 16)
                        for unit in shares[s]:
                            form(unit)
                        if s == X_FREE:
                            pe.wait_ge(ta.ready, b * len(ta.units) + len(ta.units))
                            pe.sem_inc(x_free, 1)
                    if "B" in stages:
                        scores(s)
                        if s == ODD_SCORE:
                            out = tb.bank(pe, g, "odd_score")
                            pe.wait_ge(odd_ready, 2 * g + 1)
                            pe.wait_ge(q_odd_ready, g + 1)
                            stand()
                            for hg in range(HG):
                                last = mm(out[:HEADS, 0:1], K_odds[:, q, hg, :], q_odds[:, q, hg:hg + 1], start=hg == 0,
                                          stop=hg == HG - 1)
                            last.then_inc(tb.ready, 1)
                        if s >= 2:
                            products(g, s - 2, q)
                    if "C" in stages:
                        if s < 2:
                            products(g - 1, HEADS - 2 + s, 1 - q)
                        if s == GN["mean"]:
                            pe.wait_ge(means_ready, g)
                            pe.wait_ge(ve_ready, g)
                            stand()
                            mm(norm[:, 0:HG], avg[:, :], mv[:, :, 0], start=True, stop=True).then_inc(gm_ready, 1)
                        if s == GN["var"]:
                            pe.wait_ge(q_ready, g)
                            stand()
                            mm(norm[:, 0:HG], avg[:, :], q_[:, :], start=True, stop=True).then_inc(gv_ready, 1)
            turns(pe, turn)

        @block.scalar
        def _(act):
            A = nc.scalar.activation
            for track in (ta, tb):
                track.open({"act": act})
            act.sem_inc(o_taken, 2)
            act.sem_inc(stored, 16)

            def turn(g, stages, q):
                p, b = 1 - q, g + 1

                def copy_out(g, hg, q):
                    act.wait_ge(o_ready, g * HG + hg + 1)
                    A(cTs[:, q, hg, :], O[:, hg % 2, 0:T], ACT.Copy).then_inc(o_taken, 1)

                for s in range(HEADS):
                    if "A" in stages:
                        for unit in shares[s]:
                            if unit[0] == "q":
                                continue
                            src = ta.full(act, b, unit)
                            if unit[0] == "k":
                                dst, src = KTs[:, p, int(unit[-1]), :], src[:, 0:T]
                            elif unit == "v_odd":
                                dst, src = v_odd[:, :], src[:HEADS, :]
                            else:
                                dst = Vs[:, p, int(unit[-1]), :]
                            A(dst, src, ACT.Copy).then_inc(ta.taken["act"], 1)
                    if "C" in stages:
                        if s == 1:
                            copy_out(g - 1, HG - 1, 1 - q)
                        if s == GN["norm"]:
                            act.wait_ge(affine_ready, g)
                            act.wait_ge(stored, (g - 1) * 16 * SLOTS + 16)
                            for hg in range(HG):
                                last = A(cN[:, hg, :], cTs[:, 1 - q, hg, :], ACT.Identity, bias=gbias[:, hg:hg + 1],
                                         scale=gscale[:, hg:hg + 1])
                            last.then_inc(normed, 1)
                    if "B" in stages:
                        if s == ODD_SCORE:
                            src = tb.full(act, g, "odd_score")
                            A(p_odd[:, :], src[:HEADS, 0:1], ACT.Copy, scale=SCALE).then_inc(tb.taken["act"], 1)
                        if s % SLOTS == LAST % SLOTS and s >= LAST:
                            hg = (s - LAST) // SLOTS
                            copy_out(g, hg, q)
            turns(act, turn)

        @block.vector
        def _(dve):
            v = nc.vector
            dve.wait_ge(const_in, 144)
            for track in (ta, tb):
                track.open({"dve": dve})
            dve.sem_inc(p_ready, 2)
            dve.sem_inc(ve_ready, 1)

            def turn(g, stages, q):
                p, b = 1 - q, g + 1
                chain = Chain(dve, chained, 7, g - 1)

                def group_norm(s):
                    if s == GN["stats"]:
                        dve.wait_ge(o_taken, g * HG + 2)
                        for hg in range(HG):
                            last = v.bn_stats(stats[:, hg, :], cTs[:, 1 - q, hg, :])
                        chain.link_apart(last)
                        for hg in range(HG):
                            last = v.bn_aggr(mv[:, hg, :], stats[:, hg, :])
                        last.then_inc(means_ready, 1)
                    if s == GN["square"]:
                        dve.wait_ge(gm_ready, g)
                        dve.wait_ge(means_ready, g)
                        v.tensor_copy(gmean[:, :], norm[:, 0:HG])
                        chain.link(v.tensor_tensor(d[:, :], mv[:, :, 0], norm[:, 0:HG], ALU.subtract))
                        chain.link(v.tensor_tensor(d[:, :], d[:, :], d[:, :], ALU.mult))
                        v.tensor_tensor(q_[:, :], d[:, :], mv[:, :, 1], ALU.add).then_inc(q_ready, 1)
                    if s == GN["eps"]:
                        dve.wait_ge(gv_ready, g)
                        v.tensor_scalar(ve[:, :], norm[:, 0:HG], LN_EPS, None, ALU.add).then_inc(ve_ready, 1)
                    if s == GN["affine"]:
                        dve.wait_ge(rstd_ready, g)
                        chain.link(v.tensor_tensor(gscale[:, :], rstd[:, :], gnw[:, :], ALU.mult))
                        chain.link(v.tensor_tensor(d[:, :], gmean[:, :], gscale[:, :], ALU.mult))
                        chain.link(v.tensor_tensor(gbias[:, :], gnb[:, :], d[:, :], ALU.subtract))
                        dve.sem_inc(affine_ready, 1)
                        chain.done()

                for s in range(HEADS):
                    if "A" in stages:
                        for unit in shares[s]:
                            if unit[0] != "q":
                                continue
                            hg = int(unit[-1])
                            src = ta.full(dve, b, unit)[:, 0:T].rearrange("p (o t) -> p o t", o=1)
                            v.tensor_tensor(QHs[:, p, hg, :, :], src.broadcast_to([P, SLOTS, T]),
                                            sel[:, hg, hg * SLOTS:(hg + 1) * SLOTS].rearrange("p (j o) -> p j o", o=1)
                                            .broadcast_to([P, SLOTS, T]), ALU.mult).then_inc(ta.taken["dve"], 1)
                        if s == HG:
                            ta.wait_taken(dve, b, f"q{HG - 1}")
                            v.tensor_reduce(q_odds[:, p, :], QHs[:, p, :, :, ODD], AX.X, ALU.add).then_inc(q_odd_ready, 1)
                    if "C" in stages:
                        group_norm(s)
                    if "B" in stages:
                        n = g * HEADS + s
                        dve.wait_ge(s_ready, n + 1)
                        dve.wait_ge(av_done, n + 1)
                        v.tensor_tensor(PT[:, s % NP, :], S[:, s % 2, 0:SPAN], decay[:, s, :], ALU.mult)\
                            .then_inc(p_ready, 1)
            turns(dve, turn)

        @block.gpsimd
        def _(pool):
            pool.wait_ge(const_in, 144)
            nc.gpsimd.memset(mh[:, :], -0.5).then_inc(const_made, 1)
            pool.wait_ge(const_made, 1)

            def turn(g, stages, q):
                p, b = 1 - q, g + 1
                if "A" in stages:
                    pool.wait_ge(loaded, b * 16 + 16)
                    pool.sem_inc(const_made, 1)
                    nc.gpsimd.tensor_copy(odd_x[:, :, :], xT[:, :, ODD:T].broadcast_to([P, DC, HEADS]))\
                        .then_inc(odd_copied, 1)
                    ta.wait_taken(pool, b, f"k{HG - 1}")
                    nc.gpsimd.tensor_tensor(K_odds[:, p, :, :], KTs[:, p, :, ODD:T].broadcast_to([P, HG, HEADS]),
                                            sel[:, :, :], ALU.mult).then_inc(odd_ready, 1)
                if "C" in stages:
                    pool.wait_ge(ve_ready, g + 1)
                    nc.gpsimd.tensor_tensor(rstd[:, :], ve[:, :], mh[:, :], ALU.pow).then_inc(rstd_ready, 1)
                if "A" in stages:
                    ta.wait_taken(pool, b, "v_odd")
                    nc.gpsimd.tensor_tensor(V_odds[:, p, :], v_odd[:, :], own[:, :], ALU.mult).then_inc(odd_ready, 1)
            turns(pool, turn)


N_ODD = 4
NW = 8
ODD_LN = 4
LN_HEADS = {4: (0, 1, 2, 3, 4), 10: (5, 6, 8, 9), HEADS: (11, 13, 14, 15)}
PRODUCTS = {True: {3: (0,), 4: (1, 2), 5: (3,), 6: (4,), 8: (5,), 9: (6,), 10: (7, 8), 11: (9,),
                   13: (10, 11), 15: (12, 13), 16: (14,), 17: (15,)},
            False: {7: (0,), 8: (1, 2), 9: (3,), 10: (4,), 11: (7,), 13: (5, 6, 9), 14: (8,), 15: (10,),
                    16: (12,), 18: (11, 13, 15, 14)}}
N_ONES = 11
ROOT = -0.5960716379833213
REST = 3 + 0.75 * ROOT ** 2
LINKS_A, LINKS_B = {True: 0, False: 1}, {True: 2, False: 2}
BF16 = mybir.dt.bfloat16
VC = HD + 1
BIG = -1e30


def attention(nc, causal, xT_in, wq, wk, wv, bq_in, bk_in, bv_in, own_in, sel_in, sums_in, share_in, ident_in,
              mask_in, aT_out):
    ctx = ExitStack()
    with ctx:
        r = Room(nc, ctx, "soft" if causal else "stable")
        wq_s, wk_s, wv_s = r.sb("wq", [P, DC, 512]), r.sb("wk", [P, DC, 512]), r.sb("wv", [P, DC, D])
        bq, bk = r.sb("bq", [P, HG]), r.sb("bk", [P, HG])
        bv = r.sb("bv", [P, HEADS, HD])
        own = r.sb("own", [HEADS, 512])
        sel = r.sb("sel", [P, HG, HEADS])
        ident, ident_b = r.sb("ident", [P, P]), r.sb("ident_b", [P, P], BF16)
        mask = r.sb("mask", [P, 2, P], BF16)
        sums_of = r.sb("sums_of", [P, HG, HEADS])
        share = r.sb("share", [HEADS, HG, P])
        sel_one = r.sb("sel_one", [P, HG, HEADS + 1])
        one_less, one_more = r.sb("one_less", [P, 1]), r.sb("one_more", [P, 1])
        xT = r.sb("xT", [P, DC, T])
        odd_x = r.sb("odd_x", [P, DC, HEADS])
        ones = r.sb("ones", [HEADS, P])
        QTs, KTs = r.sb("QT", [P, 2, HG, T]), r.sb("KT", [P, 2, HG, T])
        QHs = r.sb("QH", [P, 2, HG, SLOTS, T])
        Vs = r.sb("V", [P, 2, 2, HEADS, SLOT])
        v_odd, V_odds = r.sb("v_odd", [HEADS, HEADS, SLOT]), r.sb("V_odd", [HEADS, 2, 512])
        K_odds, Q_odds = r.sb("K_odd", [P, 2, HG, HEADS]), r.sb("Q_odd", [P, 2, HG, HEADS])
        negmax, negmax_T = r.sb("negmax", [P, 2, HEADS]), r.sb("negmax_T", [HEADS, 2, T])
        diag_odd = r.sb("diag_odd", [HEADS, 2, HEADS])
        U, Y, W = (r.sb(n, [P, NW, 512]) for n in ("U", "Y", "W"))
        w_oq, u_oq, y_oq = (r.sb(n, [P, 2 * HEADS]) for n in ("w_oq", "u_oq", "y_oq"))
        w_ok, u_ok, y_ok = (r.sb(n, [HEADS, T]) for n in ("w_ok", "u_ok", "y_ok"))
        oq, oq_sum = r.sb("oq", [P, HG, HEADS + 1]), r.sb("oq_sum", [P, HG])
        OT, inv = r.sb("OT", [P, HG, T]), r.sb("inv", [HEADS, T])
        aT = r.sb("aT", [P, HG, T])
        S = r.ps("S", [P, 2, 512])
        O = r.ps("O", [P, HG, 256])
        misc_a, misc_b, misc_c = r.ps("misc_a", [P, 2, 512]), r.ps("misc_b", [P, 1, 512]), r.ps("misc_c", [P, 1, 512])
        const_in, loaded, x_free, stored = r.sem("const_in"), r.sem("loaded"), r.sem("x_free"), r.sem("stored")
        ones_made, x_odd_ready, odd_ready, passed = r.sem("ones_made"), r.sem("x_odd"), r.sem("odd"), r.sem("passed")
        max_done, row_in, sp_passed = r.sem("max_done"), r.sem("row_in"), r.sem("sp_passed")
        s_ready, s_taken = r.sem("s_ready"), r.sem("s_taken")
        y_ready, t_ready, av_done = r.sem("y"), r.sem("t"), r.sem("av")
        maker = {h: "act" if causal or h in sum(LN_HEADS.values(), ()) else "dve" for h in range(HEADS)}
        made = {who: [h for h in range(HEADS) if maker[h] == who] for who in sorted(set(maker.values()))}
        w_ready = {who: r.sem(f"w_{who}") for who in made}
        ln_ready, ot_ready, ow_ready = r.sem("ln"), r.sem("ot"), r.sem("ow")
        o_taken, ot_copied = r.sem("o_taken"), r.sem("ot_copied")
        chain_a, chain_b, chain_c = r.sem("chain_a"), r.sem("chain_b"), r.sem("chain_c")

        def wait_weights(engine, g, h):
            who = maker[h % HEADS]
            engine.wait_ge(w_ready[who], (g + h // HEADS) * len(made[who]) + made[who].index(h % HEADS) + 1 + len(made[who]))

        order = [h for s in sorted(PRODUCTS[causal]) for h in PRODUCTS[causal][s]]

        def wait_multiplied(engine, g, h):
            engine.wait_ge(av_done, (g + h // HEADS) * HEADS + order.index(h % HEADS) + 1 + HEADS)

        nq = 1 if causal else T
        n_const = 12
        width = 3 * P if causal else 512

        taker = "act" if causal else "dve"
        units = [(f"{what}{g}", "dve" if what == "q" else taker) for g in range(HG) for what in "qk"]
        units += [("max0", "dve"), ("max1", "dve")] + [(v, taker) for v in ("v0", "v1", "v_odd")]
        units += [(f"max{h}", "dve") for h in range(2, HEADS)]
        units += [] if causal else [("odd_key_max", "dve")]
        units += [("odd_query_max", "dve"), ("negmax_T", "dve")]
        ta = Track(r, passed, "ta", misc_a, 2, units)
        tb = Track(r, passed, "tb", misc_b, 1, [("odd_query", "act"), ("odd_key", "act"), ("odd_out", "dve")])
        tc = Track(r, passed, "tc", misc_c, 1, [("sums", "dve")] + [(f"share{hg}", "dve") for hg in range(HG)])
        shares = [["q0", "k0", "q1"], ["k1", "q2", "k2"], ["q3", "k3"], ["max0", "max1"], ["v0", "v1", "v_odd"]]
        shares += [[f"max{2 * u}", f"max{2 * u + 1}"] for u in range(1, HEADS // 2)]
        shares += [["odd_query_max"] if causal else ["odd_key_max", "odd_query_max"], ["negmax_T"], [], []]
        assert len(shares) == HEADS and [u for s in shares for u in s] == [u for u, _ in units]
        X_FREE, ODD_Q, ODD_K, ODD_W, ODD_OUT, COPY_OUT = 6, 1, 2, 3, 9, 3 if causal else 4
        PASS_OUT = {5: "sums"} | {7 + hg: f"share{hg}" for hg in range(HG)}

        def take_projected(engine, unit, b, p):
            src = ta.full(engine, b, unit)
            n = int(unit[-1]) if unit[-1].isdigit() else 0
            if unit[0] in "qk":
                dst, bias = (QTs, bq) if unit[0] == "q" else (KTs, bk)
                dst, src, bias = dst[:, p, n, :], src[:, 0:T], bias[:, n:n + 1]
                if unit[0] == "q":
                    nc.vector.scalar_tensor_tensor(
                        QHs[:, p, n, :, :], src.rearrange("p (o t) -> p o t", o=1).broadcast_to([P, SLOTS, T]), bias,
                        sel[:, n, n * SLOTS:(n + 1) * SLOTS].rearrange("p (j o) -> p j o", o=1).broadcast_to([P, SLOTS, T]),
                        ALU.add, ALU.mult)
                if causal and unit[0] == "k":
                    last = nc.scalar.activation(dst, src, ACT.Identity, bias=bias)
                else:
                    last = nc.vector.tensor_scalar(dst, src, bias, None, ALU.add)
            else:
                dst = v_odd[:, :, 0:HD] if unit == "v_odd" else Vs[:, p, n, :, 0:HD]
                src = src[:dst.shape[0], 0:D].rearrange("p (h e) -> p h e", e=HD)
                last = nc.scalar.activation(dst, src, ACT.Copy) if causal else nc.vector.tensor_copy(dst, src)
            last.then_inc(ta.taken[ta.units[ta.at[unit]][1]], 1)
        block = ctx.enter_context(nc.Block())

        @block.sync
        def _(sp):
            for dst, src in ((wq_s, wq), (wk_s, wk), (wv_s, wv)):
                sp.dma_start(dst[:, :, :], src.rearrange("(c p) n -> p c n", p=P)).then_inc(const_in, 16)
            for dst, src in ((bq, bq_in), (bk, bk_in), (ident, ident_in), (own, own_in)):
                sp.dma_start(dst[:, :], src).then_inc(const_in, 16)
            sp.dma_start(bv[:, :, :].rearrange("p h e -> p (h e)"), bv_in.broadcast_to([P, D])).then_inc(const_in, 16)
            for dst, src in ((sel, sel_in), (mask, mask_in), (sums_of, sums_in), (share, share_in)):
                sp.dma_start(dst[:, :, :], src).then_inc(const_in, 16)

            def turn(g, stages, q):
                if "A" in stages:
                    sp.wait_ge(x_free, g + 2)
                    sp.dma_start(xT[:, :, :], xT_in[:, bass.ds((g + 1) * T, T)].rearrange("(c p) t -> p c t", p=P))\
                      .then_inc(loaded, 16)
                if "C" in stages:
                    tc.wait_taken(sp, g - 1, f"share{HG - 1}")
                    dst = aT_out[:, bass.ds((g - 1) * T, T)].rearrange("(g s e) t -> s e g t", g=HG, s=SLOTS)
                    for s in range(SLOTS):
                        sp.dma_start(dst[s], aT[SLOT * s:SLOT * s + HD, :, :]).then_inc(stored, 16)
                if "A" in stages:
                    ta.wait_taken(sp, g + 1, "negmax_T")
                    for j in range(SLOTS):
                        row = SLOT * j + HD
                        sp.dma_start(QHs[row:row + 1, 1 - q, :, j, :], negmax_T[j:HEADS:SLOTS, 1 - q, :]).then_inc(row_in, 16)
            turns(sp, turn)
            sp.wait_ge(stored, 16 * (SLOTS * B + 1))

        @block.tensor
        def _(pe):
            mm = nc.tensor.matmul
            pe.wait_ge(const_in, 16 * n_const)
            pe.wait_ge(ones_made, N_ONES)
            pe.sem_inc(x_free, 1)
            pe.sem_inc(av_done, HEADS)

            def stand():
                pe.sem_inc(passed, 1)

            def turn(g, stages, q):
                p, b = 1 - q, g + 1

                def masked(out, side):
                    for at in (0, 2 * P):
                        last = mm(out[:, at:at + P], ident_b[:, :], mask[:, side, :], start=False, stop=True,
                                  skip_group_check=True)
                    return last

                def form(unit):
                    QT, KT = QTs[:, p], KTs[:, p]
                    if unit == "v_odd":
                        pe.wait_ge(x_odd_ready, b + 1)
                    elif unit in ("odd_key_max", "odd_query_max"):
                        pe.wait_ge(odd_ready, b * N_ODD + 3)
                    elif unit == "negmax_T":
                        pe.wait_ge(max_done, b + 1)
                    elif unit.startswith("max"):
                        ta.wait_taken(pe, b, "k3")
                    out = ta.bank(pe, b, unit)
                    n = int(unit[-1]) if unit[-1].isdigit() else 0
                    if unit[0] in "qk":
                        w = wq_s if unit[0] == "q" else wk_s
                        for c in range(DC):
                            last = mm(out[:, 0:T], w[:, c, n * P:n * P + P], xT[:, c, :], start=c == 0, stop=c == DC - 1)
                    elif unit == "v_odd":
                        for c in range(DC):
                            last = mm(out[:HEADS, 0:D], odd_x[:, c, :], wv_s[:, c, :], start=c == 0, stop=c == DC - 1)
                    elif unit[0] == "v":
                        for c in range(DC):
                            last = mm(out[:, 0:D], xT[:, c, n * P:n * P + P], wv_s[:, c, :], start=c == 0, stop=c == DC - 1)
                    elif unit.startswith("max"):
                        hg, j = divmod(int(unit[3:]), SLOTS)
                        QH = QHs[:, p, hg, j, :]
                        if causal:
                            mm(out[:, 0:P], QH[:, 0:P], KT[:, hg, 0:P], start=True, stop=True,
                               skip_group_check=True)
                            mm(out[:, P:3 * P], QH[:, P:2 * P], KT[:, hg, 0:2 * P], start=False, stop=True,
                               skip_group_check=True)
                            last = masked(out, 0)
                        else:
                            for k in range(2):
                                last = mm(out[:, k * D:k * D + D], QH[:, k * P:k * P + P], KT[:, hg, 0:D],
                                          start=True, stop=True)
                    elif unit == "odd_key_max":
                        for k in range(2):
                            for hg in range(HG):
                                last = mm(out[:, k * HEADS:k * HEADS + HEADS], QT[:, hg, k * P:k * P + P],
                                          K_odds[:, p, hg, :], start=hg == 0, stop=hg == HG - 1)
                    elif unit == "odd_query_max":
                        for hg in range(HG):
                            last = mm(out[:HEADS, 0:T], Q_odds[:, p, hg, :], KT[:, hg, :], start=hg == 0, stop=hg == HG - 1)
                    else:
                        for k in range(2):
                            last = nc.tensor.transpose(out[:HEADS, k * P:k * P + P], negmax[:, k, :], ident[:, :])
                    last.then_inc(ta.ready, 1)

                def scores(h):
                    KT = KTs[:, q]
                    if h == 0:
                        pe.wait_ge(row_in, (g + 1) * 16 * SLOTS)
                    pe.wait_ge(s_taken, g * HEADS + h + 1)
                    stand()
                    hg, j = divmod(h, SLOTS)
                    QH = QHs[:, q, hg, j, :]
                    out = S[:, h % 2, :]
                    if causal:
                        mm(out[:, 0:2 * P], KT[:, hg, 0:P], QH[:, 0:2 * P], start=True, stop=True,
                           skip_group_check=True)
                        mm(out[:, 2 * P:3 * P], KT[:, hg, P:2 * P], QH[:, P:2 * P], start=False, stop=True,
                           skip_group_check=True)
                        last = masked(out, 1)
                    else:
                        for k in range(2):
                            last = mm(out[:, k * D:k * D + D], KT[:, hg, k * P:k * P + P], QH[:, 0:D], start=True,
                                      stop=True)
                    last.then_inc(s_ready, 1)

                def products(g, h, q):
                    wait_weights(pe, g, h)
                    if h == order[0]:
                        pe.wait_ge(o_taken, g + 1)
                        pe.wait_ge(odd_ready, g * N_ODD + 3)
                        if not causal:
                            pe.wait_ge(ow_ready, g + 1)
                            stand()
                            for hg in range(HG):
                                mm(O[:, hg, :], V_odds[:, q, hg * P:hg * P + P], w_ok[:, 0:2 * P], start=hg % 2 == 0,
                                   stop=False, skip_group_check=True)
                    stand()
                    hg, rows = h // SLOTS, slice(SLOT * (h % SLOTS), SLOT * (h % SLOTS) + SLOT)
                    if causal:
                        mm(O[rows, hg, :], Vs[:, q, 0, h, :], W[:, h % NW, 0:2 * P], start=True, stop=False,
                           skip_group_check=True)
                        last = mm(O[rows, hg, P:2 * P], Vs[:, q, 1, h, :], W[:, h % NW, 2 * P:3 * P], start=False,
                                  stop=True, skip_group_check=True)
                    else:
                        for k in range(2):
                            last = mm(O[rows, hg, :], Vs[:, q, k, h, :], W[:, h % NW, k * D:k * D + D], start=False,
                                      stop=k == 1, skip_group_check=True)
                    last.then_inc(av_done, 1)

                for s in range(HEADS):
                    if "A" in stages:
                        if s == 0:
                            pe.wait_ge(loaded, b * 16 + 16)
                        for unit in shares[s]:
                            form(unit)
                        if s == X_FREE:
                            pe.wait_ge(ta.ready, b * len(ta.units) + ta.at["v_odd"] + 1)
                            pe.sem_inc(x_free, 1)
                    if "B" in stages:
                        scores(s)
                        if s == ODD_Q:
                            out = tb.bank(pe, g, "odd_query")
                            pe.wait_ge(odd_ready, g * N_ODD + 4)
                            stand()
                            for k in range(2):
                                for hg in range(HG):
                                    mm(out[:, k * HEADS:k * HEADS + HEADS], KTs[:, q, hg, k * P:k * P + P],
                                       Q_odds[:, q, hg, :], start=hg == 0, stop=False)
                                last = mm(out[:, k * HEADS:k * HEADS + HEADS], ones[:, :], diag_odd[:, q, :],
                                          start=False, stop=True)
                            last.then_inc(tb.ready, 1)
                        if s == ODD_K:
                            out = tb.bank(pe, g, "odd_key")
                            for hg in range(HG):
                                mm(out[:HEADS, 0:nq], K_odds[:, q, hg, :], QTs[:, q, hg, T - nq:T], start=hg == 0,
                                   stop=False)
                            last = mm(out[:HEADS, 0:nq], ident[:HEADS, :HEADS], negmax_T[:, q, T - nq:T], start=False,
                                      stop=True)
                            last.then_inc(tb.ready, 1)
                        if s == ODD_OUT:
                            out = tb.bank(pe, g, "odd_out")
                            pe.wait_ge(ow_ready, g + 1)
                            pe.wait_ge(odd_ready, g * N_ODD + 3)
                            stand()
                            for hg in range(HG):
                                at = hg * (HEADS + 1)
                                for k in range(2):
                                    mm(out[:, at:at + HEADS],
                                       Vs[:, q, k, hg * SLOTS:hg * SLOTS + SLOTS, :].rearrange("p h e -> p (h e)"),
                                       w_oq[:, k * HEADS:k * HEADS + HEADS], start=k == 0, stop=k == 1)
                                last = mm(out[:, at + HEADS:at + HEADS + 1], V_odds[:, q, hg * P:hg * P + P],
                                          w_ok[:, nq - 1:nq], start=True, stop=True)
                            last.then_inc(tb.ready, 1)
                        for h in PRODUCTS[causal].get(s, ()):
                            products(g, h, q)
                    if "C" in stages:
                        for h in PRODUCTS[causal].get(s + HEADS, ()):
                            products(g - 1, h, 1 - q)
                    if "C" in stages and s in PASS_OUT:
                        unit = PASS_OUT[s]
                        if unit == "sums":
                            out = tc.bank(pe, g - 1, unit)
                            pe.wait_ge(ot_copied, g)
                            stand()
                            for hg in range(HG):
                                last = mm(out[:HEADS, 0:T], sums_of[:, hg, :], OT[:, hg, :], start=hg == 0,
                                          stop=hg == HG - 1)
                        else:
                            out = tc.bank(pe, g - 1, unit)
                            last = mm(out[:, 0:T], share[:, int(unit[-1]), :], inv[:, :], start=True, stop=True)
                        last.then_inc(tc.ready, 1)
            turns(pe, turn)

        @block.scalar
        def _(act):
            A = nc.scalar.activation
            act.wait_ge(const_in, 16 * n_const)
            for track in (ta, tb, tc):
                track.open({"act": act})
            act.sem_inc(stored, 16)
            act.sem_inc(s_taken, 2)
            act.wait_ge(ones_made, N_ONES)
            for who, heads in made.items():
                act.sem_inc(w_ready[who], len(heads))
            act.sem_inc(ln_ready, len(LN_HEADS))

            def wait_logs(g, h):
                row = [h % HEADS in LN_HEADS[s] for s in sorted(LN_HEADS)].index(True)
                act.wait_ge(ln_ready, (g + h // HEADS) * len(LN_HEADS) + row + 1 + len(LN_HEADS))

            def turn(g, stages, q):
                p, b = 1 - q, g + 1

                def factors(u, y, x, rows):
                    A(u, x, ACT.Identity, scale=-SCALE, bias=one_less[:rows, :])
                    return A(y, x, ACT.Square, scale=-SCALE, bias=one_more[:rows, :])

                def logs(g, s):
                    for h in LN_HEADS.get(s, ()):
                        act.wait_ge(t_ready, g * HEADS + h + 1)
                        wait_multiplied(act, g, h - NW)
                        last = A(W[:, h % NW, :], U[:, h % NW, :], ACT.Ln)
                    if s == ODD_LN:
                        act.wait_ge(ot_ready, g + 1)
                        act.wait_ge(o_taken, g + 1)
                        A(w_oq[:, :], u_oq[:, :], ACT.Ln)
                        last = A(w_ok[:, :], u_ok[:, :], ACT.Ln)
                    if s in LN_HEADS:
                        last.then_inc(ln_ready, 1)

                def exponentials(g, s):
                    if s in LN_HEADS:
                        wait_logs(g, LN_HEADS[s][0])
                        for h in LN_HEADS[s]:
                            A(W[:, h % NW, :], W[:, h % NW, :], ACT.Exp, scale=-1.0).then_inc(w_ready["act"], 1)
                    if s == ODD_LN:
                        A(w_oq[:, :], w_oq[:, :], ACT.Exp, scale=-1.0)
                        A(w_ok[:, :], w_ok[:, :], ACT.Exp, scale=-1.0).then_inc(ow_ready, 1)

                for s in range(HEADS):
                    if "A" in stages:
                        for unit in shares[s]:
                            if ta.units[ta.at[unit]][1] == "act":
                                take_projected(act, unit, b, p)
                    if "B" in stages:
                        if s < HEADS:
                            n = g * HEADS + s
                            act.wait_ge(s_ready, n + 1)
                            at = s % NW
                            if causal:
                                wait_multiplied(act, g, s - NW)
                                A(W[:, at, 0:width], S[:, s % 2, 0:width], ACT.Exp, scale=SCALE).then_inc(w_ready["act"], 1)
                                wait_weights(act, g, s)
                                act.sem_inc(s_taken, 1)
                            else:
                                if maker[(s - NW) % HEADS] == "dve":
                                    wait_weights(act, g, s - NW)
                                else:
                                    wait_logs(g, s - NW)
                                factors(U[:, at, :], Y[:, at, :], S[:, s % 2, :], P).then_inc(y_ready, 1)
                                act.wait_ge(y_ready, n + 1)
                                act.sem_inc(s_taken, 1)
                        if not causal:
                            logs(g, s)
                            exponentials(g, s - 1)
                        if s == ODD_Q:
                            src = tb.full(act, g, "odd_query")[:, 0:2 * HEADS]
                            act.wait_ge(tb.taken["dve"], g + 1)
                            if causal:
                                A(w_oq[:, :], src, ACT.Exp, scale=SCALE).then_inc(tb.taken["act"], 1)
                            else:
                                factors(u_oq[:, :], y_oq[:, :], src, P).then_inc(tb.taken["act"], 1)
                        if s == ODD_K:
                            src = tb.full(act, g, "odd_key")[:HEADS, 0:nq]
                            if causal:
                                A(w_ok[:, 0:nq], src, ACT.Exp, scale=SCALE).then_inc(tb.taken["act"], 1)
                                tb.wait_taken(act, g, "odd_key")
                                act.sem_inc(ow_ready, 1)
                            else:
                                factors(u_ok[:, :], y_ok[:, :], src, HEADS).then_inc(tb.taken["act"], 1)
                    if "C" in stages and not causal:
                        logs(g - 1, s + HEADS)
                        exponentials(g - 1, s + HEADS - 1)
            turns(act, turn)

        @block.vector
        def _(dve):
            v = nc.vector
            dve.wait_ge(const_in, 16 * n_const)
            for track in (ta, tb, tc):
                track.open({"dve": dve})
            dve.sem_inc(o_taken, 1)

            def turn(g, stages, q):
                p, b = 1 - q, g + 1
                links_a, links_b = Chain(dve, chain_a, LINKS_A[causal], b), Chain(dve, chain_b, LINKS_B[causal], g)
                links_c = Chain(dve, chain_c, 1, g - 1)

                def take(unit):
                    if unit[0] in "qkv":
                        return take_projected(dve, unit, b, p)
                    taken = ta.taken["dve"]
                    src = ta.full(dve, b, unit)
                    if unit.startswith("max"):
                        h = int(unit[3:])
                        if causal:
                            v.tensor_reduce(negmax[:, 0, h:h + 1], src[:, 0:P], AX.X, ALU.max, negate=True)
                            last = v.tensor_reduce(negmax[:, 1, h:h + 1], src[:, P:3 * P], AX.X, ALU.max, negate=True)
                        else:
                            last = v.tensor_reduce(negmax[:, :, h], src[:, :].rearrange("p (k n) -> p k n", k=2), AX.X,
                                                   ALU.max, negate=True)
                        last.then_inc(taken, 1)
                        if causal and h == HEADS - 1:
                            ta.wait_taken(dve, b, unit)
                            dve.sem_inc(max_done, 1)
                    elif unit == "odd_key_max":
                        ta.wait_taken(dve, b, f"max{HEADS - 1}")
                        both = negmax[:, :, :].rearrange("p k h -> p (k h)")
                        links_a.link(v.scalar_tensor_tensor(both, src[:, 0:2 * HEADS], -1.0, both, ALU.mult, ALU.min))
                        dve.sem_inc(taken, 1)
                        dve.sem_inc(max_done, 1)
                    elif unit == "odd_query_max":
                        v.tensor_reduce(negmax_T[:, p, ODD:T], src[:HEADS, 0:T], AX.X, ALU.max, negate=True).then_inc(taken, 1)
                    else:
                        v.tensor_copy(negmax_T[:, p, 0:2 * P], src[:HEADS, 0:2 * P]).then_inc(taken, 1)

                def cubic(u, y):
                    return v.scalar_tensor_tensor(u, y, REST, u, ALU.add, ALU.mult)

                for s in range(HEADS):
                    if "C" in stages and s == COPY_OUT:
                        dve.wait_ge(tc.taken["dve"], (g - 1) * (HG + 1) + 1)
                        dve.wait_ge(av_done, (g - 1) * HEADS + 2 * HEADS)
                        v.tensor_copy(OT[:, :, 0:2 * P], O[:, :, :])
                        links_c.link(v.tensor_copy(OT[:, :, ODD:T], oq_sum[:, :].rearrange("p (g o) -> p g o", o=1)))
                        dve.sem_inc(o_taken, 1)
                        dve.sem_inc(ot_copied, 1)
                    if "A" in stages:
                        for unit in shares[s]:
                            if ta.units[ta.at[unit]][1] == "dve":
                                take(unit)
                    if "C" in stages and s in PASS_OUT:
                        unit = PASS_OUT[s]
                        src = tc.full(dve, g - 1, unit)
                        if unit == "sums":
                            v.reciprocal(inv[:, :], src[:HEADS, 0:T]).then_inc(tc.taken["dve"], 1)
                        else:
                            if unit == "share0":
                                dve.wait_ge(stored, (g - 1) * 16 * SLOTS + 16)
                            hg = int(unit[-1])
                            v.tensor_tensor(aT[:, hg, :], OT[:, hg, :], src[:, 0:T], ALU.mult).then_inc(tc.taken["dve"], 1)
                    if "B" not in stages:
                        continue
                    n = g * HEADS + s
                    if not causal:
                        if s < HEADS:
                            dve.wait_ge(y_ready, n + 1)
                            cubic(U[:, s % NW, :], Y[:, s % NW, :]).then_inc(t_ready, 1)
                        if 1 <= s <= HEADS:
                            if maker[s - 1] == "dve":
                                dve.wait_ge(t_ready, n)
                                wait_multiplied(dve, g, s - 1 - NW)
                                v.reciprocal(W[:, (s - 1) % NW, :], U[:, (s - 1) % NW, :]).then_inc(w_ready["dve"], 1)
                        if s == ODD_W:
                            tb.wait_taken(dve, g, "odd_key")
                            cubic(u_oq[:, :], y_oq[:, :])
                            cubic(u_ok[:, :], y_ok[:, :]).then_inc(ot_ready, 1)
                    if s == ODD_OUT:
                        src = tb.full(dve, g, "odd_out")[:, 0:HG * (HEADS + 1)]
                        links_b.link(v.tensor_tensor(oq[:, :, :], src.rearrange("p (g h) -> p g h", g=HG), sel_one[:, :, :],
                                                     ALU.mult))
                        dve.sem_inc(tb.taken["dve"], 1)
                        links_b.link(v.tensor_reduce(oq_sum[:, :], oq[:, :, :], AX.X, ALU.add))
                for stage, links in (("A", links_a), ("B", links_b), ("C", links_c)):
                    if stage in stages:
                        links.done()
            turns(dve, turn)

        @block.gpsimd
        def _(pool):
            g_ = nc.gpsimd
            g_.memset(Vs[:, :, :, :, :], 0.0).then_inc(ones_made, 1)
            g_.memset(v_odd[:, :, :], 0.0).then_inc(ones_made, 1)
            g_.memset(sel_one[:, :, :], 1.0).then_inc(ones_made, 1)
            pool.wait_ge(ones_made, 3)
            for q in range(2):
                g_.memset(Vs[:, q, :, :, HD:VC], 1.0).then_inc(ones_made, 1)
            g_.memset(v_odd[:, :, HD:VC], 1.0).then_inc(ones_made, 1)
            g_.memset(ones[:, :], 1.0).then_inc(ones_made, 1)
            g_.memset(one_less[:, :], 1.0 - ROOT).then_inc(ones_made, 1)
            g_.memset(one_more[:, :], 1.0 + ROOT / 2).then_inc(ones_made, 1)
            pool.wait_ge(const_in, 16 * n_const)
            g_.tensor_copy(ident_b[:, :], ident[:, :]).then_inc(ones_made, 1)
            g_.tensor_copy(sel_one[:, :, 0:HEADS], sel[:, :, :]).then_inc(ones_made, 1)
            pool.wait_ge(ones_made, N_ONES)

            def turn(g, stages, q):
                if "A" not in stages:
                    return
                p, b = 1 - q, g + 1

                def of_heads(dst, src):
                    return g_.tensor_tensor(dst[:, p, :, :], src[:, p, :, ODD:T].broadcast_to([P, HG, HEADS]), sel[:, :, :],
                                            ALU.mult)
                pool.wait_ge(loaded, b * 16 + 16)
                pool.sem_inc(ones_made, 1)
                g_.tensor_copy(odd_x[:, :, :], xT[:, :, ODD:T].broadcast_to([P, DC, HEADS])).then_inc(x_odd_ready, 1)
                ta.wait_taken(pool, b, "v_odd")
                of_heads(K_odds, KTs)
                of_heads(Q_odds, QTs).then_inc(odd_ready, 1)
                if causal:
                    for k in range(2):
                        g_.tensor_tensor(Vs[:, p, k, :, 0:HD], Vs[:, p, k, :, 0:HD], bv[:, :, :], ALU.add)
                    g_.tensor_tensor(v_odd[:, :, 0:HD], v_odd[:, :, 0:HD], bv[:HEADS, :, :], ALU.add)\
                        .then_inc(odd_ready, 1)
                else:
                    pool.sem_inc(odd_ready, 1)
                pool.wait_ge(odd_ready, b * N_ODD + 2)
                g_.tensor_tensor(V_odds[:, p, :], v_odd[:, :, :].rearrange("k h e -> k (h e)"), own[:, :], ALU.mult).then_inc(odd_ready, 1)
                ta.wait_taken(pool, b, "odd_query_max")
                g_.tensor_tensor(diag_odd[:, p, :], ident[:HEADS, :HEADS],
                                 negmax_T[:, p, ODD:T].broadcast_to([HEADS, HEADS]), ALU.mult).then_inc(odd_ready, 1)
            turns(pool, turn)


def enter_attention(nc, cT_in, h_in, wout_in, gamma_in, beta_in, ident_in, hx_out, x_out, xT_out):
    ctx = ExitStack()
    with ctx:
        r = Room(nc, ctx, "mid")
        ident, wout = r.sb("ident", [P, P]), r.sb("wout", [P, DC, D])
        gamma, beta = r.sb("gamma", [P, DC]), r.sb("beta", [P, DC])
        cT, h = r.sb("cT", [P, 2, DC, GROUP]), r.sb("h", [P, 2, 4, D])
        h1, x, hx, xn = (r.sb(n, [P, 2, 4, D]) for n in ("h1", "x", "hx", "xn"))
        xt = r.sb("xt", [P, 2, DC, GROUP])
        stats, mv = r.sb("stats", [P, 4, 6]), r.sb("mv", [P, 4, 2])
        ve, rstd, minus_half = r.sb("ve", [P, 4]), r.sb("rstd", [P, 4]), r.sb("mh", [P, 4])
        out_ps = r.ps("out", [P, 2, 4, D])
        tp = r.ps("tp", [P, 2, DC, GROUP])
        const_in, inputs_free = r.sem("const_in"), r.sem("inputs_free")
        loaded, rows_stored, stored = ([r.sem(f"{n}{q}") for q in range(2)] for n in ("loaded", "rows_stored", "stored"))
        const_made, chained, var_ready, rstd_ready = r.sem("const_made"), r.sem("chained"), r.sem("var"), r.sem("rstds")
        out_ready, out_taken = r.sem("out_ready"), r.sem("out_taken")
        xn_ready, tp_ready, xt_ready = r.sem("xn_ready"), r.sem("tp_ready"), r.sem("xt_ready")
        rows_ready = r.sem("rows_ready")
        block = ctx.enter_context(nc.Block())

        @block.sync
        def _(sp):
            sp.dma_start(ident[:, :], ident_in).then_inc(const_in, 16)
            sp.dma_start(wout[:, :, :], wout_in.rearrange("(c p) n -> p c n", p=P)).then_inc(const_in, 16)
            sp.dma_start(gamma[:, :], gamma_in).then_inc(const_in, 16)
            sp.dma_start(beta[:, :], beta_in).then_inc(const_in, 16)

            def step(t0, g, tiles, rows, q):
                sp.wait_ge(inputs_free, g + 1)
                sp.wait_ge(out_ready, g + 1)
                sp.dma_start(cT[:, q, :, 0:tiles * rows], cT_in[:, bass.ds(t0, tiles * rows)]
                             .rearrange("(c p) t -> p c t", p=P)).then_inc(loaded[q], 16)
                sp.dma_start(h[:rows, q, 0:tiles, :], tokens(h_in, t0, tiles, rows)).then_inc(loaded[q], 16)
            groups(sp, step)

        @block.tensor
        def _(pe):
            pe.sem_inc(tp_ready, 2)
            pe.sem_inc(out_ready, 2)
            pe.wait_ge(const_in, 64)

            def step(t0, g, tiles, rows, q):
                pe.wait_ge(loaded[q], (g - q) * 16 + 32)
                pe.wait_ge(out_taken, g + 1)
                for j in range(tiles):
                    for c in range(DC):
                        last = nc.tensor.matmul(out_ps[:rows, q, j, :], cT[:, q, c, j * P:j * P + rows], wout[:, c, :],
                                                start=c == 0, stop=c == DC - 1)
                last.then_inc(out_ready, 1)
                pe.wait_ge(xt_ready, g + 1)
                pe.wait_ge(xn_ready, g + 1)
                transposed(nc, tp[:, q], xn[:, q], ident, tiles, rows).then_inc(tp_ready, 1)
            groups(pe, step)

        @block.vector
        def _(dve):
            v = nc.vector
            dve.sem_inc(inputs_free, 2)
            dve.sem_inc(out_taken, 2)

            def step(t0, g, tiles, rows, q):
                chain = Chain(dve, chained, 8, g)
                h1_, x_, hx_, xn_ = h1[:, q], x[:, q], hx[:, q], xn[:, q]
                dve.wait_ge(out_ready, g + 3)
                dve.wait_ge(rows_stored[q], (g - q) * 16 + 32)
                v.tensor_tensor(h1_[:rows, 0:tiles, :], h[:rows, q, 0:tiles, :], out_ps[:rows, q, 0:tiles, :], ALU.add)\
                    .then_inc(out_taken, 1)
                dve.wait_ge(out_taken, g + 3)
                dve.sem_inc(inputs_free, 1)
                statistics(v, chain, h1_, stats, mv, ve, tiles, rows, LN_EPS).then_inc(var_ready, 1)
                dve.wait_ge(rstd_ready, 2 * g + 1)
                dve.wait_ge(var_ready, 2 * g + 1)
                chain.link_apart(normalise(v, h1_, x_, mv, rstd, tiles, rows))
                statistics(v, chain, x_, stats, mv, ve, tiles, rows, LN_EPS).then_inc(var_ready, 1)
                v.tensor_tensor(hx_[:rows, 0:tiles, :], h1_[:rows, 0:tiles, :], x_[:rows, 0:tiles, :], ALU.add)\
                    .then_inc(rows_ready, 1)
                dve.wait_ge(rstd_ready, 2 * g + 2)
                dve.wait_ge(var_ready, 2 * g + 2)
                dve.wait_ge(tp_ready, g + 1)
                normalise(v, x_, xn_, mv, rstd, tiles, rows).then_inc(xn_ready, 1)
                chain.done()
            groups(dve, step)

        @block.gpsimd
        def _(pool):
            nc.gpsimd.memset(minus_half[:, :], -0.5).then_inc(const_made, 1)
            pool.wait_ge(const_made, 1)

            def step(t0, g, tiles, rows, q):
                for n in range(2):
                    pool.wait_ge(var_ready, 2 * g + n + 1)
                    nc.gpsimd.tensor_tensor(rstd[:rows, 0:tiles], ve[:rows, 0:tiles], minus_half[:rows, 0:tiles],
                                            ALU.pow).then_inc(rstd_ready, 1)
            groups(pool, step)

        @block.scalar
        def _(act):
            act.sem_inc(xt_ready, 2)
            for q in range(2):
                act.sem_inc(stored[q], 16)
                act.sem_inc(rows_stored[q], 32)
            act.wait_ge(const_in, 64)

            def step(t0, g, tiles, rows, q):
                act.wait_ge(stored[q], (g - q) * 8 + 16)
                act.wait_ge(tp_ready, g + 3)
                n = tiles * rows
                for c in range(DC):
                    last = nc.scalar.activation(xt[:, q, c, 0:n], tp[:, q, c, 0:n], ACT.Identity, bias=beta[:, c:c + 1],
                                                scale=gamma[:, c:c + 1])
                last.then_inc(xt_ready, 1)
                act.wait_ge(xt_ready, g + 3)
                act.dma_start(xT_out[:, bass.ds(t0, n)].rearrange("(c p) t -> p c t", p=P),
                              xt[:, q, :, 0:n]).then_inc(stored[q], 16)
                act.wait_ge(rows_ready, g + 1)
                act.dma_start(tokens(hx_out, t0, tiles, rows), hx[:rows, q, 0:tiles, :]).then_inc(rows_stored[q], 16)
                act.dma_start(tokens(x_out, t0, tiles, rows), x[:rows, q, 0:tiles, :]).then_inc(rows_stored[q], 16)
            groups(act, step)
            for q in range(2):
                act.wait_ge(rows_stored[q], 32 * (NGROUPS // 2 + 2 - q))
                act.wait_ge(stored[q], 16 * (NGROUPS // 2 + 2 - q))


EXPERTS, HIDDEN = 8, 4 * D
MOE_LINKS, MOE_OUT_LINKS = 17, 3
HB = HIDDEN // P


def experts(nc, aT_in, x_in, hx_in, wp_in, bp_in, gamma_in, beta_in, gate_w_in, gate_b_in, w1_in, b1_in, w2_in, b2_in,
            ident_in, h_out, xT_out):
    ctx = ExitStack()
    with ctx:
        r = Room(nc, ctx, "moe")
        ident, wp, bp = r.sb("ident", [P, P]), r.sb("wp", [P, DC, D]), r.sb("bp", [P, D])
        gamma, beta = r.sb("gamma", [P, DC]), r.sb("beta", [P, DC])
        gate_w, gate_b = r.sb("gate_w", [P, DC, EXPERTS]), r.sb("gate_b", [P, EXPERTS])
        w1, w2 = r.sb("w1", [P, EXPERTS, DC, HIDDEN]), r.sb("w2", [P, EXPERTS, HB, D])
        b1, b2 = r.sb("b1", [P, EXPERTS, HB]), r.sb("b2", [EXPERTS, D])
        aT, x, xn = r.sb("aT", [P, DC, EG]), r.sb("x", [P, 2, D]), r.sb("xn", [P, 2, D])
        xo, xt = r.sb("xo", [P, 2, D]), r.sb("xt", [P, DC, EG])
        accs, mTs = r.sb("acc", [P, 2, 2, D]), r.sb("mT", [P, 2, DC, EG])
        w_fulls, wTs = r.sb("w_full", [P, 2, 2, EXPERTS]), r.sb("wT", [EXPERTS, 2, EG])
        mid = r.sb("mid", [P, 2, HB, EG])
        stats, mv = r.sb("stats", [P, 2, 6]), r.sb("mv", [P, 2, 2])
        ve, rstd, minus_half = r.sb("ve", [P, 2]), r.sb("rstd", [P, 2]), r.sb("mh", [P, 2])
        stats_o, mv_o, ve_o, rstd_o = (r.sb(n, s) for n, s in (("stats_o", [P, 2, 6]), ("mv_o", [P, 2, 2]), ("ve_o", [P, 2]),
                                                               ("rstd_o", [P, 2])))
        logits, top, index = r.sb("logits", [P, 2, EXPERTS]), r.sb("top", [P, 2, 8]), r.sb("index", [P, 2, 8], U32)
        index_f, iota = r.sb("index_f", [P, 2, 8]), r.sb("iota", [P, EXPERTS])
        gap, second, total = r.sb("gap", [P, 2]), r.sb("second", [P, 2]), r.sb("total", [P, 2])
        wa, wb, one_hot = r.sb("wa", [P, 2]), r.sb("wb", [P, 2]), r.sb("one_hot", [P, 2, EXPERTS])
        hid = r.ps("hid", [P, 2, 512])
        y = r.ps("y", [P, 2, 2, D])
        ahead, behind = r.ps("ahead", [P, 2, EG]), r.ps("behind", [P, DC, EG])
        const_in, w_in, const_made, loaded, loaded_hx = (r.sem(n) for n in ("const_in", "w_in", "const_made", "loaded", "loaded_hx"))
        a_free, x_free, proj_ready, proj_taken = r.sem("a_free"), r.sem("x_free"), r.sem("proj_ready"), r.sem("proj_taken")
        chain_a, chain_b, var_ready, rstd_ready, xn_ready = (r.sem(n) for n in ("chain_a", "chain_b", "var", "rstds", "xn"))
        var_o_ready, rstd_o_ready, xo_ready = r.sem("var_o"), r.sem("rstd_o_ready"), r.sem("xo_ready")
        tp_ready, m_ready, gate_ready, gap_ready, exp_ready = (r.sem(n) for n in ("tp_ready", "m_ready", "gate", "gap", "exp"))
        w_ready, wT_ready, wT_taken = r.sem("w_ready"), r.sem("wT_ready"), r.sem("wT_taken")
        hid_ready, mid_ready, y_ready, y_taken = r.sem("hid_ready"), r.sem("mid_ready"), r.sem("y_ready"), r.sem("y_taken")
        out_ready, xt_ready = r.sem("out_ready"), r.sem("xt_ready")
        h_stored, stored, passed = r.sem("h_stored"), r.sem("stored"), r.sem("passed")
        h_ready, sp_passed = r.sem("h_ready"), r.sem("sp_passed")
        YU = EXPERTS + 1
        PE_AT = {"proj": 0, "m": 4, "gate": 5, "wT": EXPERTS, "out": 2}
        DVE_AT = {"leave": 0, "out": 1, "x3": 2, "norm": 3, "best": 6, "weights": 7}
        EXP_AT = 6
        block = ctx.enter_context(nc.Block())

        def shape_of(kind):
            return (1, TAIL) if kind == "tail" else (2, P)

        def turns(engine, turn):
            turn(-1, None, "full", None, 1)
            turn(0, "full", "full", None, 0)
            with engine.Fori(0, EGROUPS // 2 - 1) as n:
                turn(2 * n + 1, "full", "full", "full", 1)
                turn(2 * n + 2, "full", "full", "full", 0)
            turn(EGROUPS - 1, "full", "tail", "full", 1)
            turn(EGROUPS, "tail", None, "full", 0)
            turn(EGROUPS + 1, None, None, "tail", 1)

        @block.sync
        def _(sp):
            for dst, src in ((wp, wp_in), (gate_w, gate_w_in)):
                sp.dma_start(dst[:, :, :], src.rearrange("(c p) n -> p c n", p=P)).then_inc(const_in, 16)
            for dst, src in ((ident, ident_in), (gamma, gamma_in), (beta, beta_in), (b2, b2_in)):
                sp.dma_start(dst[:, :], src).then_inc(const_in, 16)
            sp.dma_start(bp[:, :], bp_in.broadcast_to([P, D])).then_inc(const_in, 16)
            sp.dma_start(gate_b[:, :], gate_b_in.broadcast_to([P, EXPERTS])).then_inc(const_in, 16)
            sp.dma_start(b1[:, :, :], b1_in).then_inc(const_in, 16)

            def turn(g, main, ahead_, behind_, q):
                if ahead_:
                    a = g + 1
                    tiles, rows = shape_of(ahead_)
                    n = tiles * rows
                    sp.wait_ge(a_free, a + 1)
                    sp.sem_inc(sp_passed, 1)
                    sp.wait_ge(x_free, a + 1)
                    sp.sem_inc(sp_passed, 1)
                    sp.dma_start(aT[:, :, 0:n], aT_in[:, bass.ds(a * EG, n)].rearrange("(c p) t -> p c t", p=P)).then_inc(loaded, 16)
                    sp.dma_start(x[:rows, 0:tiles, :], tokens(x_in, a * EG, tiles, rows)).then_inc(loaded, 16)
                    sp.wait_ge(h_stored, a * 16 + 16)
                    sp.sem_inc(sp_passed, 1)
                    sp.wait_ge(xo_ready, a + 1)
                    sp.sem_inc(sp_passed, 1)
                    sp.dma_start(accs[:rows, 1 - q, 0:tiles, :], tokens(hx_in, a * EG, tiles, rows)).then_inc(loaded_hx, 16)
                if not main and ahead_:
                    for e in range(EXPERTS):
                        sp.dma_start(w1[:, e, :, :], w1_in[:, e, :, :]).then_inc(w_in, 16)
                        sp.dma_start(w2[:, e, :, :], w2_in[:, e, :, :]).then_inc(w_in, 16)
            turns(sp, turn)

        @block.tensor
        def _(pe):
            mm = nc.tensor.matmul
            pe.sem_inc(a_free, 1)
            pe.sem_inc(y_ready, 2)
            pe.wait_ge(const_in, 16 * 9)

            def stand():
                pe.sem_inc(passed, 1)

            def turn(g, main, ahead_, behind_, q):
                m_tiles, m_rows = shape_of(main)
                mn = m_tiles * m_rows
                a, p = g + 1, 1 - q

                def hidden(e, hb):
                    u = e * HB + hb
                    pe.wait_ge(mid_ready, g * EXPERTS * HB + u + 1)
                    for c in range(DC):
                        last = mm(hid[:, u % 2, 0:mn], w1[:, e, c, hb * P:hb * P + P], mTs[:, q, c, 0:mn], start=c == 0,
                                  stop=c == DC - 1)
                    last.then_inc(hid_ready, 1)

                def out(e):
                    pe.wait_ge(mid_ready, g * EXPERTS * HB + (e + 1) * HB + 2)
                    pe.wait_ge(y_taken, g * YU + e + 2)
                    for j in range(m_tiles):
                        for hb in range(HB):
                            last = mm(y[:m_rows, (e + 1) % 2, j, :], mid[:, e % 2, hb, j * P:j * P + m_rows],
                                      w2[:, e, hb, :], start=hb == 0, stop=hb == HB - 1)
                    last.then_inc(y_ready, 1)

                for s in range(EXPERTS + 1):
                    if main and s < EXPERTS:
                        if s == 0:
                            pe.wait_ge(m_ready, g + 1)
                            stand()
                        if s == 0 and not behind_:
                            pe.wait_ge(w_in, 32 * EXPERTS)
                        for hb in range(HB):
                            hidden(s, hb)
                    if ahead_:
                        tiles, rows = shape_of(ahead_)
                        if s == PE_AT["proj"]:
                            pe.wait_ge(loaded, a * 32 + 32)
                            pe.wait_ge(wT_taken, a + 1)
                            for j in range(tiles):
                                for c in range(DC):
                                    last = mm(ahead[:rows, j, :], aT[:, c, j * P:j * P + rows], wp[:, c, :],
                                              start=c == 0, stop=c == DC - 1)
                            last.then_inc(proj_ready, 1)
                            pe.wait_ge(proj_ready, a + 1)
                            pe.sem_inc(a_free, 1)
                        if s == PE_AT["m"]:
                            pe.wait_ge(proj_taken, a + 1)
                            pe.wait_ge(xn_ready, a + 1)
                            transposed(nc, ahead, xn, ident, tiles, rows).then_inc(tp_ready, 1)
                        if s == PE_AT["gate"]:
                            pe.wait_ge(m_ready, a + 1)
                            stand()
                            for j in range(tiles):
                                for c in range(DC):
                                    last = mm(ahead[:rows, 0, j * EXPERTS:(j + 1) * EXPERTS], mTs[:, p, c, j * P:j * P + rows],
                                              gate_w[:, c, :], start=c == 0, stop=c == DC - 1)
                            last.then_inc(gate_ready, 1)
                        if s == PE_AT["wT"]:
                            pe.wait_ge(w_ready, a + 1)
                            stand()
                            for j in range(tiles):
                                last = nc.tensor.transpose(ahead[:EXPERTS, 1, j * P:j * P + rows], w_fulls[:rows, p, j, :],
                                                           ident[:rows, :rows])
                            last.then_inc(wT_ready, 1)
                    if behind_ and s == PE_AT["out"]:
                        tiles, rows = shape_of(behind_)
                        pe.wait_ge(xo_ready, g + 2)
                        pe.wait_ge(xt_ready, g)
                        transposed(nc, behind, xo, ident, tiles, rows).then_inc(out_ready, 1)
                    if main and s == 1:
                        pe.wait_ge(wT_taken, g + 2)
                        pe.wait_ge(y_taken, g * YU + 2)
                        stand()
                        for j in range(m_tiles):
                            last = mm(y[:m_rows, 0, j, :], wTs[:, q, j * P:j * P + m_rows], b2[:, :], start=True, stop=True)
                        last.then_inc(y_ready, 1)
                    if main and s >= 1:
                        out(s - 1)
            turns(pe, turn)

        @block.scalar
        def _(act):
            A = nc.scalar.activation
            act.sem_inc(mid_ready, 2)
            act.sem_inc(wT_taken, 1)
            act.sem_inc(xt_ready, 1)
            act.sem_inc(stored, 16)
            act.wait_ge(const_in, 16 * 9)

            def turn(g, main, ahead_, behind_, q):
                m_tiles, m_rows = shape_of(main)
                mn = m_tiles * m_rows
                a, p = g + 1, 1 - q
                for s in range(EXPERTS + 1):
                    if main and s < EXPERTS:
                        act.wait_ge(y_ready, g * YU + (s + 2 if s >= 2 else s + 1))
                        for hb in range(HB):
                            u = s * HB + hb
                            act.wait_ge(hid_ready, g * EXPERTS * HB + u + 1)
                            A(mid[:, s % 2, hb, 0:mn], hid[:, u % 2, 0:mn], ACT.Gelu, bias=b1[:, s, hb:hb + 1])\
                                .then_inc(mid_ready, 1)
                    if ahead_:
                        tiles, rows = shape_of(ahead_)
                        n = tiles * rows
                        if s == PE_AT["m"]:
                            act.wait_ge(tp_ready, a + 1)
                            for c in range(DC):
                                last = A(mTs[:, p, c, 0:n], ahead[:, c, 0:n], ACT.Identity, bias=beta[:, c:c + 1],
                                         scale=gamma[:, c:c + 1])
                            last.then_inc(m_ready, 1)
                        if s == EXP_AT:
                            act.wait_ge(gap_ready, a + 1)
                            A(second[:rows, 0:tiles], gap[:rows, 0:tiles], ACT.Exp).then_inc(exp_ready, 1)
                        if s == PE_AT["wT"]:
                            act.wait_ge(wT_ready, a + 1)
                            A(wTs[:, p, 0:n], ahead[:EXPERTS, 1, 0:n], ACT.Copy).then_inc(wT_taken, 1)
                    if behind_:
                        z = g - 1
                        tiles, rows = shape_of(behind_)
                        n = tiles * rows
                        if s == DVE_AT["leave"]:
                            act.wait_ge(h_ready, z + 1)
                            act.dma_start(tokens(h_out, z * EG, tiles, rows), accs[:rows, p, 0:tiles, :]).then_inc(h_stored, 16)
                        if s == PE_AT["out"]:
                            act.wait_ge(out_ready, z + 1)
                            act.wait_ge(stored, z * 16 + 16)
                            A(xt[:, :, 0:n], behind[:, :, 0:n], ACT.Copy).then_inc(xt_ready, 1)
                            act.wait_ge(xt_ready, z + 2)
                            act.dma_start(xT_out[:, bass.ds(z * EG, n)].rearrange("(c p) t -> p c t", p=P),
                                          xt[:, :, 0:n]).then_inc(stored, 16)
            turns(act, turn)
            act.wait_ge(stored, 16 * (EGROUPS + 2))
            act.wait_ge(h_stored, 16 * (EGROUPS + 3))

        @block.vector
        def _(dve):
            v = nc.vector
            dve.sem_inc(x_free, 1)
            dve.sem_inc(y_taken, 2)
            dve.sem_inc(xo_ready, 2)
            dve.wait_ge(const_made, 3)
            dve.wait_ge(const_in, 16 * 9)

            def turn(g, main, ahead_, behind_, q):
                m_tiles, m_rows = shape_of(main)
                a, p, z = g + 1, 1 - q, g - 1
                links_a, links_b = Chain(dve, chain_a, MOE_LINKS, a), Chain(dve, chain_b, MOE_OUT_LINKS, z)
                link = links_a.link

                def unit(e):
                    acc = accs[:, q]
                    dve.wait_ge(y_ready, g * YU + e + 2 + 2)
                    for j in range(m_tiles):
                        src = y[:m_rows, (e + 1) % 2, j, :]
                        if e < 0:
                            last = v.tensor_tensor(acc[:m_rows, j, :], acc[:m_rows, j, :], src, ALU.add)
                        else:
                            last = v.scalar_tensor_tensor(acc[:m_rows, j, :], src, w_fulls[:m_rows, q, j, e:e + 1],
                                                          acc[:m_rows, j, :], ALU.mult, ALU.add)
                    last.then_inc(y_taken, 1)
                    dve.wait_ge(y_taken, g * YU + e + 2 + 2)

                for s in range(EXPERTS + 1):
                    if behind_:
                        tiles, rows = shape_of(behind_)
                        if s == DVE_AT["leave"]:
                            dve.sem_inc(h_ready, 1)
                            statistics(v, links_b, accs[:, p], stats_o, mv_o, ve_o, tiles, rows, LN_EPS).then_inc(var_o_ready, 1)
                        if s == DVE_AT["out"]:
                            dve.wait_ge(rstd_o_ready, z + 1)
                            dve.wait_ge(xt_ready, z + 1)
                            normalise(v, accs[:, p], xo, mv_o, rstd_o, tiles, rows).then_inc(xo_ready, 1)
                            links_b.done()
                    if ahead_:
                        tiles, rows = shape_of(ahead_)
                        t_ = slice(0, tiles)
                        w_full = w_fulls[:, p]
                        if s == DVE_AT["x3"]:
                            dve.wait_ge(loaded_hx, a * 16 + 16)
                            dve.wait_ge(proj_ready, a + 1)
                            bias = bp[:rows, :].rearrange("p (a d) -> p a d", a=1).broadcast_to([rows, tiles, D])
                            link(v.tensor_tensor(xn[:rows, t_, :], ahead[:rows, t_, :], bias, ALU.add))
                            dve.sem_inc(proj_taken, 1)
                            acc = accs[:, p]
                            v.tensor_tensor(acc[:rows, t_, :], acc[:rows, t_, :], xn[:rows, t_, :], ALU.add)
                            links_a.link_apart(v.tensor_tensor(x[:rows, t_, :], x[:rows, t_, :], xn[:rows, t_, :], ALU.add))
                            statistics(v, links_a, x, stats, mv, ve, tiles, rows, LN_EPS).then_inc(var_ready, 1)
                        if s == DVE_AT["norm"]:
                            dve.wait_ge(rstd_ready, a + 1)
                            normalise(v, x, xn, mv, rstd, tiles, rows).then_inc(xn_ready, 1)
                            dve.wait_ge(xn_ready, a + 1)
                            dve.sem_inc(x_free, 1)
                        if s == DVE_AT["best"]:
                            dve.wait_ge(gate_ready, a + 1)
                            bias = gate_b[:rows, :].rearrange("p (a d) -> p a d", a=1).broadcast_to([rows, tiles, EXPERTS])
                            links_a.link_apart(v.tensor_tensor(logits[:rows, t_, :], ahead[:rows, 0, 0:tiles * EXPERTS]
                                                               .rearrange("p (j e) -> p j e", e=EXPERTS), bias, ALU.add))
                            for j in range(tiles):
                                last = v.max(top[:rows, j, :], logits[:rows, j, :])
                            links_a.link_apart(last)
                            for j in range(tiles):
                                last = v.max_index(index[:rows, j, :], top[:rows, j, :], logits[:rows, j, :])
                            v.tensor_tensor(gap[:rows, t_], top[:rows, t_, 1], top[:rows, t_, 0], ALU.subtract)\
                                .then_inc(gap_ready, 1)
                            link(last)
                            link(v.tensor_copy(index_f[:rows, t_, :], index[:rows, t_, :]))
                        if s == DVE_AT["weights"]:
                            dve.wait_ge(exp_ready, a + 1)
                            link(v.tensor_scalar(total[:rows, t_], second[:rows, t_], 1.0, None, ALU.add))
                            link(v.reciprocal(wa[:rows, t_], total[:rows, t_]))
                            link(v.tensor_tensor(wb[:rows, t_], wa[:rows, t_], second[:rows, t_], ALU.mult))
                            for j in range(tiles):
                                v.tensor_scalar(one_hot[:rows, j, :], iota[:rows, :], index_f[:rows, j, 1:2],
                                                wb[:rows, j:j + 1], ALU.is_equal, ALU.mult)
                                last = v.tensor_scalar(w_full[:rows, j, :], iota[:rows, :], index_f[:rows, j, 0:1],
                                                       wa[:rows, j:j + 1], ALU.is_equal, ALU.mult)
                            link(last)
                            link(v.tensor_tensor(w_full[:rows, t_, :], w_full[:rows, t_, :], one_hot[:rows, t_, :], ALU.add))
                            dve.sem_inc(w_ready, 1)
                            links_a.done()
                    if main and s >= 1:
                        if s == 1:
                            unit(-1)
                        unit(s - 1)
            turns(dve, turn)

        @block.gpsimd
        def _(pool):
            nc.gpsimd.memset(minus_half[:, :], -0.5).then_inc(const_made, 1)
            nc.gpsimd.iota(iota[:, :], [[1, EXPERTS]], base=0, channel_multiplier=0, allow_small_or_imprecise_dtypes=True)\
                .then_inc(const_made, 1)
            pool.wait_ge(const_made, 2)
            pool.sem_inc(const_made, 1)
            pool.sem_inc(h_stored, 32)

            def turn(g, main, ahead_, behind_, q):
                if behind_:
                    tiles, rows = shape_of(behind_)
                    pool.wait_ge(var_o_ready, g)
                    nc.gpsimd.tensor_tensor(rstd_o[:rows, 0:tiles], ve_o[:rows, 0:tiles], minus_half[:rows, 0:tiles],
                                            ALU.pow).then_inc(rstd_o_ready, 1)
                if ahead_:
                    tiles, rows = shape_of(ahead_)
                    pool.wait_ge(var_ready, g + 2)
                    nc.gpsimd.tensor_tensor(rstd[:rows, 0:tiles], ve[:rows, 0:tiles], minus_half[:rows, 0:tiles],
                                            ALU.pow).then_inc(rstd_ready, 1)
            turns(pool, turn)

PH, PK = 8, 8
NKEYS = 64
JB = NKEYS // 2
SUB = 16
LAG = 5
NHID = 8
ROUTE_LINKS = 61
PE_AT = {"proj": 0, "tp": 7, "sims": (8, 12), "fields": (17, 25), "scatter": ((21, 24, 26, 27), (29, 30, 31, 33))}
DVE_AT = {"h": 1, "x": 3, "xn": 4, "pick": ((8, 9, 10, 11, 12, 13, 14), (15, 16, 17, 19, 20, 22, 22)),
          "one_hot": ((18, 21, 24, 25), (26, 27, 28, 30))}


def product_keys(nc, aT_in, h_in, wout_in, bout_in, norm_w_in, w_q_in, keys_in, down_in, up_in, ident_in, h_out):
    ctx = ExitStack()
    with ctx:
        r = Room(nc, ctx, "peer")
        ident, wout, bout = r.sb("ident", [P, P]), r.sb("wout", [P, DC, D]), r.sb("bout", [P, D])
        norm_w = r.sb("norm_w", [P, DC])
        down, up = r.sb("down", [P, DC, JB, P]), r.sb("up", [P, JB, D])
        simw = r.sb("simw", [P, DC, 2 * PH * NKEYS])
        G = r.sb("G", [P, 2, JB, EG])
        G_flat = G[:, :, :, :].rearrange("p g a b -> p (g a b)")
        w_q = G_flat[:, 0:16 * D].rearrange("p (a b) -> p a b", a=16)
        keys = G_flat[:, 16 * D:16 * D + 16 * NKEYS].rearrange("p (a b) -> p a b", a=16)
        hin = r.sb("hin", [P, 2, D])
        aT, xnT = r.sb("aT", [P, DC, EG]), r.sb("xnT", [P, 2, DC, EG])
        h, x = r.sb("h", [P, 2, 2, D]), r.sb("x", [P, 2, D])
        stats, mv = r.sb("stats", [P, 2, 6]), r.sb("mv", [P, 2, 2])
        ve, rstd, minus_half, m2 = (r.sb(n, [P, 2]) for n in ("ve", "rstd", "mh", "m2"))
        best, best_i = r.sb("best", [P, 2 * PH, 8]), r.sb("best_i", [P, 2 * PH, 8], U32)
        best_if = r.sb("best_if", [P, 2 * PH, 8])
        sums = r.sb("sums", [P, PH, 8, 8])
        fs, pk = r.sb("fs", [P, PH, PK]), r.sb("pk", [P, PH * PK], U32)
        pk_u, pk_f = r.sb("pk_u", [P, 2, PH * PK], U32), r.sb("pk_f", [P, 2, PH * PK])
        picked = r.sb("picked", [P, PH, PK, 8])
        j_f, j_u, j_parts, par = r.sb("j_f", [P, 64]), r.sb("j_u", [P, 64], U32), r.sb("j_parts", [P, 2, 64], U32), r.sb("par", [P, 64])
        fields = r.sb("fields", [P, 4, 64])
        FT = r.sb("FT", [P, 2, 4, 64])
        iota = r.sb("iota", [P, NKEYS])
        eq = r.sb("eq", [P, 2, SUB, NKEYS])
        iota_j = r.sb("iota_j", [P, 2 * JB])
        one_i, one_j = r.sb("one_i", [P, 2, SUB, 2, NKEYS]), r.sb("one_j", [P, 2, SUB, 2 * JB])
        hid = r.sb("hid", [P, NHID, EG])
        route = r.ps("route", [P, 2, 512])
        turned = r.ps("turned", [P, 512])
        work = r.ps("work", [P, 2, 512])
        total = r.ps("total", [P, 2, D])
        scat = r.ps("scat", [P, 2, SUB // 2, 2 * JB])
        const_in, const_made, loaded, a_free, h_stored = (r.sem(n) for n in ("const_in", "const_made", "loaded", "a_free", "h_stored"))
        simw_ready, simw_taken = r.sem("simw_ready"), r.sem("simw_taken")
        proj_ready, proj_taken, chained, var_ready, rstd_ready = (r.sem(n) for n in ("proj", "proj_taken", "chained", "var", "rstds"))
        xn_ready, tp_ready, tp_taken = r.sem("xn"), r.sem("tp"), r.sem("tp_taken")
        sims_ready, sims_taken, fields_ready, f_ready, f_taken = (r.sem(n) for n in ("sims", "sims_taken", "fields_r", "f", "f_taken"))
        one_ready, eq_ready, odd_ready, scat_ready, scat_taken = r.sem("one"), r.sem("eq_r"), r.sem("odd"), r.sem("scat_r"), r.sem("scat_taken")
        hid_ready, gelu_ready, gated, up_done = r.sem("hid_r"), r.sem("gelu"), r.sem("gated"), r.sem("up_done")
        out_taken, passed, sp_passed = r.sem("out_taken"), r.sem("passed"), r.sem("sp_passed")
        h_free = r.sem("h_free")
        dve_passed, pool_passed = r.sem("dve_passed"), r.sem("pool_passed")
        N_CONST = 9
        block = ctx.enter_context(nc.Block())

        def shape_of(is_tail):
            return (1, TAIL, 1, TAIL) if is_tail else (2, P, 2, P // 2)

        def turns(engine, turn):
            turn(-1, None, "full", 1)
            with engine.Fori(0, EGROUPS - 2, 2) as g:
                turn(g, "full", "full", 0)
                turn(g + 1, "full", "full", 1)
            turn(EGROUPS - 2, "full", "full", 0)
            turn(EGROUPS - 1, "full", "tail", 1)
            turn(EGROUPS, "tail", None, 0)

        @block.sync
        def _(sp):
            sp.dma_start(w_q, w_q_in).then_inc(const_in, 16)
            sp.dma_start(keys, keys_in).then_inc(const_in, 16)
            sp.dma_start(wout[:, :, :], wout_in.rearrange("(c p) n -> p c n", p=P)).then_inc(const_in, 16)
            sp.dma_start(ident[:, :], ident_in).then_inc(const_in, 16)
            sp.dma_start(bout[:, :], bout_in.broadcast_to([P, D])).then_inc(const_in, 16)
            sp.dma_start(norm_w[:, :], norm_w_in).then_inc(const_in, 16)
            for c in range(DC):
                sp.dma_start(down[:, c, :, :], down_in[:, c, :, :]).then_inc(const_in, 16)
            sp.dma_start(up[:, :, :], up_in).then_inc(const_in, 16)

            def turn(g, blocks, routing, q):
                if routing is None:
                    return
                tiles, rows, _, _ = shape_of(routing == "tail")
                ga, n = g + 1, tiles * rows
                sp.wait_ge(a_free, ga + 1)
                sp.sem_inc(sp_passed, 1)
                sp.wait_ge(h_free, ga + 1)
                sp.sem_inc(sp_passed, 1)
                sp.dma_start(aT[:, :, 0:n], aT_in[:, bass.ds(ga * EG, n)].rearrange("(c p) t -> p c t", p=P))\
                  .then_inc(loaded, 16)
                sp.dma_start(hin[:rows, 0:tiles, :], tokens(h_in, ga * EG, tiles, rows)).then_inc(loaded, 16)
            turns(sp, turn)

        @block.tensor
        def _(pe):
            mm = nc.tensor.matmul
            pe.sem_inc(a_free, 1)
            pe.sem_inc(scat_ready, 4)
            pe.sem_inc(up_done, NHID)
            pe.wait_ge(const_in, 16 * N_CONST)
            for c in range(DC):
                for half in range(2):
                    for n in range(PH):
                        s = half * PH + n
                        last = mm(route[:, half, n * NKEYS:(n + 1) * NKEYS], w_q[:, s, c * P:c * P + P], keys[:, s, :],
                                  start=True, stop=True)
                last.then_inc(simw_ready, 1)
                pe.wait_ge(simw_taken, c + 1)

            def stand():
                pe.sem_inc(passed, 1)

            def turn(g, blocks, routing, q):
                tiles, rows, halves, tt = shape_of(routing == "tail")
                b_tiles, b_rows, _, _ = shape_of(blocks == "tail")
                nb = b_tiles * b_rows
                ga, b = g + 1, 1 - q
                for jj in range(JB + LAG):
                    if blocks and jj < JB:
                        pe.wait_ge(gelu_ready, g * JB + jj + 1)
                        if jj == 0:
                            pe.wait_ge(tp_taken, g + 1)
                            stand()
                        for c in range(DC):
                            last = mm(work[:, jj % 2, 0:nb], down[:, c, jj, :], xnT[:, q, c, 0:nb], start=c == 0,
                                      stop=c == DC - 1)
                        last.then_inc(hid_ready, 1)
                    if routing and jj == PE_AT["proj"]:
                        pe.wait_ge(loaded, ga * 32 + 32)
                        pe.wait_ge(sims_taken, ga * 2 + 1)
                        stand()
                        for j in range(tiles):
                            for c in range(DC):
                                last = mm(route[:rows, 0, j * D:j * D + D], aT[:, c, j * P:j * P + rows],
                                          wout[:, c, :], start=c == 0, stop=c == DC - 1)
                        last.then_inc(proj_ready, 1)
                        pe.wait_ge(proj_ready, ga + 1)
                        pe.sem_inc(a_free, 1)
                    if routing and jj == PE_AT["tp"]:
                        pe.wait_ge(proj_taken, ga + 1)
                        pe.wait_ge(xn_ready, ga + 1)
                        for c in range(DC):
                            for j in range(tiles):
                                last = nc.tensor.transpose(route[:, 0, c * EG + j * P:c * EG + j * P + rows],
                                                           x[:rows, j, c * P:c * P + P], ident[:rows, :rows])
                        last.then_inc(tp_ready, 1)
                    for j in range(tiles if routing else 0):
                        t = ga * 2 + j
                        if jj == PE_AT["sims"][j]:
                            pe.wait_ge(tp_taken, ga + 1)
                            pe.wait_ge(sims_taken, t + 1)
                            stand()
                            for half in range(2):
                                for c in range(DC):
                                    last = mm(route[:rows, half, :], xnT[:, b, c, j * P:j * P + rows],
                                              simw[:, c, half * 512:half * 512 + 512], start=c == 0, stop=c == DC - 1)
                            last.then_inc(sims_ready, 1)
                        if jj == PE_AT["fields"][j]:
                            pe.wait_ge(fields_ready, t + 1)
                            pe.wait_ge(f_taken, t + 1)
                            stand()
                            for half in range(halves):
                                part = slice(64 * half, 64 * half + tt)
                                for f in range(4):
                                    last = mm(turned[64 * half:64 * half + 64, f * 64:f * 64 + tt], fields[part, f, :],
                                              ident[part, part], start=True, stop=True)
                            last.then_inc(f_ready, 1)
                        if jj in PE_AT["scatter"][j][:tt // SUB]:
                            s = PE_AT["scatter"][j].index(jj)
                            u = t * 4 + s
                            q_ = 64 * halves
                            pe.wait_ge(one_ready, u + 1)
                            pe.wait_ge(odd_ready, u + 1)
                            for k in range(SUB):
                                bank, at = divmod(k, SUB // 2)
                                if at == 0:
                                    pe.wait_ge(scat_taken, u * 2 + bank + 1)
                                    stand()
                                last = mm(scat[:, bank, at, :], one_i[:q_, s % 2, k, :, :].rearrange("p a i -> p (a i)"),
                                          one_j[:q_, s % 2, k, :], start=True, stop=True)
                                if at == SUB // 2 - 1:
                                    last.then_inc(scat_ready, 1)
                    if blocks and jj >= LAG:
                        e = jj - LAG
                        pe.wait_ge(gated, g * JB + e + 1)
                        if e == 0:
                            pe.wait_ge(out_taken, g + 1)
                            stand()
                        for j in range(b_tiles):
                            last = mm(total[:b_rows, j, :], hid[:, e % NHID, j * P:j * P + b_rows], up[:, e, :],
                                      start=e == 0 and j == 0, stop=e == JB - 1, skip_group_check=True)
                        last.then_inc(up_done, 1)
            turns(pe, turn)

        @block.scalar
        def _(act):
            A = nc.scalar.activation
            act.sem_inc(gelu_ready, 2)
            act.sem_inc(f_taken, 1)
            act.sem_inc(scat_taken, 2)
            act.sem_inc(h_stored, 32)
            act.wait_ge(const_in, 16 * N_CONST)
            for c in range(DC):
                act.wait_ge(simw_ready, c + 1)
                A(simw[:, c, :].rearrange("p (a b) -> p a b", a=2), route[:, :, :], ACT.Copy).then_inc(simw_taken, 1)

            def turn(g, blocks, routing, q):
                tiles, rows, halves, tt = shape_of(routing == "tail")
                b_tiles, b_rows, _, _ = shape_of(blocks == "tail")
                nb, n = b_tiles * b_rows, tiles * rows
                ga, b = g + 1, 1 - q
                for jj in range(JB + LAG):
                    if blocks and jj < JB:
                        act.wait_ge(hid_ready, g * JB + jj + 1)
                        act.wait_ge(up_done, g * JB + jj + 1)
                        A(hid[:, jj % NHID, 0:nb], work[:, jj % 2, 0:nb], ACT.Gelu).then_inc(gelu_ready, 1)
                    if routing and jj == PE_AT["tp"]:
                        act.wait_ge(tp_ready, ga + 1)
                        for c in range(DC):
                            last = A(xnT[:, b, c, 0:n], route[:, 0, c * EG:c * EG + n], ACT.Copy, scale=norm_w[:, c:c + 1])
                        last.then_inc(tp_taken, 1)
                    for j in range(tiles if routing else 0):
                        t = ga * 2 + j
                        if jj == PE_AT["fields"][j]:
                            act.wait_ge(f_ready, t + 1)
                            src = turned[:64 * halves, 0:256].rearrange("p (f t) -> p f t", f=4)[:, :, 0:tt]
                            A(FT[:64 * halves, j, :, 0:tt], src, ACT.Copy).then_inc(f_taken, 1)
                        if jj in PE_AT["scatter"][j][:tt // SUB]:
                            s = PE_AT["scatter"][j].index(jj)
                            for bank in range(2):
                                act.wait_ge(scat_ready, (t * 4 + s) * 2 + bank + 5)
                                at = j * P + s * SUB + bank * (SUB // 2)
                                to = G[:, b, :, at:at + SUB // 2] if halves == 1 else \
                                    G[:, b, :, j * P:j * P + P].rearrange("p j (h t) -> p j h t", h=2)[:, :, :, at - j * P:at - j * P + SUB // 2]
                                if halves == 1:
                                    A(to.rearrange("p j t -> p t j"), scat[:, bank, :, 0:JB], ACT.Copy).then_inc(scat_taken, 1)
                                else:
                                    A(to.rearrange("p j h t -> p t h j"), scat[:, bank, :, :].rearrange("p t (h j) -> p t h j", h=2),
                                      ACT.Copy).then_inc(scat_taken, 1)
                if blocks:
                    act.wait_ge(out_taken, g + 2)
                    act.dma_start(tokens(h_out, g * EG, b_tiles, b_rows), h[:b_rows, q, 0:b_tiles, :]).then_inc(h_stored, 16)
            turns(act, turn)
            act.wait_ge(h_stored, 16 * (EGROUPS + 3))

        @block.vector
        def _(dve):
            v = nc.vector
            dve.sem_inc(sims_taken, 1)
            dve.sem_inc(out_taken, 1)
            dve.sem_inc(h_free, 1)
            dve.wait_ge(const_made, 5)
            dve.wait_ge(const_in, 16 * N_CONST)

            def pick(step, t, link, link_apart, rows):
                R = slice(0, rows)
                flat = sums[R].rearrange("p h a b -> p h (a b)")
                sims = route[R, :, :].rearrange("p a (h s k) -> p (a h s) k", s=2, k=NKEYS)
                eight = iota[R, 0:8].rearrange("p (o a) -> p o a", o=1).broadcast_to([rows, 64, 8])
                num = best_if[R, :, :].rearrange("p (h s) k -> p h s k", s=2)

                def number(side, dst):
                    where = pk_f[R, side, :].rearrange("p (k o) -> p k o", o=1).broadcast_to([rows, 64, 8])
                    link(v.tensor_tensor(picked[R].rearrange("p h k a -> p (h k) a"), where, eight, ALU.is_equal))
                    link(v.tensor_tensor(picked[R], picked[R], num[:, :, side, :].rearrange("p h (o a) -> p h o a", o=1)
                                         .broadcast_to([rows, PH, PK, 8]), ALU.mult))
                    link(v.tensor_reduce(dst, picked[R].rearrange("p h k a -> p (h k) a"), AX.X, ALU.add))

                if step == 0:
                    dve.wait_ge(sims_ready, t + 1)
                    dve.sem_inc(dve_passed, 1)
                    for s in range(2 * PH):
                        last = v.max(best[R, s, :], sims[:, s, :])
                    link_apart(last)
                elif step == 1:
                    for s in range(2 * PH):
                        last = v.max_index(best_i[R, s, :], best[R, s, :], sims[:, s, :])
                    link(last)
                    dve.sem_inc(sims_taken, 1)
                    v.tensor_copy(best_if[R], best_i[R])
                elif step == 2:
                    s1 = best[R, :, :].rearrange("p (h s) k -> p h s k", s=2)
                    b1 = s1[:, :, 0, :].rearrange("p h (k o) -> p h k o", o=1).broadcast_to([rows, PH, 8, 8])
                    b2 = s1[:, :, 1, :].rearrange("p h (o k) -> p h o k", o=1).broadcast_to([rows, PH, 8, 8])
                    link_apart(v.tensor_tensor(sums[R], b1, b2, ALU.add))
                    for h_ in range(PH):
                        last = v.max(fs[R, h_, :], flat[:, h_, :])
                    link_apart(last)
                elif step == 3:
                    for h_ in range(PH):
                        last = v.max_index(pk[R, h_ * PK:(h_ + 1) * PK], fs[R, h_, :], flat[:, h_, :])
                    link(last)
                    v.tensor_scalar(pk_u[R, 0, :], pk[R, :], 3, None, ALU.logical_shift_right)
                    link(v.tensor_scalar(pk_u[R, 1, :], pk[R, :], 7, None, ALU.bitwise_and))
                    link(v.tensor_copy(pk_f[R], pk_u[R]))
                elif step == 4:
                    number(0, fields[R, 0, :])
                elif step == 5:
                    number(1, j_f[R, :])
                else:
                    link(v.tensor_copy(j_u[R, :], j_f[R, :]))
                    v.tensor_scalar(j_parts[R, 0, :], j_u[R, :], 1, None, ALU.logical_shift_right)
                    link(v.tensor_scalar(j_parts[R, 1, :], j_u[R, :], 1, None, ALU.bitwise_and))
                    v.tensor_copy(fields[R, 1, :], j_parts[R, 0, :])
                    link(v.tensor_copy(par[R, :], j_parts[R, 1, :]))
                    weight = fs[R].rearrange("p h k -> p (h k)")
                    link(v.scalar_tensor_tensor(fields[R, 3, :], weight, 0.0, par[R, :], ALU.max, ALU.mult))
                    v.scalar_tensor_tensor(fields[R, 2, :], weight, 0.0, fields[R, 3, :], ALU.max, ALU.subtract)\
                        .then_inc(fields_ready, 1)

            def one_hot(s, t, j, link, halves):
                q = 64 * halves
                at = slice(s * SUB, (s + 1) * SUB)

                def wide(f, n):
                    return FT[:q, j, f, at].rearrange("p (t o) -> p t o", o=1).broadcast_to([q, SUB, n])

                def numbers(row, n):
                    return row[:q, 0:n].rearrange("p (o i) -> p o i", o=1).broadcast_to([q, SUB, n])
                if s == 0:
                    dve.wait_ge(f_taken, t + 2)
                dve.wait_ge(scat_ready, (t * 4 + s) * 2 + 2)
                link(v.tensor_tensor(eq[:q, s % 2], wide(0, NKEYS), numbers(iota, NKEYS), ALU.is_equal))
                dve.sem_inc(eq_ready, 1)
                v.tensor_tensor(one_j[:q, s % 2], wide(1, 2 * JB), numbers(iota_j, 2 * JB), ALU.is_equal)
                v.tensor_tensor(one_i[:q, s % 2, :, 0, :], eq[:q, s % 2], wide(2, NKEYS), ALU.mult).then_inc(one_ready, 1)

            def turn(g, blocks, routing, q):
                tiles, rows, halves, tt = shape_of(routing == "tail")
                b_tiles, b_rows, _, _ = shape_of(blocks == "tail")
                nb = b_tiles * b_rows
                ga, b = g + 1, 1 - q
                chain = Chain(dve, chained, ROUTE_LINKS, ga)
                link = chain.link
                R, t_ = slice(0, rows), slice(0, tiles)
                for jj in range(JB):
                    if blocks:
                        dve.wait_ge(gelu_ready, g * JB + jj + 3)
                        if jj == 0:
                            dve.wait_ge(scat_taken, g * 16 + (18 if blocks == "full" else 4))
                        v.tensor_tensor(hid[:, jj % NHID, 0:nb], hid[:, jj % NHID, 0:nb], G[:, q, jj, 0:nb], ALU.mult)\
                            .then_inc(gated, 1)
                    if not routing:
                        continue
                    if jj == DVE_AT["h"]:
                        dve.wait_ge(loaded, ga * 32 + 32)
                        bias = bout[R, :].rearrange("p (a d) -> p a d", a=1).broadcast_to([rows, tiles, D])
                        hb = h[:, b]
                        dve.wait_ge(h_stored, ga * 16 + 16)
                        link(v.tensor_tensor(hb[R, t_, :], hin[R, t_, :], bias, ALU.add))
                        dve.sem_inc(h_free, 1)
                        dve.wait_ge(proj_ready, ga + 1)
                        proj = route[R, 0, :].rearrange("p (k d) -> p k d", k=2)[:, t_, :]
                        chain.link_apart(v.tensor_tensor(hb[R, t_, :], hb[R, t_, :], proj, ALU.add))
                        dve.sem_inc(proj_taken, 1)
                        statistics(v, chain, hb, stats, mv, ve, tiles, rows, LN_EPS).then_inc(var_ready, 1)
                    if jj == DVE_AT["x"]:
                        dve.wait_ge(rstd_ready, 2 * ga + 1)
                        chain.link_apart(normalise(v, h[:, b], x, mv, rstd, tiles, rows))
                        link(statistics(v, chain, x, stats, mv, ve, tiles, rows, RMS_EPS))
                        link(v.tensor_tensor(m2[R, t_], mv[R, t_, 0], mv[R, t_, 0], ALU.mult))
                        v.tensor_tensor(ve[R, t_], ve[R, t_], m2[R, t_], ALU.add).then_inc(var_ready, 1)
                    if jj == DVE_AT["xn"]:
                        dve.wait_ge(rstd_ready, 2 * ga + 2)
                        for j in range(tiles):
                            last = v.tensor_scalar(x[R, j, :], x[R, j, :], rstd[R, j:j + 1], None, ALU.mult)
                        last.then_inc(xn_ready, 1)
                    for j in range(tiles):
                        t = ga * 2 + j
                        for step, at in enumerate(DVE_AT["pick"][j]):
                            if at == jj:
                                pick(step, t, link, chain.link_apart, rows)
                        if jj in DVE_AT["one_hot"][j][:tt // SUB]:
                            one_hot(DVE_AT["one_hot"][j].index(jj), t, j, link, halves)
                if blocks:
                    dve.wait_ge(up_done, g * JB + JB + NHID)
                    v.tensor_tensor(h[:b_rows, q, 0:b_tiles, :], h[:b_rows, q, 0:b_tiles, :], total[:b_rows, 0:b_tiles, :],
                                    ALU.add).then_inc(out_taken, 1)
                assert routing != "full" or chain.count == ROUTE_LINKS, chain.count
            turns(dve, turn)

        @block.gpsimd
        def _(pool):
            nc.gpsimd.memset(minus_half[:, :], -0.5).then_inc(const_made, 1)
            nc.gpsimd.iota(iota[:, :], [[1, NKEYS]], base=0, channel_multiplier=0, allow_small_or_imprecise_dtypes=True)\
                .then_inc(const_made, 1)
            pool.wait_ge(const_made, 2)
            for half in range(2):
                nc.gpsimd.iota(iota_j[64 * half:64 * half + 64, :], [[1, 2 * JB]], base=-JB * half, channel_multiplier=0,
                               allow_small_or_imprecise_dtypes=True).then_inc(const_made, 1)
            pool.wait_ge(const_made, 4)
            pool.sem_inc(const_made, 1)

            def turn(g, blocks, routing, q):
                if routing is None:
                    return
                tiles, rows, halves, tt = shape_of(routing == "tail")
                for n in range(2):
                    pool.wait_ge(var_ready, 2 * (g + 1) + n + 1)
                    nc.gpsimd.tensor_tensor(rstd[:rows, 0:tiles], ve[:rows, 0:tiles], minus_half[:rows, 0:tiles],
                                            ALU.pow).then_inc(rstd_ready, 1)
                n = 64 * halves
                for j in range(tiles):
                    for s in range(tt // SUB):
                        t = (g + 1) * 2 + j
                        pool.wait_ge(eq_ready, t * 4 + s + 1)
                        pool.sem_inc(pool_passed, 1)
                        nc.gpsimd.tensor_tensor(
                            one_i[:n, s % 2, :, 1, :], eq[:n, s % 2],
                            FT[:n, j, 3, s * SUB:(s + 1) * SUB].rearrange("p (t o) -> p t o", o=1).broadcast_to([n, SUB, NKEYS]),
                            ALU.mult).then_inc(odd_ready, 1)
            turns(pool, turn)


def padded_heads(w, axis):
    w = np.moveaxis(np.asarray(w), axis, 0)
    out = np.zeros((HEADS, SLOT) + w.shape[1:], w.dtype)
    out[:, :HD] = w.reshape((HEADS, HD) + w.shape[1:])
    return np.ascontiguousarray(np.moveaxis(out.reshape((HEADS * SLOT,) + w.shape[1:]), 0, axis))


def on_slots(vec):
    return np.ascontiguousarray(vec.reshape(HG, P).T)


def constants():
    p = np.arange(P)
    head = np.arange(HEADS)
    gamma = np.array([1.0 - 2.0 ** (-5 - 8 * i // HEADS) for i in range(HEADS)], np.float32)
    query = np.concatenate([np.arange(T), np.arange(P, T)])
    key = np.concatenate([np.zeros(T, np.int64), np.full(T - P, P)])[None, :] + p[:, None]
    diff = query[None, :] - key
    power = gamma[None, :, None] ** np.maximum(diff, 0).astype(np.float32)[:, None, :]
    decay = np.where(diff[:, None, :] >= 0, power * np.float32(SCALE), np.float32(0)).astype(np.float32)
    col = np.arange(HEADS * SLOT)
    own = (col[None, :] // SLOT == head[:, None]).astype(np.float32)
    sel = (head[None, None, :] == SLOTS * np.arange(HG)[None, :, None] + (p // SLOT)[:, None, None]).astype(np.float32)
    avg = ((p[:, None] // SLOT == p[None, :] // SLOT) & (p[:, None] % SLOT < HD)).astype(np.float32) / HD
    valid = p[None, :] <= p[:, None]
    mask = np.where(np.stack([valid, valid.T], 1), 0.0, BIG).astype(mybir.dt.np(BF16))
    aug = np.zeros((HEADS, HG, P), np.float32)
    aug[head, head // SLOTS, SLOT * (head % SLOTS) + HD] = 1
    ones_row = np.zeros((HEADS, SLOT), np.float32)
    ones_row[:, HD] = 1
    return {"mask": mask, "sums_of": np.ascontiguousarray(aug.T), "share": np.ascontiguousarray(sel.T), "ones_row": ones_row.reshape(-1), "ident": np.eye(P, dtype=np.float32), "decay": decay, "own": own, "sel": sel, "avg": avg.astype(np.float32)}


def laid_out(inputs):
    a = {k: np.asarray(v) for k, v in inputs.items()}
    c = constants()
    tight = np.ascontiguousarray

    def by_state(m):
        return m.reshape(PAIRS, 2, 64).transpose(1, 2, 0).reshape(P, PAIRS)

    def column(vec):
        return tight(vec.reshape(DC, P).T)

    def head_weight(w):
        return padded_heads(w.transpose(1, 0, 2).reshape(D, D), 1)

    def slots(vec):
        return on_slots(padded_heads(vec, 0))

    b_ri, qkv, zero = a["L0_tok_B_ri"], a["L1_attn_w_qkv"], np.zeros(D, np.float32)
    down = a["L1_ffn_expert_down"].reshape(NKEYS, JB, 2, DC, P)
    up = a["L1_ffn_expert_up"].reshape(NKEYS, JB, 2, D)
    return {
        "cls_tok": a["cls_tok"].reshape(1, D),
        "log_dt": tight(a["L0_tok_log_dt"].reshape(PAIRS, 2).T),
        "inv_A_real": tight(by_state(a["L0_tok_inv_A_real"])),
        "A_imag": tight(by_state(a["L0_tok_A_imag"])),
        "B_ri": tight(np.stack([by_state(b_ri[..., 0]), by_state(b_ri[..., 1])], 1)),
        "C_ri": tight(a["x"].reshape(B, PAIRS, 2, 64, 2).transpose(2, 3, 4, 1, 0).reshape(P, 2, PAIRS, B)),
        "ret_wq": head_weight(a["L0_attn_Wq"]), "ret_wk": head_weight(a["L0_attn_Wk"]),
        "ret_wv": head_weight(a["L0_attn_Wv"]),
        "ret_gnw": slots(a["L0_attn_gn_weight"]), "ret_gnb": slots(a["L0_attn_gn_bias"]),
        "ret_wout": a["L0_attn_Wout"],
        "ln1_g": column(a["L0_ffn_ln1_g"]), "ln1_b": column(a["L0_ffn_ln1_b"]),
        "ln2_g": column(a["L0_ffn_ln2_g"]), "ln2_b": column(a["L0_ffn_ln2_b"]),
        "soft_wq": padded_heads(a["L0_ffn_Wq"], 1), "soft_wk": padded_heads(a["L0_ffn_Wk"], 1),
        "soft_wv": a["L0_ffn_Wv"], "soft_bq": slots(a["L0_ffn_bq"]),
        "soft_bk": on_slots(np.where(c["ones_row"] > 0, c["ones_row"], padded_heads(a["L0_ffn_bk"], 0))),
        "soft_bv": a["L0_ffn_bv"].reshape(1, D), "soft_wp": a["L0_ffn_Wp"], "soft_bp": a["L0_ffn_bp"].reshape(1, D),
        "gate_w": a["L0_ffn_gate_W"], "gate_b": a["L0_ffn_gate_b"].reshape(1, EXPERTS),
        "moe_w1": tight(a["L0_ffn_exp_W1"].reshape(EXPERTS, DC, P, HIDDEN).transpose(2, 0, 1, 3)),
        "moe_b1": tight(a["L0_ffn_exp_b1"].reshape(EXPERTS, HB, P).transpose(2, 0, 1)),
        "moe_w2": tight(a["L0_ffn_exp_W2"].reshape(EXPERTS, HB, P, D).transpose(2, 0, 1, 3)),
        "moe_b2": a["L0_ffn_exp_b2"],
        "stable_wq": padded_heads(tight(qkv[:D].T), 1), "stable_wk": padded_heads(tight(qkv[D:2 * D].T), 1),
        "stable_wv": tight(qkv[2 * D:].T), "stable_bq": on_slots(padded_heads(zero, 0)),
        "stable_bk": on_slots(c["ones_row"]), "stable_bv": zero.reshape(1, D),
        "stable_wout": tight(a["L1_attn_w_out"].T), "stable_bout": a["L1_attn_b_out"].reshape(1, D),
        "norm_w": column(a["L1_ffn_norm_w"]),
        "peer_w_q": tight(a["L1_ffn_w_q"].reshape(2 * PH, P, D).transpose(1, 0, 2)),
        "peer_keys": tight(a["L1_ffn_keys"].transpose(3, 0, 2, 1).reshape(P, 2 * PH, NKEYS)),
        "peer_down": tight(down.transpose(4, 3, 1, 2, 0).reshape(P, DC, JB, P)),
        "peer_up": tight(up.transpose(2, 0, 1, 3).reshape(P, JB, D)),
        "ident": c["ident"], "decay": c["decay"], "own": c["own"], "sel": c["sel"], "avg": c["avg"],
        "sums_of": c["sums_of"], "share": c["share"], "mask": c["mask"],
    }


def tower(nc, i, out):
    rows = out.rearrange("b t d -> (b t) d")

    def scratch(name, shape):
        return nc.dram_tensor(name, shape, F32, kind="Internal").ap()

    h0 = scratch("h0", (B, T, D))
    xT, aT = scratch("xT", (D, NTOK)), scratch("aT", (D, NTOK))
    x2, hx, h2 = scratch("x2", (NTOK, D)), scratch("hx", (NTOK, D)), scratch("h2", (NTOK, D))
    h0_rows = h0.rearrange("b t d -> (b t) d")
    token_mixer(nc, i["log_dt"], i["inv_A_real"], i["A_imag"], i["B_ri"], i["C_ri"], i["cls_tok"], h0)
    enter_retention(nc, h0_rows, i["ident"], xT)
    retention(nc, xT, i["ret_wq"], i["ret_wk"], i["ret_wv"], i["ret_gnw"], i["ret_gnb"], i["decay"], i["own"], i["sel"],
              i["avg"], aT)
    enter_attention(nc, aT, h0_rows, i["ret_wout"], i["ln1_g"], i["ln1_b"], i["ident"], hx, x2, xT)
    attention(nc, True, xT, i["soft_wq"], i["soft_wk"], i["soft_wv"], i["soft_bq"], i["soft_bk"], i["soft_bv"],
              i["own"], i["sel"], i["sums_of"], i["share"], i["ident"], i["mask"], aT)
    experts(nc, aT, x2, hx, i["soft_wp"], i["soft_bp"], i["ln2_g"], i["ln2_b"], i["gate_w"], i["gate_b"],
            i["moe_w1"], i["moe_b1"], i["moe_w2"], i["moe_b2"], i["ident"], h2, xT)
    attention(nc, False, xT, i["stable_wq"], i["stable_wk"], i["stable_wv"], i["stable_bq"], i["stable_bk"],
              i["stable_bv"], i["own"], i["sel"], i["sums_of"], i["share"], i["ident"], i["mask"], aT)
    product_keys(nc, aT, h2, i["stable_wout"], i["stable_bout"], i["norm_w"], i["peer_w_q"], i["peer_keys"],
                 i["peer_down"], i["peer_up"], i["ident"], rows)


def kernel(**inputs):
    import concourse.bacc as bacc
    from concourse.bass_utils import run_bass_kernel_spmd

    arrays = laid_out(inputs)
    nc = bacc.Bacc("TRN2", target_bir_lowering=False, num_devices=1)
    aps = {name: nc.dram_tensor(f"in_{name}", a.shape, mybir.dt.from_np(a.dtype), kind="ExternalInput").ap()
           for name, a in arrays.items()}
    out = nc.dram_tensor("out", (B, T, D), F32, kind="ExternalOutput").ap()
    tower(nc, aps, out)
    result = run_bass_kernel_spmd(nc, [{f"in_{name}": a for name, a in arrays.items()}], core_ids=[0])
    return result.results[0]["out"]
```
